# Optimizing a Trainium2 kernel written in Bass

```python
import numpy as np
import jax
import jax.numpy as jnp

def _softmax(x, axis=-1):
    return jax.nn.softmax(x, axis=axis)

def _gelu(x):
    return jax.nn.gelu(x, approximate=True)

def _silu(x):
    return jax.nn.silu(x)

def _sigmoid(x):
    return jax.nn.sigmoid(x)

def _layernorm(x, axis=-1, eps=1e-05):
    m = jnp.mean(x, axis=axis, keepdims=True)
    v = jnp.var(x, axis=axis, keepdims=True)
    return (x - m) / jnp.sqrt(v + eps)

def _scatter_add(tgt, idx, src, axis=0):
    return tgt.at[idx].add(src)

def _segment_sum(src, seg, n):
    return jax.ops.segment_sum(src, seg, n)
kernel_name = 'mk_adaln_d1_jaxref_r4_8ba7d6'

def setup_inputs(seed: int=0):
    np.random.seed(seed)
    _w = jnp.asarray

    def _L0_attn_setup():
        import jax, jax.numpy as jnp
        import numpy as np
        N_HEADS = 16
        ROPE_BASE = 10000.0

        def _rotate_every_two(x):
            x_even = x[..., ::2]
            x_odd = x[..., 1::2]
            return jnp.stack((-x_odd, x_even), axis=-1).reshape(x.shape)

        def _rope_cos_sin(seq_len, head_dim):
            inv_freq = 1.0 / ROPE_BASE ** (jnp.arange(0, head_dim, 2, dtype=jnp.float32) / head_dim)
            pos = jnp.arange(seq_len, dtype=jnp.float32)
            freqs = pos[:, None] * inv_freq[None, :]
            emb = jnp.repeat(freqs, 2, axis=-1)
            return (jnp.cos(emb)[None, None], jnp.sin(emb)[None, None])
        key = jax.random.key(seed)
        ks = jax.random.split(key, 5)
        B, S, D = (2, 512, 256)
        std = 0.02
        return {'x': jax.random.normal(ks[0], (B, S, D), dtype=jnp.float32), 'Wq': jax.random.normal(ks[1], (D, D), dtype=jnp.float32) * std, 'Wk': jax.random.normal(ks[2], (D, D), dtype=jnp.float32) * std, 'Wv': jax.random.normal(ks[3], (D, D), dtype=jnp.float32) * std, 'Wo': jax.random.normal(ks[4], (D, D), dtype=jnp.float32) * std}
    _L0_attn_in = _L0_attn_setup()

    def _L0_ffn_setup():
        import jax, jax.numpy as jnp
        import numpy as np
        MICRO_BATCHES = 2
        TOP_K = 2
        NUM_EXPERTS = 8
        B, S, D = (4, 1024, 256)
        H = 4 * D
        key = jax.random.key(seed)
        ks = jax.random.split(key, 8)
        s = 0.02
        return {'x': jax.random.normal(ks[0], (B, S, D), jnp.float32), 'ln_scale': jnp.ones((D,), jnp.float32), 'ln_bias': jnp.zeros((D,), jnp.float32), 'attn_w': jax.random.normal(ks[1], (D, D), jnp.float32) * s, 'attn_b': jnp.zeros((D,), jnp.float32), 'gate_w': jax.random.normal(ks[2], (NUM_EXPERTS, D), jnp.float32) * s, 'w1': jax.random.normal(ks[3], (NUM_EXPERTS, D, H), jnp.float32) * s, 'b1': jnp.zeros((NUM_EXPERTS, H), jnp.float32), 'w2': jax.random.normal(ks[4], (NUM_EXPERTS, H, D), jnp.float32) * s, 'b2': jnp.zeros((NUM_EXPERTS, D), jnp.float32), 'next_w': jax.random.normal(ks[5], (D, D), jnp.float32) * s, 'next_b': jnp.zeros((D,), jnp.float32)}
    _L0_ffn_in = _L0_ffn_setup()
    _L0_c = _w((lambda *s: np.random.randn(*s).astype(np.float32) * 0.05)(1, 256))
    _L0_wmod = _w((lambda *s: np.random.randn(*s).astype(np.float32) * 0.05)(256, 6 * 256) * 256 ** (-0.5))
    _d = {'L0_attn_x': _L0_attn_in['x'], 'L0_attn_Wq': _L0_attn_in['Wq'], 'L0_attn_Wk': _L0_attn_in['Wk'], 'L0_attn_Wv': _L0_attn_in['Wv'], 'L0_attn_Wo': _L0_attn_in['Wo'], 'L0_ffn_ln_scale': _L0_ffn_in['ln_scale'], 'L0_ffn_ln_bias': _L0_ffn_in['ln_bias'], 'L0_ffn_attn_w': _L0_ffn_in['attn_w'], 'L0_ffn_attn_b': _L0_ffn_in['attn_b'], 'L0_ffn_gate_w': _L0_ffn_in['gate_w'], 'L0_ffn_w1': _L0_ffn_in['w1'], 'L0_ffn_b1': _L0_ffn_in['b1'], 'L0_ffn_w2': _L0_ffn_in['w2'], 'L0_ffn_b2': _L0_ffn_in['b2'], 'L0_ffn_next_w': _L0_ffn_in['next_w'], 'L0_ffn_next_b': _L0_ffn_in['next_b'], 'L0_c': _L0_c, 'L0_wmod': _L0_wmod}
    _x0 = _d['L0_attn_x']
    _d['L0_attn_x'] = jax.random.normal(jax.random.fold_in(jax.random.key(seed), 1), (1, 4096, 256), dtype=_x0.dtype)
    del _x0
    return _d

def reference(L0_attn_x, L0_attn_Wq, L0_attn_Wk, L0_attn_Wv, L0_attn_Wo, L0_ffn_ln_scale, L0_ffn_ln_bias, L0_ffn_attn_w, L0_ffn_attn_b, L0_ffn_gate_w, L0_ffn_w1, L0_ffn_b1, L0_ffn_w2, L0_ffn_b2, L0_ffn_next_w, L0_ffn_next_b, L0_c, L0_wmod):

    def _L0_attn_ref(x, Wq, Wk, Wv, Wo):
        import jax, jax.numpy as jnp
        import numpy as np
        N_HEADS = 16
        ROPE_BASE = 10000.0

        def _rotate_every_two(x):
            x_even = x[..., ::2]
            x_odd = x[..., 1::2]
            return jnp.stack((-x_odd, x_even), axis=-1).reshape(x.shape)

        def _rope_cos_sin(seq_len, head_dim):
            inv_freq = 1.0 / ROPE_BASE ** (jnp.arange(0, head_dim, 2, dtype=jnp.float32) / head_dim)
            pos = jnp.arange(seq_len, dtype=jnp.float32)
            freqs = pos[:, None] * inv_freq[None, :]
            emb = jnp.repeat(freqs, 2, axis=-1)
            return (jnp.cos(emb)[None, None], jnp.sin(emb)[None, None])
        B, S, D = x.shape
        H = N_HEADS
        hd = D // H
        scale = hd ** (-0.5)

        def shape_heads(t):
            return t.reshape(B, S, H, hd).transpose(0, 2, 1, 3)
        q = shape_heads(x @ Wq.T)
        k = shape_heads(x @ Wk.T)
        v = shape_heads(x @ Wv.T)
        cos, sin = _rope_cos_sin(S, hd)
        q = q * cos + _rotate_every_two(q) * sin
        k = k * cos + _rotate_every_two(k) * sin
        scores = jnp.einsum('bhqd,bhkd->bhqk', q, k) * scale
        qpos = jnp.arange(S)[:, None]
        kpos = jnp.arange(S)[None, :]
        mask = jnp.where(kpos > qpos, jnp.float32(-jnp.inf), jnp.float32(0.0))
        scores = scores + mask[None, None]
        attn = jax.nn.softmax(scores.astype(jnp.float32), axis=-1).astype(q.dtype)
        out = jnp.einsum('bhqk,bhkd->bhqd', attn, v)
        out = out.transpose(0, 2, 1, 3).reshape(B, S, D)
        return out @ Wo.T

    def _L0_ffn_ref(x, ln_scale, ln_bias, attn_w, attn_b, gate_w, w1, b1, w2, b2, next_w, next_b):
        import jax, jax.numpy as jnp
        import numpy as np
        MICRO_BATCHES = 2
        TOP_K = 2
        NUM_EXPERTS = 8
        B, S, D = (4, 1024, 256)
        H = 4 * D
        b, s, d = x.shape
        flat = x.reshape(b * s, d)
        mu = jnp.mean(flat, axis=-1, keepdims=True)
        var = jnp.mean((flat - mu) ** 2, axis=-1, keepdims=True)
        xn = (flat - mu) * jax.lax.rsqrt(var + 1e-05) * ln_scale + ln_bias
        x_attn = xn @ attn_w.T + attn_b + flat
        logits = x_attn @ gate_w.T
        _vals, _idx = jax.lax.top_k(logits, TOP_K)
        e = w1.shape[0]
        n = b * s // (MICRO_BATCHES * e)
        xe = x_attn.reshape(MICRO_BATCHES, e, n, d)
        h = jax.nn.gelu(jnp.einsum('mend,edh->menh', xe, w1) + b1[None, :, None, :], approximate=False)
        eo = jnp.einsum('menh,ehd->mend', h, w2) + b2[None, :, None, :]
        eo = eo.reshape(b * s, d)
        out = jax.nn.gelu(eo @ next_w.T + next_b, approximate=False)
        return out.reshape(b, s, d)
    x = L0_attn_x
    mod = (_silu(L0_c) @ L0_wmod).reshape(L0_c.shape[0], 6, 1, -1)
    sa, ca, ga, sb, cb, gb = (mod[:, 0], mod[:, 1], mod[:, 2], mod[:, 3], mod[:, 4], mod[:, 5])
    ga = (2 * (ga >= 0) - 1) * jnp.maximum(jnp.abs(ga), 0.25)
    gb = (2 * (gb >= 0) - 1) * jnp.maximum(jnp.abs(gb), 0.25)
    h = _layernorm(x, axis=-1) * (1 + ca) + sa
    x = x + ga * _L0_attn_ref(h, L0_attn_Wq, L0_attn_Wk, L0_attn_Wv, L0_attn_Wo)
    h = _layernorm(x, axis=-1) * (1 + cb) + sb
    x = x + gb * _L0_ffn_ref(h, L0_ffn_ln_scale, L0_ffn_ln_bias, L0_ffn_attn_w, L0_ffn_attn_b, L0_ffn_gate_w, L0_ffn_w1, L0_ffn_b1, L0_ffn_w2, L0_ffn_b2, L0_ffn_next_w, L0_ffn_next_b)
    return x

_drawn_inputs = setup_inputs


def setup_inputs(seed=0):
    import zlib

    import numpy as np

    out = dict(_drawn_inputs(seed))
    spreads = {'L0_ffn_ln_scale': (1.0, 0.6),
     'L0_ffn_ln_bias': (0.0, 0.8),
     'L0_ffn_attn_b': (0.0, 0.8),
     'L0_ffn_b1': (0.0, 0.8),
     'L0_ffn_b2': (0.0, 2.0),
     'L0_ffn_next_b': (0.0, 2.0)}
    factors = {'L0_attn_Wq': 8.0,
     'L0_attn_Wk': 8.0,
     'L0_attn_Wv': 8.0,
     'L0_attn_Wo': 8.0,
     'L0_ffn_attn_w': 8.0,
     'L0_ffn_w1': 8.0,
     'L0_ffn_w2': 8.0,
     'L0_ffn_next_w': 8.0,
     'L0_c': 4.324,
     'L0_wmod': 3.829}
    for name, (base, spread) in spreads.items():
        noise = np.random.default_rng([zlib.crc32(name.encode()), seed]).standard_normal(out[name].shape)
        drawn = base * np.exp(spread * noise) if base else spread * noise
        out[name] = jnp.asarray(drawn.astype(out[name].dtype))
    for name, factor in factors.items():
        out[name] = (out[name] * factor).astype(out[name].dtype)
    return out
```

```python
from contextlib import ExitStack

import numpy as np

import concourse.bass as bass
from concourse import mybir
from concourse.alu_op_type import AluOpType as ALU

F32 = mybir.dt.float32
BF16 = mybir.dt.bfloat16
ACT = mybir.ActivationFunctionType
AX_X = mybir.AxisListType.X

P = 128
S = 4096
D = 256
HEADS = 16
HD = D // HEADS
QUADS = 4
JH = HEADS // QUADS
CW = 512
CHUNKS = S // CW
TILES = CW // P
HALF = D // P
PARTS = 3
Q_PART = (0, 0, 1, 1, 0, 2)
K_PART = (0, 1, 0, 1, 2, 0)
KROWS = len(Q_PART) * HD
MROWS = PARTS * JH
VW = HD + 1
EXPERTS = 8
HID = 1024
HK = HID // P
NEG = -3.0e38
EPS = 1e-5
FREE = 1


def first_step(c):
    return 2 * c * (c + 1)


STEPS = [(c, kb) for c in range(CHUNKS) for kb in range(TILES * (c + 1))]
NSTEPS = len(STEPS)
SBANKS = 3
UNITS = NSTEPS * JH


def max_units(c):
    return ([("full", c, t, kc, pair) for kc in range(c) for t in range(TILES) for pair in range(2)]
            + [("diag", c, t, c, pair) for t in range(TILES) for pair in range(2)])


def late_turns(chunks, lag):
    out, due = [], []
    for c in chunks:
        for u in max_units(c):
            out.append(u)
            for d in list(due):
                d[1] -= 1
                if d[1] == 0:
                    out.append(("turn", d[0], 0, 0, 0))
                    due.remove(d)
        due.append([c, lag])
    return out + [("turn", d[0], 0, 0, 0) for d in due]


AHEAD = 3
HEAD_UNITS = late_turns(range(AHEAD), 5)


def side_units():
    at = [[] for _ in range(NSTEPS + 1)]
    own = late_turns(range(AHEAD, CHUNKS), 5)
    own_steps = first_step(CHUNKS - 1) - 3
    for n, u in enumerate(own):
        at[n * own_steps // len(own)].append(u)
    begin = first_step(CHUNKS - 1) + 9
    for n, u in enumerate(HEAD_UNITS):
        at[begin + n * (NSTEPS - begin) // len(HEAD_UNITS)].append(u)
    for c in range(CHUNKS):
        at[min(first_step(c + 1) + 2, NSTEPS)].append(("norm", c, 0, 0, 0))
    return at


SIDE = side_units()
SIDE_FLAT = [u for us in SIDE for u in us]
HEAD_N = len(HEAD_UNITS)
SIDE_N = len(SIDE_FLAT)
assert SIDE_N % 2 == 0


def slot_uses(slot):
    before = len([n for n in range(HEAD_N) if n % 2 == slot])
    return before, SIDE_N // 2


def count_units(kinds, until=None):
    return len([u for u in (SIDE_FLAT if until is None else SIDE_FLAT[:until]) if u[0] in kinds])


def build(nc, x, wqk, wvT, woT, lnsb, attnT, attnb, w1, b1, w2, b2, nextT, nextb, cvec, wmod,
          rope, ident, mask, later, lastones, out):
    parts = nc.dram_tensor("parts_scratch", [PARTS, QUADS, P, S], BF16, kind="Internal").ap()

    with ExitStack() as whole:
        def sem(name):
            return whole.enter_context(nc.semaphore(name))

        def keep(name, shape, dt=F32):
            return whole.enter_context(nc.sbuf_tensor(name, shape, dt))

        PS = whole.enter_context(nc.psum_tensor("banks", [P, 8 * 512], F32))

        def bank(b, n=1):
            return PS[:, b * 512:(b + n) * 512]

        id_f = keep("id_f", [P, P])
        mod_bc = keep("mod_bc", [P, 6 * D])
        mod_col = keep("mod_col", [P, 16])
        wo_g = keep("wo_g", [P, HALF, D])
        att_o = keep("att_o", [P, S // P, D])

        project(nc, sem, bank, whole, dict(
            x=x, wqk=wqk, wvT=wvT, woT=woT, cvec=cvec, wmod=wmod, rope=rope, ident=ident, parts=parts,
            id_f=id_f, mod_bc=mod_bc, mod_col=mod_col, wo_g=wo_g, att_o=att_o, mask=mask, later=later, lastones=lastones))
        feed(nc, sem, bank, dict(
            x=x, lnsb=lnsb, attnT=attnT, attnb=attnb, w1=w1, b1=b1, w2=w2, b2=b2, nextT=nextT, nextb=nextb,
            id_f=id_f, mod_bc=mod_bc, mod_col=mod_col, wo_g=wo_g, att_o=att_o, out=out))


def begin(engine, *semaphores):
    for s in semaphores:
        engine.sem_inc(s, FREE)


def alone(engine, passed):
    engine.sem_inc(passed, 1)


def project(nc, sem, bank, whole, a):
    with ExitStack() as ctx:
        v_all = ctx.enter_context(nc.sbuf_tensor("v_all", [P, QUADS, S // P, JH, VW], F32))
        with ExitStack() as mine:
            project_block(nc, sem, bank, mine, a, v_all)
        with ExitStack() as mine:
            attend_block(nc, sem, bank, mine, a, v_all)


def project_block(nc, sem, bank, ctx, a, v_all):
    def sb(name, shape, dt=F32):
        return ctx.enter_context(nc.sbuf_tensor(name, shape, dt))

    w_qk = sb("w_qk", [P, HALF, QUADS, P])
    w_v = sb("w_v", [P, HALF, D])
    w_m = sb("w_m", [P, HALF, 6 * D])
    w_o = sb("w_o", [P, HALF, D])
    c_col = sb("c_col", [P, HALF])
    c_exp = sb("c_exp", [P, HALF])
    c_inv = sb("c_inv", [P, HALF])
    c_silu = sb("c_silu", [P, HALF])
    c_wide = sb("c_wide", [P, HALF, P])
    ones = sb("ones", [P, P])
    gate_s = sb("gate_s", [P, 2, D])
    gate_m = sb("gate_m", [P, 2, D])
    half_neg = sb("half_neg", [P, TILES])
    xs = sb("xs", [P, 2, TILES, D])
    stats = sb("stats", [P, 2, TILES, 6])
    mv = sb("mv", [P, 2, TILES, 2])
    var_e = sb("var_e", [P, 2, TILES])
    rstd = sb("rstd", [P, 2, TILES])
    xn = sb("xn", [P, 2, TILES, D])
    hT = sb("hT", [P, 2, HALF, CW])
    cs = sb("cs", [P, 2, 2, CW])
    qf = sb("qf", [P, QUADS, CW])
    qs = sb("qs", [P, QUADS, CW])
    p1 = sb("p1", [P, QUADS, CW], BF16)
    p2 = sb("p2", [P, QUADS, CW], BF16)
    p3 = sb("p3", [P, QUADS, CW], BF16)
    pp = (p1, p2, p3)

    passed_dve, passed_pool, passed_sp = sem("passed_dve"), sem("passed_pool"), sem("passed_sp")
    w_in, c_in, ones_set, silu_e, silu_s = sem("w_in"), sem("c_in"), sem("ones_set"), sem("silu_e"), sem("silu_s")
    mod_ps, mod_ev, gate_st, wo_rdy, const_p = sem("mod_ps"), sem("mod_ev"), sem("gate_st"), sem("wo_rdy"), sem("const_p")
    x_in = [sem("x_in0"), sem("x_in1")]
    cs_in = [sem("cs_in0"), sem("cs_in1")]
    st_done, mv_done, var_done, rstd_done, xn_done = (sem("st_done"), sem("mv_done"), sem("var_done"),
                                                      sem("rstd_done"), sem("xn_done"))
    hT_ps, hT_ev = sem("hT_ps"), sem("hT_ev")
    qk_ps, qf_ev, swapped = sem("qk_ps"), sem("qf_ev"), [sem(f"swapped{g}") for g in range(QUADS)]
    v_ps, v_ev = sem("v_ps"), sem("v_ev")
    cos_done, sin_done, rot_done = sem("cos_done"), sem("sin_done"), sem("rot_done")
    p1_done, r1_done, p2_done, p3_done = sem("p1_done"), sem("r1_done"), sem("p2_done"), sem("p3_done")
    stored = [sem(f"stored{g}") for g in range(QUADS)]

    with nc.Block() as block:
        @block.sync
        def _(sp):
            begin(sp, *stored)
            sp.dma_start(c_col[:, :], a["cvec"]).then_inc(c_in, 16)
            sp.dma_start(w_m[:, :, :], a["wmod"].rearrange("(h p) n -> p h n", p=P)).then_inc(w_in, 16)
            sp.dma_start(a["id_f"][:, :], a["ident"]).then_inc(w_in, 16)
            sp.dma_start(w_qk[:, :, :, :], a["wqk"].rearrange("(h p) g n -> p h g n", p=P)).then_inc(w_in, 16)
            sp.dma_start(w_v[:, :, :], a["wvT"].rearrange("(h p) n -> p h n", p=P)).then_inc(w_in, 16)
            sp.dma_start(w_o[:, :, :], a["woT"].rearrange("(h p) n -> p h n", p=P)).then_inc(w_in, 16)
            with sp.Fori(0, CHUNKS // 2) as i:
                for par in range(2):
                    sp.wait_ge(xn_done, FREE + i * 2 * TILES)
                    alone(sp, passed_sp)
                    sp.dma_start(xs[:, par, :, :],
                                 a["x"][0, bass.ds((i * 2 + par) * CW, CW), :].rearrange("(t p) d -> p t d", p=P))\
                        .then_inc(x_in[par], 16)
                    sp.wait_ge(cos_done, FREE + i * 2 * QUADS)
                    sp.wait_ge(sin_done, FREE + i * 2 * QUADS)
                    alone(sp, passed_sp)
                    sp.dma_start(cs[:, par, :, :], a["rope"][:, :, bass.ds((i * 2 + par) * CW, CW)])\
                        .then_inc(cs_in[par], 16)
                for par in range(2):
                    for g in range(QUADS):
                        sp.wait_ge(qf_ev, FREE + i * 2 * QUADS + par * QUADS + g + 1)
                        sp.dma_start(qs[0:P:2, g, :], qf[1:P:2, g, :]).then_inc(swapped[g], 16)
                        sp.dma_start(qs[1:P:2, g, :], qf[0:P:2, g, :]).then_inc(swapped[g], 16)
                    for g in range(QUADS):
                        for n, done in enumerate((p1_done, p2_done, p3_done)):
                            sp.wait_ge(done, i * 2 * QUADS + par * QUADS + g + 1)
                            alone(sp, passed_sp)
                            sp.dma_start(a["parts"][n, g, :, bass.ds((i * 2 + par) * CW, CW)], pp[n][:, g, :])\
                                .then_inc(stored[g], 16)
            for g in range(QUADS):
                sp.wait_ge(stored[g], FREE + 16 * PARTS * CHUNKS)

        @block.gpsimd
        def _(pool):
            begin(pool, sin_done)
            nc.gpsimd.memset(ones[:, :], 1.0).then_inc(ones_set, 1)
            nc.gpsimd.memset(half_neg[:, :], -0.5).then_inc(const_p, 1)
            nc.gpsimd.memset(v_all[:, :, :, :, HD:VW], 1.0).then_inc(const_p, 1)
            pool.wait_ge(const_p, 2)
            with pool.Fori(0, CHUNKS // 2) as i:
                for par in range(2):
                    pool.wait_ge(mv_done, (i * 2 + par + 1) * TILES)
                    pool.wait_ge(xn_done, FREE + i * 2 * TILES)
                    alone(pool, passed_pool)
                    nc.gpsimd.tensor_scalar(var_e[:, par, :], mv[:, par, :, 1], EPS, None, ALU.add)\
                        .then_inc(var_done, 1)
                    pool.wait_ge(var_done, i * 2 + par + 1)
                    nc.gpsimd.tensor_tensor(rstd[:, par, :], var_e[:, par, :], half_neg[:, :], ALU.pow)\
                        .then_inc(rstd_done, 1)
                for par in range(2):
                    for g in range(QUADS):
                        if g == 0:
                            pool.wait_ge(cs_in[par], i * 16 + 16)
                        pool.wait_ge(swapped[g], i * 64 + par * 32 + 32)
                        nc.gpsimd.tensor_tensor(qs[:, g, :], qs[:, g, :], cs[:, par, 1, :], ALU.mult)\
                            .then_inc(sin_done, 1)
                    for g in range(QUADS):
                        pool.wait_ge(r1_done, FREE + i * 2 * QUADS + par * QUADS + g + 1)
                        pool.wait_ge(p2_done, i * 2 * QUADS + par * QUADS + g + 1)
                        pool.wait_ge(stored[g], FREE + i * 96 + par * 48)
                        nc.gpsimd.tensor_tensor(p3[:, g, :], qs[:, g, :], p2[:, g, :], ALU.subtract)\
                            .then_inc(p3_done, 1)

        @block.vector
        def _(dve):
            begin(dve, xn_done, cos_done, r1_done)
            dve.wait_ge(silu_e, 1)
            nc.vector.tensor_scalar(c_inv[:, :], c_exp[:, :], 1.0, None, ALU.add).then_inc(silu_s, 1)
            dve.wait_ge(silu_s, 1)
            nc.vector.reciprocal(c_exp[:, :], c_inv[:, :]).then_inc(silu_s, 1)
            dve.wait_ge(silu_s, 2)
            nc.vector.tensor_tensor(c_silu[:, :], c_col[:, :], c_exp[:, :], ALU.mult).then_inc(silu_s, 1)
            dve.wait_ge(silu_s, 3)
            dve.wait_ge(ones_set, 1)
            for h in range(HALF):
                nc.vector.tensor_scalar(c_wide[:, h, :], ones[:, :], c_silu[:, h:h + 1], None, ALU.mult)\
                    .then_inc(silu_s, 1)
            dve.wait_ge(mod_ps, 2)
            for n in range(3):
                nc.vector.tensor_copy(a["mod_bc"][:, n * 512:(n + 1) * 512], bank(n)).then_inc(mod_ev, 1)
            for k, plus in enumerate((0.0, 1.0, 0.0, 1.0)):
                nc.vector.tensor_scalar(a["mod_col"][:, 2 * k:2 * k + 2], bank(3)[:, 2 * k:2 * k + 2], plus, None, ALU.add)\
                    .then_inc(mod_ev, 1)
            dve.wait_ge(mod_ev, 7)
            nc.vector.tensor_scalar(a["mod_bc"][:, 4 * D:5 * D], a["mod_bc"][:, 4 * D:5 * D], 1.0, None, ALU.add)\
                .then_inc(mod_ev, 1)
            for n, k in enumerate((2, 5)):
                gate = a["mod_bc"][:, k * D:(k + 1) * D]
                nc.vector.tensor_scalar(gate_s[:, n, :], gate, 0.0, 2.0, ALU.is_ge, ALU.mult).then_inc(gate_st, 1)
                nc.vector.scalar_tensor_tensor(out=gate_m[:, n, :], in0=gate, scalar=-1.0, in1=gate,
                                               op0=ALU.mult, op1=ALU.max).then_inc(gate_st, 1)
            dve.wait_ge(gate_st, 4)
            for n in range(2):
                nc.vector.tensor_scalar(gate_m[:, n, :], gate_m[:, n, :], 0.25, None, ALU.max).then_inc(gate_st, 1)
            dve.wait_ge(gate_st, 6)
            for n, k in enumerate((2, 5)):
                nc.vector.scalar_tensor_tensor(out=a["mod_bc"][:, k * D:(k + 1) * D], in0=gate_s[:, n, :], scalar=-1.0,
                                               in1=gate_m[:, n, :], op0=ALU.add, op1=ALU.mult).then_inc(gate_st, 1)
            dve.wait_ge(gate_st, 8)
            dve.wait_ge(w_in, 80)
            for h in range(HALF):
                nc.vector.tensor_tensor(a["wo_g"][:, h, :], w_o[:, h, :], a["mod_bc"][:, 2 * D:3 * D], ALU.mult)\
                    .then_inc(wo_rdy, 1)
            dve.wait_ge(wo_rdy, 2)
            with dve.Fori(0, CHUNKS // 2) as i:
                for par in range(2):
                    dve.wait_ge(x_in[par], i * 16 + 16)
                    for t in range(TILES):
                        nc.vector.bn_stats(stats[:, par, t, :], xs[:, par, t, :]).then_inc(st_done, 1)
                    for t in range(TILES):
                        dve.wait_ge(st_done, (i * 2 + par) * TILES + t + 1)
                        alone(dve, passed_dve)
                        nc.vector.bn_aggr(mv[:, par, t, :], stats[:, par, t, :]).then_inc(mv_done, 1)
                for par in range(2):
                    dve.wait_ge(rstd_done, i * 2 + par + 1)
                    dve.wait_ge(hT_ps, FREE + i * 4)
                    for t in range(TILES):
                        nc.vector.tensor_scalar(xn[:, par, t, :], xs[:, par, t, :], mv[:, par, t, 0:1],
                                                rstd[:, par, t:t + 1], ALU.subtract, ALU.mult).then_inc(xn_done, 1)
                for par in range(2):
                    base = i * 2 * QUADS + par * QUADS
                    for g in range(QUADS):
                        if g == 0:
                            dve.wait_ge(cs_in[par], i * 16 + 16)
                        dve.wait_ge(swapped[g], i * 64 + par * 32 + 32)
                        nc.vector.tensor_tensor(qf[:, g, :], qf[:, g, :], cs[:, par, 0, :], ALU.mult)\
                            .then_inc(cos_done, 1)
                    for g in range(QUADS):
                        dve.wait_ge(sin_done, FREE + base + g + 1)
                        dve.wait_ge(cos_done, FREE + base + g + 1)
                        nc.vector.tensor_tensor(qf[:, g, :], qf[:, g, :], qs[:, g, :], ALU.add).then_inc(rot_done, 1)
                    for g in range(QUADS):
                        dve.wait_ge(p1_done, base + g + 1)
                        dve.wait_ge(rot_done, base + g + 1)
                        nc.vector.tensor_tensor(qs[:, g, :], qf[:, g, :], p1[:, g, :], ALU.subtract)\
                            .then_inc(r1_done, 1)

        @block.scalar
        def _(act):
            begin(act, v_ev, qf_ev)
            act.wait_ge(c_in, 16)
            nc.scalar.activation(c_exp[:, :], c_col[:, :], ACT.Exp, scale=-1.0).then_inc(silu_e, 1)
            act.wait_ge(mod_ev, 7)
            with act.Fori(0, CHUNKS // 2) as i:
                for par in range(2):
                    act.wait_ge(hT_ps, FREE + i * 4 + par * 2 + 2)
                    act.wait_ge(v_ps, FREE + i * 8)
                    for h in range(HALF):
                        nc.scalar.activation(hT[:, par, h, :], bank(2 * par + h), ACT.Identity,
                                             bias=a["mod_col"][:, h:h + 1], scale=a["mod_col"][:, 2 + h:3 + h])\
                            .then_inc(hT_ev, 1)
                for par in range(2):
                    base = i * 2 * QUADS + par * QUADS
                    for g in range(QUADS):
                        act.wait_ge(qk_ps, base + g + 1)
                        act.wait_ge(r1_done, FREE + base)
                        nc.scalar.activation(qf[:, g, :], bank(4 + g), ACT.Copy).then_inc(qf_ev, 1)
                    for t in range(TILES):
                        act.wait_ge(v_ps, FREE + (i * 2 + par) * TILES + t - t % 2 + 2)
                        nc.scalar.activation(
                            v_all[:, :, bass.ds((i * 2 + par) * TILES + t, 1), :, 0:HD]
                            .rearrange("p g o j d -> p g (o j) d"),
                            bank(2 * par + t // 2)[:, (t % 2) * D:(t % 2 + 1) * D]
                            .rearrange("p (g j d) -> p g j d", g=QUADS, j=JH), ACT.Copy).then_inc(v_ev, 1)
                    for g in range(QUADS):
                        act.wait_ge(rot_done, base + g + 1)
                        act.wait_ge(stored[g], FREE + i * 96 + par * 48)
                        nc.scalar.activation(p1[:, g, :], qf[:, g, :], ACT.Copy).then_inc(p1_done, 1)
                    for g in range(QUADS):
                        act.wait_ge(r1_done, FREE + base + g + 1)
                        nc.scalar.activation(p2[:, g, :], qs[:, g, :], ACT.Copy).then_inc(p2_done, 1)

        @block.tensor
        def _(pe):
            begin(pe, v_ps, hT_ps)
            pe.wait_ge(w_in, 80)
            pe.wait_ge(silu_s, 5)
            for n in range(3):
                for h in range(HALF):
                    mm = nc.tensor.matmul(bank(n), c_wide[:, h, :], w_m[:, h, n * 512:(n + 1) * 512],
                                          start=(h == 0), stop=(h == HALF - 1))
            mm.then_inc(mod_ps, 1)
            for k, m in enumerate((0, 1, 3, 4)):
                for half in range(HALF):
                    for h in range(HALF):
                        col = m * D + half * P
                        mm = nc.tensor.matmul(bank(3)[:, 2 * k + half:2 * k + half + 1], w_m[:, h, col:col + P],
                                              c_silu[:, h:h + 1], start=(h == 0), stop=(h == HALF - 1))
            mm.then_inc(mod_ps, 1)
            pe.wait_ge(mod_ev, 7)
            with pe.Fori(0, CHUNKS // 2) as i:
                for par in range(2):
                    pe.wait_ge(xn_done, FREE + (i * 2 + par + 1) * TILES)
                    pe.wait_ge(v_ev, FREE + i * 2 * TILES)
                    for h in range(HALF):
                        for t in range(TILES):
                            mm = nc.tensor.transpose(bank(2 * par + h)[:, t * P:(t + 1) * P],
                                                     xn[:, par, t, h * P:(h + 1) * P], a["id_f"][:, :])
                        mm.then_inc(hT_ps, 1)
                for par in range(2):
                    pe.wait_ge(hT_ev, i * 4 + par * 2 + 2)
                    for g in range(QUADS):
                        pe.wait_ge(qf_ev, FREE + i * 2 * QUADS + par * QUADS)
                        for h in range(HALF):
                            mm = nc.tensor.matmul(bank(4 + g), w_qk[:, h, g, :], hT[:, par, h, :],
                                                  start=(h == 0), stop=(h == HALF - 1))
                        mm.then_inc(qk_ps, 1)
                    for t in range(TILES):
                        for h in range(HALF):
                            mm = nc.tensor.matmul(bank(2 * par + t // 2)[:, (t % 2) * D:(t % 2 + 1) * D],
                                                  hT[:, par, h, t * P:(t + 1) * P], w_v[:, h, :],
                                                  start=(h == 0), stop=(h == HALF - 1))
                        mm.then_inc(v_ps, 1)


def attend_block(nc, sem, bank, ctx, a, v_all):
    def sb(name, shape, dt=F32):
        return ctx.enter_context(nc.sbuf_tensor(name, shape, dt))

    QRING = 4
    k_aug = sb("k_aug", [P, JH, S], BF16)
    q_aug = sb("q_aug", [P, QRING, JH, CW], BF16)
    v_cur = sb("v_cur", [P, S // P, JH, VW])
    prob = sb("prob", [P, 2, JH, CW])
    o_sb = sb("o_sb", [P, 2, CW])
    mask = sb("mask_sb", [P, CW])
    id_b = sb("id_b", [P, P], BF16)
    later_k = sb("later_k", [P, P], BF16)
    mx = sb("mx", [P, QRING, TILES, JH, CHUNKS])
    nm = sb("nm", [P, QRING, TILES * JH])
    nm_r = sb("nm_r", [P, QRING, TILES * JH])
    nm_p = sb("nm_p", [P, QRING, TILES * JH, PARTS], BF16)
    l_inv = sb("l_inv", [P, 2, TILES, JH, 1])

    score = [bank(n) for n in range(SBANKS)]
    pv = bank(3)
    side = [bank(4, 2), bank(6, 2)]
    PV_ROWS = 32

    passed_dve, passed_pool, passed_sp = sem("a_passed_dve"), sem("a_passed_pool"), sem("a_passed_sp")
    consts_in, id_cast, pv_zero = sem("consts_in"), sem("id_cast"), sem("pv_zero")
    k_in = [sem(f"k_in{r}") for r in range(CHUNKS)]
    v_in = [sem(f"v_in{r}") for r in range(CHUNKS)]
    q_in = [sem(f"q_in{r}") for r in range(QRING)]
    st_done = sem("scores_done")
    exp_done = [sem(f"exp_done{b}") for b in range(SBANKS)]
    pv_done = [sem(f"pv_done{b}") for b in range(2)]
    out_ev = sem("out_ev")
    side_done = sem("side_done")
    side_free = [sem("side_free0"), sem("side_free1")]
    nm_done, cut_done = sem("nm_done"), sem("cut_done")
    max_done, linv_done = sem("max_done"), sem("linv_done")

    def exp_count(g, u):
        return g * (UNITS // SBANKS) + u // SBANKS + 1

    def slot_of(n, head):
        return n % 2 if head else (HEAD_N + 1 + n) % 2

    def uses_before(n, head, g):
        if head:
            return n // 2
        before = len([m for m in range(HEAD_N) if m % 2 == slot_of(n, False)])
        return g * (SIDE_N // 2) + before + n // 2

    def ready_count(n, head, g):
        return n + 1 if head else g * SIDE_N + HEAD_N + n + 1

    def maxima_before(n, head, g):
        units = HEAD_UNITS[:n] if head else SIDE_FLAT[:n]
        k = len([u for u in units if u[0] in ("full", "diag")])
        k2 = len([u for u in SIDE_FLAT if u[0] in ("full", "diag")])
        kh = len([u for u in HEAD_UNITS if u[0] in ("full", "diag")])
        return k if head else g * k2 + kh + k

    def items(c, g, head):
        if head:
            return c
        return g * CHUNKS + c if c >= AHEAD else g * CHUNKS + CHUNKS + c

    def steps_before(g, c, kb):
        return g * NSTEPS + first_step(c) + kb

    with nc.Block() as block:
        @block.sync
        def _(sp):
            def load_keys(g, r):
                for n in range(len(K_PART)):
                    sp.dma_start(
                        k_aug[n * HD:(n + 1) * HD, :, r * CW:(r + 1) * CW],
                        a["parts"][K_PART[n], bass.ds(g, 1), P // 2:P, r * CW:(r + 1) * CW]
                        .rearrange("o (j d) s -> d (o j) s", j=JH)).then_inc(k_in[r], 16)

            def load_values(g, r):
                sp.dma_start(v_cur[:, r * TILES:(r + 1) * TILES, :, :],
                             v_all[:, bass.ds(g, 1), r * TILES:(r + 1) * TILES, :, :]
                             .rearrange("p o k j v -> p (o k) j v")).then_inc(v_in[r], 16)

            def load_queries(g, c):
                for n in range(len(Q_PART)):
                    sp.dma_start(
                        q_aug[n * HD:(n + 1) * HD, c % QRING, :, :],
                        a["parts"][Q_PART[n], bass.ds(g, 1), 0:P // 2, c * CW:(c + 1) * CW]
                        .rearrange("o (j d) s -> d (o j) s", j=JH)).then_inc(q_in[c % QRING], 16)

            sp.dma_start(mask[:, :], a["mask"]).then_inc(consts_in, 16)
            sp.dma_start(later_k[:, :], a["later"]).then_inc(consts_in, 16)
            sp.dma_start(k_aug[KROWS:KROWS + MROWS, :, :], a["lastones"]).then_inc(consts_in, 16)
            for r in range(CHUNKS):
                load_keys(0, r)
                if r < AHEAD:
                    load_queries(0, r)
                load_values(0, r)
            with sp.Fori(0, QUADS) as g:
                for c in range(AHEAD, CHUNKS):
                    if c > AHEAD:
                        sp.wait_ge(st_done, FREE + g * UNITS + JH * first_step(c - QRING + 1))
                    else:
                        sp.wait_ge(st_done, FREE + g * UNITS)
                    alone(sp, passed_sp)
                    load_queries(g, c)
                for c in range(AHEAD):
                    sp.wait_ge(st_done, FREE + g * UNITS + JH * first_step(c + QRING + 1))
                    alone(sp, passed_sp)
                    load_queries((g + 1) % QUADS, c)
                for r in range(CHUNKS):
                    last = first_step(CHUNKS - 1) + r * TILES + TILES - 1
                    sp.wait_ge(st_done, FREE + g * UNITS + JH * (last + 1))
                    alone(sp, passed_sp)
                    load_keys((g + 1) % QUADS, r)
                    sp.wait_ge(pv_done[last % 2], FREE + g * (NSTEPS // 2) + last // 2 + 1)
                    alone(sp, passed_sp)
                    load_values((g + 1) % QUADS, r)
            for r in range(CHUNKS):
                sp.wait_ge(k_in[r], 16 * len(K_PART) * (QUADS + 1))
                sp.wait_ge(v_in[r], 16 * (QUADS + 1))

        @block.tensor
        def _(pe):
            begin(pe, st_done, *pv_done)
            def turned(g, c):
                if c >= AHEAD:
                    n = SIDE_FLAT.index(("turn", c, 0, 0, 0))
                    return side_free[slot_of(n, False)], FREE + uses_before(n, False, g) + 1
                n = HEAD_UNITS.index(("turn", c, 0, 0, 0))
                m = SIDE_FLAT.index(("turn", c, 0, 0, 0))
                assert slot_of(n, True) == slot_of(m, False)
                return side_free[slot_of(n, True)], FREE + g * (SIDE_N // 2) + max(
                    uses_before(n, True, 0) + 1, uses_before(m, False, 0) - SIDE_N // 2 + 1)

            def key_loads(g, r):
                pe.wait_ge(k_in[r], (g + 1) * (16 * len(K_PART)))

            def side_unit(g, n, head):
                kind, c, t, kc, pair = HEAD_UNITS[n] if head else SIDE_FLAT[n]
                slot = side[slot_of(n, head)]
                pe.wait_ge(side_free[slot_of(n, head)], FREE + uses_before(n, head, g))
                if kind in ("full", "diag"):
                    width = CW if kind == "full" else (t + 1) * P
                    for jj in range(2):
                        j = 2 * pair + jj
                        mm = nc.tensor.matmul(slot[:, jj * CW:jj * CW + width],
                                              q_aug[0:KROWS, c % QRING, j, t * P:(t + 1) * P],
                                              k_aug[0:KROWS, j, kc * CW:kc * CW + width], start=True, stop=True)
                elif kind == "turn":
                    pe.wait_ge(cut_done, (items(c, g, head) + 1) * 4)
                    for t in range(TILES):
                        mm = nc.tensor.transpose(
                            slot.bitcast(BF16)[KROWS:KROWS + MROWS, t * P:(t + 1) * P],
                            nm_p[:, c % QRING, t * JH:(t + 1) * JH, :].rearrange("p j n -> p (j n)"), id_b[:, :])
                else:
                    pe.wait_ge(out_ev, FREE + g * CHUNKS + c + 1)
                    for t in range(TILES):
                        mm = nc.tensor.transpose(slot[:, t * P:(t + 1) * P], o_sb[:, c % 2, t * P:(t + 1) * P],
                                                 a["id_f"][:, :])
                mm.then_inc(side_done, 1)

            def queries_loaded(g, c, head=False):
                uses = g * (CHUNKS // QRING) + c // QRING
                pe.wait_ge(q_in[c % QRING], (uses + 1) * (16 * len(Q_PART)))

            def values(g, s):
                c, kb = STEPS[s]
                t = kb - TILES * c
                q0 = max(t, 0) * P
                if kb == 0:
                    pe.wait_ge(out_ev, FREE + g * CHUNKS + c)
                u = JH * s + JH - 1
                pe.wait_ge(exp_done[u % SBANKS], FREE + exp_count(g, u))
                if t >= 0:
                    pe.wait_ge(v_in[c], (g + 1) * 16)
                for j in range(JH):
                    mm = nc.tensor.matmul(pv[32 * j:32 * j + VW, q0:CW], v_cur[:, kb, j, :],
                                          prob[:, s % 2, j, q0:CW], start=(kb == 0),
                                          stop=(kb == TILES * (c + 1) - 1), skip_group_check=True)
                mm.then_inc(pv_done[s % 2], 1)

            pe.wait_ge(consts_in, 48)
            pe.wait_ge(id_cast, 1)
            pe.wait_ge(pv_zero, 1)
            for n, unit in enumerate(HEAD_UNITS):
                if unit[0] != "turn":
                    key_loads(0, unit[3])
                    queries_loaded(0, unit[1])
                side_unit(0, n, True)
            with pe.Fori(0, QUADS) as g:
                n = 0
                for s, (c, kb) in enumerate(STEPS):
                    t = kb - TILES * c
                    q0 = max(t, 0) * P
                    mine = SIDE[s]
                    if kb == 0:
                        pe.wait_ge(*turned(g, c))
                    if t == 0:
                        key_loads(g, c)
                    for j in range(JH):
                        u = JH * s + j
                        pe.wait_ge(exp_done[u % SBANKS], FREE + g * (UNITS // SBANKS) + u // SBANKS)
                        mm = nc.tensor.matmul(score[u % SBANKS][:, q0:CW],
                                              k_aug[0:KROWS + MROWS, j, kb * P:(kb + 1) * P],
                                              q_aug[0:KROWS + MROWS, c % QRING, j, q0:CW], start=True, stop=True)
                        if t >= 0:
                            mm = nc.tensor.matmul(score[u % SBANKS][:, q0:q0 + P], id_b[:, :], later_k[:, :],
                                                  start=False, stop=True, skip_group_check=True)
                        mm.then_inc(st_done, 1)
                        lo, hi = len(mine) * j // JH, len(mine) * (j + 1) // JH
                        for unit in mine[lo:hi]:
                            if unit[0] in ("full", "diag"):
                                nxt = 1 if unit[1] < AHEAD else 0
                                if unit[0] == "diag" and unit[2] == 0 and unit[4] == 0 or unit[3] == 0:
                                    queries_loaded(g + nxt, unit[1])
                                key_loads(g + nxt, unit[3])
                            side_unit(g, n, False)
                            n += 1
                    if s:
                        values(g, s - 1)
                values(g, NSTEPS - 1)
                for unit in SIDE[NSTEPS]:
                    side_unit(g, n, False)
                    n += 1

        @block.scalar
        def _(act):
            begin(act, out_ev, *exp_done)
            nc.scalar.activation(id_b[:, :], a["id_f"][:, :], ACT.Copy).then_inc(id_cast, 1)

            def turn(g, n, head):
                c = (HEAD_UNITS if head else SIDE_FLAT)[n][1]
                act.wait_ge(side_done, ready_count(n, head, g))
                slot = side[slot_of(n, head)]
                nc.scalar.activation(q_aug[KROWS:KROWS + MROWS, c % QRING, :, :],
                                     slot.bitcast(BF16)[KROWS:KROWS + MROWS, 0:CW].unsqueeze(1)
                                     .broadcast_to([MROWS, JH, CW]), ACT.Copy)\
                    .then_inc(side_free[slot_of(n, head)], 1)

            def take_out(g, c):
                last = first_step(c + 1) - 1
                act.wait_ge(pv_done[last % 2], FREE + g * (NSTEPS // 2) + last // 2 + 1)
                act.wait_ge(linv_done, FREE + g * CHUNKS + c)
                nc.scalar.activation(o_sb[:, c % 2, :], pv, ACT.Copy).then_inc(out_ev, 1)

            for n, unit in enumerate(HEAD_UNITS):
                if unit[0] == "turn":
                    turn(0, n, True)
            act.wait_ge(pv_zero, 1)
            with act.Fori(0, QUADS) as g:
                n = 0
                for s, (c, kb) in enumerate(STEPS):
                    t = kb - TILES * c
                    q0 = max(t, 0) * P
                    for j in range(JH):
                        u = JH * s + j
                        act.wait_ge(st_done, FREE + g * UNITS + u + 1)
                        if j == 0:
                            act.wait_ge(pv_done[s % 2], FREE + g * (NSTEPS // 2) + s // 2)
                        nc.scalar.activation(prob[:, s % 2, j, q0:CW], score[u % SBANKS][:, q0:CW], ACT.Exp,
                                             scale=float(HD) ** -0.5).then_inc(exp_done[u % SBANKS], 1)
                        if c and kb == 1 and j == 1:
                            take_out(g, c - 1)
                    for unit in SIDE[s]:
                        if unit[0] == "turn":
                            turn(g, n, False)
                        n += 1
                take_out(g, CHUNKS - 1)
                for unit in SIDE[NSTEPS]:
                    if unit[0] == "turn":
                        turn(g, n, False)
                    n += 1

        @block.vector
        def _(dve):
            begin(dve, linv_done, *side_free)
            nc.vector.memset(pv, 0.0).then_inc(pv_zero, 1)
            dve.wait_ge(consts_in, 48)

            def side_unit(g, n, head):
                kind, c, t, kc, pair = HEAD_UNITS[n] if head else SIDE_FLAT[n]
                if kind == "turn":
                    return
                dve.wait_ge(side_done, ready_count(n, head, g))
                if kind == "diag":
                    alone(dve, passed_dve)
                slot = side[slot_of(n, head)]
                free = side_free[slot_of(n, head)]
                if kind == "full":
                    nc.vector.tensor_reduce(mx[:, c % QRING, t, 2 * pair:2 * pair + 2, kc],
                                            slot.rearrange("p (j s) -> p j s", j=2), AX_X, ALU.max).then_inc(free, 1)
                elif kind == "diag":
                    width = (t + 1) * P
                    for jj in range(2):
                        ins = nc.vector.tensor_tensor_reduce(
                            slot[:, jj * CW:jj * CW + width], slot[:, jj * CW:jj * CW + width], mask[:, CW - width:CW],
                            1.0, NEG, ALU.add, ALU.max, mx[:, c % QRING, t, 2 * pair + jj, kc:kc + 1])
                        ins.then_inc(max_done if jj == 0 else free, 1)
                    if t == TILES - 1 and pair == 1:
                        dve.wait_ge(free, FREE + uses_before(n, head, g) + 1)
                        before = uses_before(n - 1, head, g) + 1
                        dve.wait_ge(side_free[slot_of(n - 1, head)], FREE + before)
                        nc.vector.tensor_reduce(nm[:, c % QRING, :],
                                                mx[:, c % QRING, :, :, 0:c + 1].rearrange("p t j k -> p (t j) k"),
                                                AX_X, ALU.max, negate=True).then_inc(nm_done, 1)
                else:
                    blocks = slot[:, 0:CW].rearrange("p (t j v) -> p t j v", t=TILES, j=JH)
                    nc.vector.reciprocal(l_inv[:, c % 2, :, :, :], blocks[:, :, :, HD:HD + 1]).then_inc(linv_done, 1)
                    dve.wait_ge(linv_done, FREE + g * CHUNKS + c + 1)
                    nc.vector.tensor_tensor(
                        a["att_o"][:, c * TILES:(c + 1) * TILES, bass.ds(g * (JH * HD), JH * HD)]
                        .rearrange("p t (j d) -> p t j d", j=JH),
                        blocks[:, :, :, 0:HD], l_inv[:, c % 2, :, :, :].broadcast_to([P, TILES, JH, HD]),
                        ALU.mult).then_inc(free, 1)

            for n in range(HEAD_N):
                side_unit(0, n, True)
            with dve.Fori(0, QUADS) as g:
                for n in range(SIDE_N):
                    side_unit(g, n, False)

        @block.gpsimd
        def _(pool):
            def cut(g, c, head):
                r = c % QRING
                k = items(c, g, head)
                pool.wait_ge(nm_done, k + 1)
                alone(pool, passed_pool)
                nc.gpsimd.tensor_copy(nm_p[:, r, :, 0], nm[:, r, :]).then_inc(cut_done, 1)
                pool.wait_ge(cut_done, 4 * k + 1)
                nc.gpsimd.tensor_tensor(nm_r[:, r, :], nm[:, r, :], nm_p[:, r, :, 0], ALU.subtract)\
                    .then_inc(cut_done, 1)
                pool.wait_ge(cut_done, 4 * k + 2)
                alone(pool, passed_pool)
                nc.gpsimd.tensor_copy(nm_p[:, r, :, 1], nm_r[:, r, :]).then_inc(cut_done, 1)
                pool.wait_ge(cut_done, 4 * k + 3)
                nc.gpsimd.tensor_tensor(nm_p[:, r, :, 2], nm_r[:, r, :], nm_p[:, r, :, 1], ALU.subtract)\
                    .then_inc(cut_done, 1)

            def after_unit(g, n, head):
                kind, c, t, kc, pair = (HEAD_UNITS if head else SIDE_FLAT)[n]
                if kind == "diag" and t == TILES - 1 and pair == 1:
                    cut(g, c, head)

            for n in range(HEAD_N):
                after_unit(0, n, True)
            with pool.Fori(0, QUADS) as g:
                for n in range(SIDE_N):
                    after_unit(g, n, False)


def feed(nc, sem, bank, a):
    with ExitStack() as ctx:
        x1 = ctx.enter_context(nc.sbuf_tensor("x1", [P, S // P, D], F32))
        xaT = ctx.enter_context(nc.sbuf_tensor("xaT", [P, HALF, S], F32))
        with ExitStack() as mine:
            mix_block(nc, sem, bank, mine, a, x1, xaT)
        with ExitStack() as mine:
            expert_block(nc, sem, bank, mine, a, x1, xaT)


def mix_block(nc, sem, bank, ctx, a, x1, xaT):
    def sb(name, shape, dt=F32):
        return ctx.enter_context(nc.sbuf_tensor(name, shape, dt))

    w_a = sb("w_a", [P, HALF, D])
    ab_col = sb("ab_col", [P, HALF])
    ln_col = sb("ln_col", [P, 2 * HALF])
    half_neg = sb("half_neg2", [P, TILES])
    xs = sb("xs2", [P, 2, TILES, D])
    oc = sb("oc", [P, 2, TILES, D])
    oT = sb("oT", [P, 2, HALF, CW])
    stats = sb("stats2", [P, 2, TILES, 6])
    mv = sb("mv2", [P, 2, TILES, 2])
    var_e = sb("var_e2", [P, 2, TILES])
    rstd = sb("rstd2", [P, 2, TILES])
    xn = sb("xn2", [P, 2, TILES, D])
    h2 = sb("h2", [P, 2, TILES, D])
    h2T = sb("h2T", [P, 2, HALF, CW])
    x3T = sb("x3T", [P, 2, HALF, CW])

    passed_dve, passed_pool, passed_sp = sem("m_passed_dve"), sem("m_passed_pool"), sem("m_passed_sp")
    w_in, x_in, o_in = sem("m_w_in"), [sem("m_x_in0"), sem("m_x_in1")], [sem("m_o_in0"), sem("m_o_in1")]
    half_set = sem("m_half_set")
    oT_ps, oT_ev, wo_ps, x1_done = sem("oT_ps"), sem("oT_ev"), sem("wo_ps"), sem("x1_done")
    st_done, mv_done, var_done, rstd_done, xn_done = (sem("m_st_done"), sem("m_mv_done"), sem("m_var_done"),
                                                      sem("m_rstd_done"), sem("m_xn_done"))
    scaled, h2_done = sem("m_scaled"), sem("h2_done")
    h2_ps, x3_ps, h2T_ev, x3T_ev, at_ps, xa_done = (sem("h2_ps"), sem("x3_ps"), sem("h2T_ev"), sem("x3T_ev"),
                                                    sem("at_ps"), sem("xa_done"))

    with nc.Block() as block:
        @block.sync
        def _(sp):
            sp.dma_start(w_a[:, :, :], a["attnT"].rearrange("(h p) n -> p h n", p=P)).then_inc(w_in, 16)
            sp.dma_start(ab_col[:, :], a["attnb"]).then_inc(w_in, 16)
            sp.dma_start(ln_col[:, :], a["lnsb"]).then_inc(w_in, 16)
            with sp.Fori(0, CHUNKS // 2) as i:
                for par in range(2):
                    sp.wait_ge(oT_ps, FREE + i * 4)
                    alone(sp, passed_sp)
                    sp.dma_start(oc[:, par, :, :], a["att_o"][:, bass.ds((i * 2 + par) * TILES, TILES), :])\
                        .then_inc(o_in[par], 16)
                    sp.wait_ge(x1_done, FREE + i * 4)
                    alone(sp, passed_sp)
                    sp.dma_start(xs[:, par, :, :],
                                 a["x"][0, bass.ds((i * 2 + par) * CW, CW), :].rearrange("(t p) d -> p t d", p=P))\
                        .then_inc(x_in[par], 16)
            for par in range(2):
                sp.wait_ge(o_in[par], 16 * CHUNKS // 2)
                sp.wait_ge(x_in[par], 16 * CHUNKS // 2)

        @block.tensor
        def _(pe):
            begin(pe, oT_ps, wo_ps, at_ps, x3_ps, h2_ps)
            pe.wait_ge(w_in, 48)
            with pe.Fori(0, CHUNKS // 2) as i:
                for par in range(2):
                    pe.wait_ge(o_in[par], i * 16 + 16)
                    pe.wait_ge(xa_done, FREE + i * 4)
                    for h in range(HALF):
                        for t in range(TILES):
                            mm = nc.tensor.transpose(bank(2 * par + h)[:, t * P:(t + 1) * P],
                                                     oc[:, par, t, h * P:(h + 1) * P], a["id_f"][:, :])
                        mm.then_inc(oT_ps, 1)
                for par in range(2):
                    pe.wait_ge(oT_ev, i * 4 + par * 2 + 2)
                    pe.wait_ge(x3T_ev, FREE + i * 4)
                    for t in range(TILES):
                        for h in range(HALF):
                            mm = nc.tensor.matmul(bank(4 + 2 * par + t // 2)[:, (t % 2) * D:(t % 2 + 1) * D],
                                                  oT[:, par, h, t * P:(t + 1) * P], a["wo_g"][:, h, :],
                                                  start=(h == 0), stop=(h == HALF - 1))
                        if t % 2:
                            mm.then_inc(wo_ps, 1)
                for par in range(2):
                    pe.wait_ge(h2_done, i * 2 + par + 1)
                    for h in range(HALF):
                        for t in range(TILES):
                            mm = nc.tensor.transpose(bank(2 * par + h)[:, t * P:(t + 1) * P],
                                                     h2[:, par, t, h * P:(h + 1) * P], a["id_f"][:, :])
                        mm.then_inc(h2_ps, 1)
                for par in range(2):
                    pe.wait_ge(xn_done, i * (4 * TILES) + (3 + par) * TILES)
                    for h in range(HALF):
                        for t in range(TILES):
                            mm = nc.tensor.transpose(bank(4 + 2 * par + h)[:, t * P:(t + 1) * P],
                                                     xn[:, par, t, h * P:(h + 1) * P], a["id_f"][:, :])
                        mm.then_inc(x3_ps, 1)
                for par in range(2):
                    pe.wait_ge(x3T_ev, FREE + i * 4 + par * 2 + 2)
                    pe.wait_ge(h2T_ev, i * 4 + par * 2 + 2)
                    for m in range(HALF):
                        for h in range(HALF):
                            mm = nc.tensor.matmul(bank(2 * par + m), w_a[:, h, m * P:(m + 1) * P],
                                                  x3T[:, par, h, :], start=(h == 0), stop=(h == HALF - 1))
                        mm.then_inc(at_ps, 1)

        @block.scalar
        def _(act):
            begin(act, x3T_ev)
            act.wait_ge(w_in, 48)
            with act.Fori(0, CHUNKS // 2) as i:
                for par in range(2):
                    act.wait_ge(oT_ps, FREE + i * 4 + par * 2 + 2)
                    act.wait_ge(wo_ps, FREE + i * 4)
                    for h in range(HALF):
                        nc.scalar.activation(oT[:, par, h, :], bank(2 * par + h), ACT.Copy).then_inc(oT_ev, 1)
                for par in range(2):
                    act.wait_ge(h2_ps, FREE + i * 4 + par * 2 + 2)
                    act.wait_ge(xa_done, FREE + i * 4)
                    for h in range(HALF):
                        nc.scalar.activation(h2T[:, par, h, :], bank(2 * par + h), ACT.Copy).then_inc(h2T_ev, 1)
                for par in range(2):
                    act.wait_ge(x3_ps, FREE + i * 4 + par * 2 + 2)
                    act.wait_ge(at_ps, FREE + i * 4)
                    for h in range(HALF):
                        nc.scalar.activation(x3T[:, par, h, :], bank(4 + 2 * par + h), ACT.Identity,
                                             bias=ln_col[:, HALF + h:HALF + h + 1], scale=ln_col[:, h:h + 1])\
                            .then_inc(x3T_ev, 1)

        @block.vector
        def _(dve):
            begin(dve, x1_done, xa_done)
            dve.wait_ge(w_in, 48)
            with dve.Fori(0, CHUNKS // 2) as i:
                def tile_stats(par, src, k):
                    base = i * (4 * TILES) + k * (2 * TILES) + par * TILES
                    for t in range(TILES):
                        nc.vector.bn_stats(stats[:, par, t, :], src(t)).then_inc(st_done, 1)
                    for t in range(TILES):
                        dve.wait_ge(st_done, base + t + 1)
                        alone(dve, passed_dve)
                        nc.vector.bn_aggr(mv[:, par, t, :], stats[:, par, t, :]).then_inc(mv_done, 1)

                for par in range(2):
                    dve.wait_ge(x_in[par], i * 16 + 16)
                    for b in range(2):
                        dve.wait_ge(wo_ps, FREE + i * 4 + par * 2 + b + 1)
                        nc.vector.tensor_tensor(
                            x1[:, bass.ds((i * 2 + par) * TILES + 2 * b, 2), :],
                            bank(4 + 2 * par + b).rearrange("p (t d) -> p t d", t=2),
                            xs[:, par, 2 * b:2 * b + 2, :], ALU.add).then_inc(x1_done, 1)
                    dve.wait_ge(x1_done, FREE + i * 4 + par * 2 + 2)
                    alone(dve, passed_dve)
                    tile_stats(par, lambda t, par=par: x1[:, bass.ds((i * 2 + par) * TILES + t, 1), :]
                               .rearrange("p o d -> p (o d)"), 0)
                for par in range(2):
                    dve.wait_ge(rstd_done, i * 4 + par + 1)
                    dve.wait_ge(x3_ps, FREE + i * 4)
                    for t in range(TILES):
                        nc.vector.tensor_scalar(
                            xn[:, par, t, :],
                            x1[:, bass.ds((i * 2 + par) * TILES + t, 1), :].rearrange("p o d -> p (o d)"),
                            mv[:, par, t, 0:1], rstd[:, par, t:t + 1], ALU.subtract, ALU.mult).then_inc(xn_done, 1)
                for par in range(2):
                    dve.wait_ge(h2_done, i * 2 + par + 1)
                    dve.wait_ge(xn_done, i * (4 * TILES) + (par + 1) * TILES)
                    tile_stats(par, lambda t, par=par: h2[:, par, t, :], 1)
                for par in range(2):
                    dve.wait_ge(rstd_done, i * 4 + 2 + par + 1)
                    for t in range(TILES):
                        nc.vector.tensor_scalar(xn[:, par, t, :], h2[:, par, t, :], mv[:, par, t, 0:1],
                                                rstd[:, par, t:t + 1], ALU.subtract, ALU.mult).then_inc(xn_done, 1)
                for par in range(2):
                    dve.wait_ge(h2T_ev, i * 4 + par * 2 + 2)
                    for m in range(HALF):
                        dve.wait_ge(at_ps, FREE + i * 4 + par * 2 + m + 1)
                        nc.vector.scalar_tensor_tensor(
                            out=xaT[:, m, bass.ds((i * 2 + par) * CW, CW)], in0=bank(2 * par + m),
                            scalar=ab_col[:, m:m + 1], in1=h2T[:, par, m, :], op0=ALU.add, op1=ALU.add)\
                            .then_inc(xa_done, 1)

        @block.gpsimd
        def _(pool):
            nc.gpsimd.memset(half_neg[:, :], -0.5).then_inc(half_set, 1)
            pool.wait_ge(half_set, 1)
            with pool.Fori(0, CHUNKS // 2) as i:
                def inverse_std(par, k):
                    n = i * 4 + 2 * k + par
                    pool.wait_ge(mv_done, (n + 1) * TILES)
                    alone(pool, passed_pool)
                    nc.gpsimd.tensor_scalar(var_e[:, par, :], mv[:, par, :, 1], EPS, None, ALU.add)\
                        .then_inc(var_done, 1)
                    pool.wait_ge(var_done, n + 1)
                    nc.gpsimd.tensor_tensor(rstd[:, par, :], var_e[:, par, :], half_neg[:, :], ALU.pow)\
                        .then_inc(rstd_done, 1)

                for par in range(2):
                    inverse_std(par, 0)
                for par in range(2):
                    pool.wait_ge(xn_done, i * (4 * TILES) + (par + 1) * TILES)
                    pool.wait_ge(h2_ps, FREE + i * 4)
                    nc.gpsimd.tensor_tensor(
                        h2[:, par, :, :], xn[:, par, :, :],
                        a["mod_bc"][:, 4 * D:5 * D].unsqueeze(1).broadcast_to([P, TILES, D]), ALU.mult).then_inc(scaled, 1)
                    pool.wait_ge(scaled, i * 2 + par + 1)
                    nc.gpsimd.tensor_tensor(
                        h2[:, par, :, :], h2[:, par, :, :],
                        a["mod_bc"][:, 3 * D:4 * D].unsqueeze(1).broadcast_to([P, TILES, D]), ALU.add).then_inc(h2_done, 1)
                for par in range(2):
                    inverse_std(par, 1)


def expert_block(nc, sem, bank, ctx, a, x1, xaT):
    def sb(name, shape, dt=F32):
        return ctx.enter_context(nc.sbuf_tensor(name, shape, dt))

    w1_s = sb("w1_s", [P, 2, HALF, HID])
    w2_s = sb("w2_s", [P, 2, HK, D])
    b1_s = sb("b1_s", [P, 2, HK])
    b2_s = sb("b2_s", [P, 2, HALF])
    w_n = sb("w_n", [P, HALF, D])
    nb_bc = sb("nb_bc", [P, D])
    hid = sb("hid", [P, HK, CW])
    eoT = sb("eoT", [P, HALF, CW])
    y = sb("y", [P, 2, 2, D])
    yg = sb("yg", [P, 2, 2, D])

    w_in, passed_sp = sem("e_w_in"), sem("e_passed_sp")
    w1_in, w2_in = [sem("w1_in0"), sem("w1_in1")], [sem("w2_in0"), sem("w2_in1")]
    h_ps, h_act, e_ps, e_ev, n_ps, y_pre, y_act, y_gate, y_done = (
        sem("h_ps"), sem("h_act"), sem("e_ps"), sem("e_ev"), sem("n_ps"), sem("y_pre"), sem("y_act"),
        sem("y_gate"), sem("y_done"))
    y_out = [sem("y_out0"), sem("y_out1")]
    HB = 4

    with nc.Block() as block:
        @block.sync
        def _(sp):
            begin(sp, *y_out)
            sp.dma_start(w_n[:, :, :], a["nextT"].rearrange("(h p) n -> p h n", p=P)).then_inc(w_in, 16)
            sp.dma_start(nb_bc[:, :], a["nextb"].rearrange("(a n) -> a n", a=1).broadcast_to([P, D])).then_inc(w_in, 16)
            def load(e, par):
                sp.dma_start(w1_s[:, par, :, :],
                             a["w1"][bass.ds(e, 1), :, :].rearrange("o (h p) n -> p (o h) n", p=P)).then_inc(w1_in[par], 16)
                sp.dma_start(b1_s[:, par, :], a["b1"][bass.ds(e, 1), :, :].rearrange("o p k -> p (o k)"))\
                    .then_inc(w1_in[par], 16)
                sp.dma_start(w2_s[:, par, :, :],
                             a["w2"][bass.ds(e, 1), :, :].rearrange("o (k p) n -> p (o k) n", p=P)).then_inc(w2_in[par], 16)
                sp.dma_start(b2_s[:, par, :], a["b2"][bass.ds(e, 1), :, :].rearrange("o p k -> p (o k)"))\
                    .then_inc(w2_in[par], 16)

            def store(e):
                for b in range(2):
                    sp.wait_ge(y_done, FREE + e * 2 + b + 1)
                    alone(sp, passed_sp)
                    sp.dma_start(a["out"][0, bass.ds(e * 256 + b * 2048, 256), :].rearrange("(t p) d -> p t d", p=P),
                                 y[:, b, :, :]).then_inc(y_out[b], 16)

            for par in range(2):
                load(par, par)
            with sp.Fori(0, EXPERTS // 2 - 1) as i:
                for par in range(2):
                    store(i * 2 + par)
                    load(i * 2 + par + 2, par)
            for par in range(2):
                store(EXPERTS - 2 + par)
            for b in range(2):
                sp.wait_ge(y_out[b], FREE + 16 * EXPERTS)

        @block.tensor
        def _(pe):
            begin(pe, n_ps, e_ps)
            pe.wait_ge(w_in, 32)
            with pe.Fori(0, EXPERTS // 2) as i:
                for par in range(2):
                    e = i * 2 + par
                    pe.wait_ge(w1_in[par], i * 32 + 32)
                    for k in range(HK):
                        pe.wait_ge(h_act, FREE + e * HK + (k - HB + 1 if k >= HB else 0))
                        for h in range(HALF):
                            rhs = xaT[:, h, :].rearrange("p (m s) -> p m s", m=2)[:, :, bass.ds(e * 256, 256)]
                            mm = nc.tensor.matmul(bank(k % HB), w1_s[:, par, h, k * P:(k + 1) * P], rhs,
                                                  start=(h == 0), stop=(h == HALF - 1))
                        mm.then_inc(h_ps, 1)
                    pe.wait_ge(w2_in[par], i * 32 + 32)
                    pe.wait_ge(e_ev, FREE + e * HALF)
                    for m in range(HALF):
                        for k in range(HK):
                            if m == 0:
                                pe.wait_ge(h_act, FREE + e * HK + k + 1)
                            mm = nc.tensor.matmul(bank(4 + m), w2_s[:, par, k, m * P:(m + 1) * P], hid[:, k, :],
                                                  start=(k == 0), stop=(k == HK - 1))
                        mm.then_inc(e_ps, 1)
                    pe.wait_ge(e_ev, FREE + e * HALF + HALF)
                    for b in range(2):
                        pe.wait_ge(y_pre, FREE + e * 2 + b if b == 0 else e * 2)
                        for t in range(2):
                            for h in range(HALF):
                                tok = (2 * b + t) * P
                                mm = nc.tensor.matmul(bank(6 + b)[:, t * D:(t + 1) * D], eoT[:, h, tok:tok + P],
                                                      w_n[:, h, :], start=(h == 0), stop=(h == HALF - 1))
                        mm.then_inc(n_ps, 1)

        @block.scalar
        def _(act):
            begin(act, h_act)
            with act.Fori(0, EXPERTS // 2) as i:
                for par in range(2):
                    e = i * 2 + par
                    act.wait_ge(w1_in[par], i * 32 + 32)
                    act.wait_ge(e_ps, FREE + e * HALF)
                    for k in range(HK):
                        act.wait_ge(h_ps, e * HK + k + 1)
                        nc.scalar.activation(hid[:, k, :], bank(k % HB), ACT.Gelu, bias=b1_s[:, par, k:k + 1])\
                            .then_inc(h_act, 1)
                    for b in range(2):
                        act.wait_ge(y_pre, FREE + e * 2 + b + 1)
                        act.wait_ge(y_done, FREE + e * 2)
                        nc.scalar.activation(yg[:, b, :, :], y[:, b, :, :], ACT.Gelu).then_inc(y_act, 1)

        @block.vector
        def _(dve):
            begin(dve, e_ev, y_pre, y_done)
            dve.wait_ge(w_in, 32)
            with dve.Fori(0, EXPERTS // 2) as i:
                for par in range(2):
                    e = i * 2 + par
                    dve.wait_ge(w2_in[par], i * 32 + 32)
                    dve.wait_ge(n_ps, FREE + e * 2)
                    for m in range(HALF):
                        dve.wait_ge(e_ps, FREE + e * HALF + m + 1)
                        nc.vector.tensor_scalar(eoT[:, m, :], bank(4 + m), b2_s[:, par, m:m + 1], None, ALU.add)\
                            .then_inc(e_ev, 1)
                    for b in range(2):
                        dve.wait_ge(n_ps, FREE + e * 2 + b + 1)
                        dve.wait_ge(y_out[b], FREE + e * 16)
                        nc.vector.tensor_tensor(y[:, b, :, :], bank(6 + b).rearrange("p (t d) -> p t d", t=2),
                                                nb_bc[:, :].unsqueeze(1).broadcast_to([P, 2, D]), ALU.add)\
                            .then_inc(y_pre, 1)

                    for b in range(2):
                        dve.wait_ge(y_act, e * 2 + b + 1)
                        nc.vector.tensor_tensor(yg[:, b, :, :], yg[:, b, :, :],
                                                a["mod_bc"][:, 5 * D:6 * D].unsqueeze(1).broadcast_to([P, 2, D]),
                                                ALU.mult).then_inc(y_gate, 1)
                    for b in range(2):
                        dve.wait_ge(y_gate, e * 2 + b + 1)
                        nc.vector.tensor_tensor(y[:, b, :, :], yg[:, b, :, :],
                                                x1[:, bass.ds(e * 2 + 16 * b, 2), :], ALU.add).then_inc(y_done, 1)


def rope_table():
    inv = (1.0 / np.float32(10000.0) ** (np.arange(0, HD, 2, dtype=np.float32) / np.float32(HD))).astype(np.float32)
    angle = (np.arange(S, dtype=np.float32)[None, :] * inv[:, None]).astype(np.float32).astype(np.float64)
    cos = np.repeat(np.cos(angle), 2, axis=0)
    sin = np.repeat(np.sin(angle), 2, axis=0)
    sin[0::2] *= -1.0
    both = np.stack([np.tile(cos, (P // HD, 1)), np.tile(sin, (P // HD, 1))], axis=1)
    return np.ascontiguousarray(both.astype(np.float32))


def constants():
    mask = np.zeros((P, CW), np.float32)
    q, k = np.arange(P)[:, None], np.arange(P)[None, :]
    mask[:, CW - P:] = np.where(k > q, np.float32(-1e38), np.float32(0))
    later = np.where(q > k, np.float32(-1e30), np.float32(0)).astype(mybir.dt.np(BF16))
    last = np.zeros((MROWS, JH, S), mybir.dt.np(BF16))
    for j in range(JH):
        last[PARTS * j:PARTS * (j + 1), j, :] = 1
    return {"rope": rope_table(), "ident": np.eye(P, dtype=np.float32), "mask": mask, "later": later, "lastones": last}


def kernel(**inputs):
    import concourse.bacc as _bacc
    from concourse.bass_utils import run_bass_kernel_spmd as _run

    a = {k: np.asarray(v) for k, v in inputs.items()}

    def quads(w):
        return w.T.reshape(D, QUADS, JH * HD)

    def column(v):
        return v.reshape(HALF, P).T

    arrays = {
        "x": a["L0_attn_x"],
        "wqk": np.concatenate([quads(a["L0_attn_Wq"]), quads(a["L0_attn_Wk"])], axis=2),
        "wvT": a["L0_attn_Wv"].T,
        "woT": a["L0_attn_Wo"].T,
        "lnsb": np.concatenate([column(a["L0_ffn_ln_scale"]), column(a["L0_ffn_ln_bias"])], axis=1),
        "attnT": a["L0_ffn_attn_w"].T,
        "attnb": column(a["L0_ffn_attn_b"]),
        "w1": a["L0_ffn_w1"],
        "b1": a["L0_ffn_b1"].reshape(EXPERTS, HK, P).transpose(0, 2, 1),
        "w2": a["L0_ffn_w2"],
        "b2": a["L0_ffn_b2"].reshape(EXPERTS, HALF, P).transpose(0, 2, 1),
        "nextT": a["L0_ffn_next_w"].T,
        "nextb": a["L0_ffn_next_b"],
        "cvec": column(a["L0_c"]),
        "wmod": a["L0_wmod"],
        **constants(),
    }
    nc = _bacc.Bacc("TRN2", target_bir_lowering=False, num_devices=1)
    args, given = {}, {}
    for name, v in arrays.items():
        v = np.ascontiguousarray(v)
        given[f"in_{name}"] = v
        args[name] = nc.dram_tensor(f"in_{name}", v.shape, mybir.dt.from_np(v.dtype), kind="ExternalInput").ap()
    args["out"] = nc.dram_tensor("out_0", (1, S, D), F32, kind="ExternalOutput").ap()
    build(nc, **args)
    r = _run(nc, [given], core_ids=[0])
    return r.results[0]["out_0"]
```

```python
from contextlib import ExitStack

import numpy as np

import concourse.bass as bass
from concourse import mybir
from concourse.alu_op_type import AluOpType as ALU

F32 = mybir.dt.float32
BF16 = mybir.dt.bfloat16
ACT = mybir.ActivationFunctionType
AX_X = mybir.AxisListType.X

P = 128
S = 4096
D = 256
HEADS = 16
HD = D // HEADS
QUADS = 4
JH = HEADS // QUADS
CW = 512
CHUNKS = S // CW
TILES = CW // P
HALF = D // P
PARTS = 3
Q_PART = (0, 1, 2, 0, 0, 1)
K_PART = (0, 1, 0, 1, 2, 0)
Q_RUNS = ((0, 0, 3), (3, 0, 1), (4, 0, 2))
K_RUNS = ((0, 0, 2), (2, 0, 3), (5, 0, 1))
KROWS = len(Q_PART) * HD
MROWS = PARTS * JH
VW = HD + 1
EXPERTS = 8
HID = 1024
HK = HID // P
NEG = -3.0e38
EPS = 1e-5
FREE = 1


def first_step(c):
    return 2 * c * (c + 1)


STEPS = [(c, kb) for c in range(CHUNKS) for kb in range(TILES * (c + 1))]
NSTEPS = len(STEPS)
SBANKS = 3
UNITS = NSTEPS * JH


def max_units(c):
    return ([("full", c, t, kc, pair) for kc in range(c) for t in range(TILES) for pair in range(2)]
            + [("diag", c, t, c, pair) for t in range(TILES) for pair in range(2)])


def late_turns(chunks, lag):
    out, due = [], []
    for c in chunks:
        for u in max_units(c):
            out.append(u)
            for d in list(due):
                d[1] -= 1
                if d[1] == 0:
                    out.append(("turn", d[0], 0, 0, 0))
                    due.remove(d)
        due.append([c, lag])
    return out + [("turn", d[0], 0, 0, 0) for d in due]


AHEAD = 3
HEAD_UNITS = late_turns(range(AHEAD), 4)


def side_cost(unit):
    kind, c, t, kc, pair = unit
    if kind == "full":
        return 125 + 2 * CW * 1.04
    if kind == "diag":
        return 2 * (125 + (t + 1) * P * 1.04)
    return 400


def earliest_step(unit, next_quad):
    kind, c, t, kc, pair = unit
    if kind == "norm":
        return min(first_step(c + 1) + 3, NSTEPS)
    if next_quad:
        return first_step(CHUNKS - 1) + TILES * (max(kc, c if kind == "turn" else kc) + 1) + 3
    return first_step(c - AHEAD) + 2


def side_units():
    at = [[[] for _ in range(JH)] for _ in range(NSTEPS + 1)]
    width = [min(CW, CW * (c + 1) - P * kb) for c, kb in STEPS]
    begins = [sum(width[:s]) for s in range(NSTEPS + 1)]
    queue = [(u, False) for u in late_turns(range(AHEAD, CHUNKS), LAG)] + [(u, True) for u in HEAD_UNITS]
    norms = [("norm", c, 0, 0, 0) for c in range(CHUNKS)]
    due, work = [], 0
    for unit, next_quad in queue:
        work += side_cost(unit)
        if unit[0] == "turn":
            due.append((begins[NSTEPS - 1 if next_quad else first_step(unit[1]) - TURNED], work))
    done = credit = 0.0
    for s in range(NSTEPS):
        for j in range(JH):
            now = begins[s] + width[s] * j / JH
            pace = max([(w - done) / max(d - now, 1) for d, w in due if w > done], default=0)
            credit = min(credit + pace * width[s] / JH, 2500)
            if norms and s >= earliest_step(norms[0], False) and j == JH - 1:
                at[s][j].append(norms.pop(0))
                credit -= 400
            while queue and s >= earliest_step(*queue[0]) and (credit > side_cost(queue[0][0]) or s == NSTEPS - 1
                                                               and j == JH - 1 and len(queue) > 2):
                unit = queue.pop(0)[0]
                credit -= side_cost(unit)
                done += side_cost(unit)
                at[s][j].append(unit)
    at[NSTEPS][0] += [u for u, _ in queue] + norms
    return at


TURNED = 3
LAG = 3
SIDE = side_units()
SIDE_FLAT = [u for step in SIDE for us in step for u in us]
HEAD_N = len(HEAD_UNITS)
SIDE_N = len(SIDE_FLAT)
assert SIDE_N % 2 == 0
assert all(s < first_step(u[1]) or u[1] < AHEAD
           for s, step in enumerate(SIDE) for us in step for u in us if u[0] == "turn")


def slot_uses(slot):
    before = len([n for n in range(HEAD_N) if n % 2 == slot])
    return before, SIDE_N // 2


def count_units(kinds, until=None):
    return len([u for u in (SIDE_FLAT if until is None else SIDE_FLAT[:until]) if u[0] in kinds])


def build(nc, x, wqk, wvT, woT, lnsb, attnT, attnb, w1, b1, w2, b2, nextT, nextb, cvec, wmod,
          rope, ident, mask, later, lastones, out):
    parts = nc.dram_tensor("parts_scratch", [PARTS, 2, HD // 2, 2 * JH, QUADS, S], BF16, kind="Internal").ap()

    with ExitStack() as whole:
        def sem(name):
            return whole.enter_context(nc.semaphore(name))

        def keep(name, shape, dt=F32):
            return whole.enter_context(nc.sbuf_tensor(name, shape, dt))

        PS = whole.enter_context(nc.psum_tensor("banks", [P, 8 * 512], F32))

        def bank(b, n=1):
            return PS[:, b * 512:(b + n) * 512]

        id_f = keep("id_f", [P, P])
        mod_bc = keep("mod_bc", [P, 6 * D])
        mod_col = keep("mod_col", [P, 16])
        wo_g = keep("wo_g", [P, HALF, D])
        att_o = keep("att_o", [P, S // P, D])

        project(nc, sem, bank, whole, dict(
            x=x, wqk=wqk, wvT=wvT, woT=woT, cvec=cvec, wmod=wmod, rope=rope, ident=ident, parts=parts,
            id_f=id_f, mod_bc=mod_bc, mod_col=mod_col, wo_g=wo_g, att_o=att_o, mask=mask, later=later, lastones=lastones))
        feed(nc, sem, bank, dict(
            x=x, lnsb=lnsb, attnT=attnT, attnb=attnb, w1=w1, b1=b1, w2=w2, b2=b2, nextT=nextT, nextb=nextb,
            id_f=id_f, mod_bc=mod_bc, mod_col=mod_col, wo_g=wo_g, att_o=att_o, out=out))


def begin(engine, *semaphores):
    for s in semaphores:
        engine.sem_inc(s, FREE)


def alone(engine, passed):
    engine.sem_inc(passed, 1)


def project(nc, sem, bank, whole, a):
    with ExitStack() as ctx:
        v_all = ctx.enter_context(nc.sbuf_tensor("v_all", [P, QUADS, S // P, JH, VW], F32))
        with ExitStack() as mine:
            project_block(nc, sem, bank, mine, a, v_all)
        with ExitStack() as mine:
            attend_block(nc, sem, bank, mine, a, v_all)


def project_block(nc, sem, bank, ctx, a, v_all):
    def sb(name, shape, dt=F32):
        return ctx.enter_context(nc.sbuf_tensor(name, shape, dt))

    w_qk = sb("w_qk", [P, HALF, 2, 2, P])
    w_v = sb("w_v", [P, HALF, D])
    w_m = sb("w_m", [P, HALF, 6 * D])
    w_o = sb("w_o", [P, HALF, D])
    c_col = sb("c_col", [P, HALF])
    c_exp = sb("c_exp", [P, HALF])
    c_inv = sb("c_inv", [P, HALF])
    c_silu = sb("c_silu", [P, HALF])
    c_wide = sb("c_wide", [P, HALF, P])
    ones = sb("ones", [P, P])
    gate_s = sb("gate_s", [P, 2, D])
    gate_m = sb("gate_m", [P, 2, D])
    half_neg = sb("half_neg", [P, TILES])
    xs = sb("xs", [P, 2, TILES, D])
    stats = sb("stats", [P, 2, TILES, 6])
    mv = sb("mv", [P, 2, TILES, 2])
    var_e = sb("var_e", [P, 2, TILES])
    rstd = sb("rstd", [P, 2, TILES])
    xn = sb("xn", [P, TILES, D])
    hT = sb("hT", [P, 2, HALF, CW])
    cs = sb("cs", [P, 2, 2, CW])
    qk = sb("qk", [P, 2, 2, CW])
    rot = sb("rot", [P, 2, 2, 2, CW])
    rest = sb("rest", [P, 2, 2, 2, CW])
    pp = [sb(f"p{n + 1}", [P, 2, 2, CW], BF16) for n in range(PARTS)]

    passed_dve, passed_pool, passed_sp = sem("passed_dve"), sem("passed_pool"), sem("passed_sp")
    c_in, id_in, wmod_in, wqk_in, wv_in, late_in = (sem("c_in"), sem("id_in"), sem("wmod_in"), sem("wqk_in"),
                                                    sem("wv_in"), sem("late_in"))
    ones_set, silu_e, silu_s = sem("ones_set"), sem("silu_e"), sem("silu_s")
    mod_ps, mod_ev, gate_st, wo_rdy, const_p = sem("mod_ps"), sem("mod_ev"), sem("gate_st"), sem("wo_rdy"), sem("const_p")
    x_in = [sem("x_in0"), sem("x_in1")]
    cs_in = [sem("cs_in0"), sem("cs_in1")]
    st_done, mv_done, var_done, rstd_done, xn_done = (sem("st_done"), sem("mv_done"), sem("var_done"),
                                                      sem("rstd_done"), sem("xn_done"))
    hT_ps, hT_ev = sem("hT_ps"), sem("hT_ev")
    qk_ps, qk_ev = sem("qk_ps"), sem("qk_ev")
    v_ps, v_ev = sem("v_ps"), sem("v_ev")
    cos_done, sin_done, rot_done = sem("cos_done"), sem("sin_done"), sem("rot_done")
    p1_done, r1_done, p2_done, p3_done = sem("p1_done"), sem("r1_done"), sem("p2_done"), sem("p3_done")
    stored = [sem(f"stored{n}") for n in range(PARTS)]
    STORES = 4
    T_BANKS, V_BANKS, QK_BANKS = (0, 1), (2, 3), 4

    def slots(engine, front, back, loops=CHUNKS // 2 - 1):
        front(0, 0)
        with engine.Fori(0, loops) as i:
            for off in (1, 2):
                front(i, off)
                back(i, off - 1)
        for c in range(2 * loops + 1, CHUNKS + 1):
            if c < CHUNKS:
                front(c // 2, c % 2)
            back((c - 1) // 2, (c - 1) % 2)

    def is_last(i, off):
        return isinstance(i, int) and 2 * i + off == CHUNKS - 1

    def is_first(i, off):
        return isinstance(i, int) and 2 * i + off == 0

    with nc.Block() as block:
        @block.sync
        def _(sp):
            begin(sp, *stored)

            def load_x(i, off):
                if off >= 2:
                    sp.wait_ge(xn_done, TILES * (i * 2 + off - 1))
                    alone(sp, passed_sp)
                sp.dma_start(xs[:, off % 2, :, :],
                             a["x"][0, bass.ds((i * 2 + off) * CW, CW), :].rearrange("(t p) d -> p t d", p=P))\
                    .then_inc(x_in[off % 2], 16)

            def load_cs(i, off):
                if off >= 2:
                    sp.wait_ge(cos_done, 2 * (i * 2 + off - 1))
                    sp.wait_ge(sin_done, 2 * (i * 2 + off - 1))
                    alone(sp, passed_sp)
                sp.dma_start(cs[:, off % 2, :, :], a["rope"][:, :, bass.ds((i * 2 + off) * CW, CW)])\
                    .then_inc(cs_in[off % 2], 16)

            def store(i, off):
                for n, done in enumerate((p1_done, p2_done, p3_done)):
                    sp.wait_ge(done, (FREE if n == 2 else 0) + 2 * (i * 2 + off) + 2)
                    alone(sp, passed_sp)
                    for z in range(2):
                        rows = slice(z * P // 2, (z + 1) * P // 2)
                        for eo in range(2):
                            sp.dma_start(
                                a["parts"][n, eo, :, :, 2 * z:2 * z + 2, bass.ds((i * 2 + off) * CW, CW)]
                                .rearrange("d h b s -> (d h) b s"),
                                pp[n][rows, eo, :, :]).then_inc(stored[n], 16)

            sp.dma_start(c_col[:, :], a["cvec"]).then_inc(c_in, 16)
            load_x(0, 0)
            sp.dma_start(a["id_f"][:, :], a["ident"]).then_inc(id_in, 16)
            w_mod = a["wmod"].rearrange("(h p) n -> p h n", p=P)
            sp.dma_start(w_m[:, :, 0:2 * D], w_mod[:, :, 0:2 * D]).then_inc(wmod_in, 16)
            sp.dma_start(w_qk[:, :, :, :, :], a["wqk"].rearrange("(h p) e b n -> p h e b n", p=P)).then_inc(wqk_in, 16)
            load_x(0, 1)
            load_cs(0, 0)
            sp.dma_start(w_v[:, :, :], a["wvT"].rearrange("(h p) n -> p h n", p=P)).then_inc(wv_in, 16)
            load_cs(0, 1)
            load_x(0, 2)
            sp.dma_start(w_m[:, :, 2 * D:], w_mod[:, :, 2 * D:]).then_inc(late_in, 16)
            sp.dma_start(w_o[:, :, :], a["woT"].rearrange("(h p) n -> p h n", p=P)).then_inc(late_in, 16)
            with sp.Fori(0, 2) as i:
                for off in (1, 2):
                    load_x(i, off + 2)
                    load_cs(i, off + 1)
                    store(i, off - 1)
            for c in range(5, CHUNKS + 1):
                if c + 2 < CHUNKS:
                    load_x(c // 2, c % 2 + 2)
                if c + 1 < CHUNKS:
                    load_cs((c - 1) // 2, (c - 1) % 2 + 2)
                store((c - 1) // 2, (c - 1) % 2)
            for n in range(PARTS):
                sp.wait_ge(stored[n], FREE + 16 * STORES * CHUNKS)

        @block.gpsimd
        def _(pool):
            begin(pool, p3_done)
            nc.gpsimd.memset(half_neg[:, :], -0.5).then_inc(const_p, 1)
            nc.gpsimd.memset(ones[:, :], 1.0).then_inc(ones_set, 1)
            pool.wait_ge(const_p, 1)

            def inverse_std(i, off):
                pool.wait_ge(mv_done, TILES * (i * 2 + off + 1))
                if off >= 2:
                    pool.wait_ge(xn_done, TILES * (i * 2 + off - 1))
                alone(pool, passed_pool)
                nc.gpsimd.tensor_scalar(var_e[:, off % 2, :], mv[:, off % 2, :, 1], EPS, None, ALU.add)\
                    .then_inc(var_done, 1)
                pool.wait_ge(var_done, i * 2 + off + 1)
                nc.gpsimd.tensor_tensor(rstd[:, off % 2, :], var_e[:, off % 2, :], half_neg[:, :], ALU.pow)\
                    .then_inc(rstd_done, 1)

            def front(i, off):
                if not is_last(i, off):
                    inverse_std(i, off + 1)
                par = off % 2
                pool.wait_ge(cs_in[par], 16 * (i + off // 2 + 1))
                if off:
                    pool.wait_ge(p3_done, FREE + 2 * (i * 2 + off - 1))
                for eo in range(2):
                    pool.wait_ge(qk_ev, 2 * (i * 2 + off) + eo + 1)
                    nc.gpsimd.tensor_tensor(rest[:, par, eo, :, :], qk[:, eo, :, :],
                                            cs[:, par, 1:2, :].broadcast_to([P, 2, CW]), ALU.mult)\
                        .then_inc(sin_done, 1)

            def back(i, off):
                pool.wait_ge(stored[2], FREE + 16 * STORES * (i * 2 + off))
                for eo in range(2):
                    pool.wait_ge(r1_done, FREE + 2 * (i * 2 + off) + eo + 1)
                    pool.wait_ge(p2_done, 2 * (i * 2 + off) + eo + 1)
                    nc.gpsimd.tensor_tensor(pp[2][:, eo, :, :], rest[:, off % 2, eo, :, :], pp[1][:, eo, :, :],
                                            ALU.subtract).then_inc(p3_done, 1)

            inverse_std(0, 0)
            nc.gpsimd.memset(v_all[:, :, :, :, HD:VW], 1.0).then_inc(const_p, 1)
            slots(pool, front, back)

        @block.vector
        def _(dve):
            begin(dve, r1_done)

            def moments(i, off):
                par = off % 2
                dve.wait_ge(x_in[par], 16 * (i + off // 2 + 1))
                for t in range(TILES):
                    nc.vector.bn_stats(stats[:, par, t, :], xs[:, par, t, :]).then_inc(st_done, 1)
                for t in range(TILES):
                    dve.wait_ge(st_done, TILES * (i * 2 + off) + t + 1)
                    alone(dve, passed_dve)
                    nc.vector.bn_aggr(mv[:, par, t, :], stats[:, par, t, :]).then_inc(mv_done, 1)

            def normalise(i, off):
                par = off % 2
                dve.wait_ge(rstd_done, i * 2 + off + 1)
                if off:
                    dve.wait_ge(hT_ps, HALF * (i * 2 + off))
                for t in range(TILES):
                    nc.vector.tensor_scalar(xn[:, t, :], xs[:, par, t, :], mv[:, par, t, 0:1],
                                            rstd[:, par, t:t + 1], ALU.subtract, ALU.mult).then_inc(xn_done, 1)

            def by_cos(i, off):
                par = off % 2
                dve.wait_ge(cs_in[par], 16 * (i + off // 2 + 1))
                if off:
                    dve.wait_ge(r1_done, FREE + 2 * (i * 2 + off - 1))
                for eo in range(2):
                    dve.wait_ge(qk_ev, 2 * (i * 2 + off) + eo + 1)
                    nc.vector.tensor_tensor(rot[:, par, eo, :, :], qk[:, eo, :, :],
                                            cs[:, par, 0:1, :].broadcast_to([P, 2, CW]), ALU.mult)\
                        .then_inc(cos_done, 1)

            def rotate(i, off):
                par = off % 2
                dve.wait_ge(sin_done, 2 * (i * 2 + off) + 2)
                dve.wait_ge(cos_done, 2 * (i * 2 + off) + 2)
                for eo in range(2):
                    nc.vector.tensor_tensor(rot[:, par, eo, :, :], rot[:, par, eo, :, :], rest[:, par, 1 - eo, :, :],
                                            ALU.subtract if eo == 0 else ALU.add).then_inc(rot_done, 1)

            def cut(i, off):
                par = off % 2
                dve.wait_ge(rot_done, 2 * (i * 2 + off) + 2)
                for eo in range(2):
                    dve.wait_ge(p1_done, 2 * (i * 2 + off) + eo + 1)
                    nc.vector.tensor_tensor(rest[:, par, eo, :, :], rot[:, par, eo, :, :], pp[0][:, eo, :, :],
                                            ALU.subtract).then_inc(r1_done, 1)

            def modulation():
                dve.wait_ge(mod_ps, 3)
                for n in (1, 2):
                    nc.vector.tensor_copy(a["mod_bc"][:, n * 512:(n + 1) * 512], bank(n - 1)).then_inc(mod_ev, 1)
                for k, plus in ((2, 0.0), (3, 1.0)):
                    nc.vector.tensor_scalar(a["mod_col"][:, 2 * k:2 * k + 2], bank(QK_BANKS)[:, 2 * k:2 * k + 2], plus,
                                            None, ALU.add).then_inc(mod_ev, 1)
                dve.wait_ge(mod_ev, 6)
                nc.vector.tensor_scalar(a["mod_bc"][:, 4 * D:5 * D], a["mod_bc"][:, 4 * D:5 * D], 1.0, None, ALU.add)\
                    .then_inc(mod_ev, 1)
                for n, k in enumerate((2, 5)):
                    gate = a["mod_bc"][:, k * D:(k + 1) * D]
                    nc.vector.tensor_scalar(gate_s[:, n, :], gate, 0.0, 2.0, ALU.is_ge, ALU.mult).then_inc(gate_st, 1)
                    nc.vector.scalar_tensor_tensor(out=gate_m[:, n, :], in0=gate, scalar=-1.0, in1=gate,
                                                   op0=ALU.mult, op1=ALU.max).then_inc(gate_st, 1)
                dve.wait_ge(gate_st, 4)
                for n in range(2):
                    nc.vector.tensor_scalar(gate_m[:, n, :], gate_m[:, n, :], 0.25, None, ALU.max).then_inc(gate_st, 1)
                dve.wait_ge(gate_st, 6)
                for n, k in enumerate((2, 5)):
                    nc.vector.scalar_tensor_tensor(out=a["mod_bc"][:, k * D:(k + 1) * D], in0=gate_s[:, n, :],
                                                   scalar=-1.0, in1=gate_m[:, n, :], op0=ALU.add, op1=ALU.mult)\
                        .then_inc(gate_st, 1)
                dve.wait_ge(gate_st, 8)
                for h in range(HALF):
                    nc.vector.tensor_tensor(a["wo_g"][:, h, :], w_o[:, h, :], a["mod_bc"][:, 2 * D:3 * D], ALU.mult)\
                        .then_inc(wo_rdy, 1)
                dve.wait_ge(wo_rdy, 2)

            dve.wait_ge(silu_e, 1)
            nc.vector.tensor_scalar(c_inv[:, :], c_exp[:, :], 1.0, None, ALU.add).then_inc(silu_s, 1)
            dve.wait_ge(silu_s, 1)
            nc.vector.reciprocal(c_exp[:, :], c_inv[:, :]).then_inc(silu_s, 1)
            dve.wait_ge(silu_s, 2)
            nc.vector.tensor_tensor(c_silu[:, :], c_col[:, :], c_exp[:, :], ALU.mult).then_inc(silu_s, 1)
            moments(0, 0)
            normalise(0, 0)
            dve.wait_ge(mod_ps, 1)
            for k, plus in ((0, 0.0), (1, 1.0)):
                nc.vector.tensor_scalar(a["mod_col"][:, 2 * k:2 * k + 2], bank(QK_BANKS)[:, 2 * k:2 * k + 2], plus,
                                        None, ALU.add).then_inc(mod_ev, 1)
            dve.wait_ge(silu_s, 3)
            dve.wait_ge(ones_set, 1)
            for h in range(HALF):
                nc.vector.tensor_scalar(c_wide[:, h, :], ones[:, :], c_silu[:, h:h + 1], None, ALU.mult)\
                    .then_inc(silu_s, 1)

            moments(0, 1)
            normalise(0, 1)
            by_cos(0, 0)
            with dve.Fori(0, CHUNKS // 2 - 1) as i:
                for off in (1, 2):
                    moments(i, off + 1)
                    rotate(i, off - 1)
                    normalise(i, off + 1)
                    by_cos(i, off)
                    cut(i, off - 1)
            last = CHUNKS // 2 - 1
            rotate(last, 0)
            by_cos(last, 1)
            cut(last, 0)
            rotate(last, 1)
            cut(last, 1)
            dve.wait_ge(late_in, 32)
            modulation()

        @block.scalar
        def _(act):
            act.wait_ge(c_in, 16)
            nc.scalar.activation(c_exp[:, :], c_col[:, :], ACT.Exp, scale=-1.0).then_inc(silu_e, 1)
            act.wait_ge(mod_ev, 2)

            def modulate(i, off):
                if off >= 2:
                    act.wait_ge(v_ps, TILES * (i * 2 + off - 1))
                for h in range(HALF):
                    act.wait_ge(hT_ps, HALF * (i * 2 + off) + h + 1)
                    nc.scalar.activation(hT[:, off % 2, h, :], bank(T_BANKS[h]), ACT.Identity,
                                         bias=a["mod_col"][:, h:h + 1], scale=a["mod_col"][:, 2 + h:3 + h])\
                        .then_inc(hT_ev, 1)

            def take_qk(i, off):
                for eo in range(2):
                    act.wait_ge(qk_ps, 2 * (i * 2 + off) + eo + 1)
                    if off:
                        act.wait_ge(cos_done, 2 * (i * 2 + off - 1) + eo + 1)
                        act.wait_ge(sin_done, 2 * (i * 2 + off - 1) + eo + 1)
                    nc.scalar.activation(qk[:, eo, :, :], bank(QK_BANKS + 2 * eo, 2).rearrange("p (b s) -> p b s", b=2),
                                         ACT.Copy).then_inc(qk_ev, 1)

            def take_v(i, off):
                for t in range(TILES):
                    act.wait_ge(v_ps, TILES * (i * 2 + off) + t - t % 2 + 2)
                    nc.scalar.activation(
                        v_all[:, :, bass.ds((i * 2 + off) * TILES + t, 1), :, 0:HD]
                        .rearrange("p g o j d -> p g (o j) d"),
                        bank(V_BANKS[t // 2])[:, (t % 2) * D:(t % 2 + 1) * D]
                        .rearrange("p (g j d) -> p g j d", g=QUADS, j=JH), ACT.Copy).then_inc(v_ev, 1)

            def part1(i, off):
                act.wait_ge(stored[0], FREE + 16 * STORES * (i * 2 + off))
                act.wait_ge(r1_done, FREE + 2 * (i * 2 + off))
                for eo in range(2):
                    act.wait_ge(rot_done, 2 * (i * 2 + off) + eo + 1)
                    nc.scalar.activation(pp[0][:, eo, :, :], rot[:, off % 2, eo, :, :], ACT.Copy).then_inc(p1_done, 1)

            def part2(i, off):
                act.wait_ge(stored[1], FREE + 16 * STORES * (i * 2 + off))
                act.wait_ge(p3_done, FREE + 2 * (i * 2 + off))
                for eo in range(2):
                    act.wait_ge(r1_done, FREE + 2 * (i * 2 + off) + eo + 1)
                    nc.scalar.activation(pp[1][:, eo, :, :], rest[:, off % 2, eo, :, :], ACT.Copy).then_inc(p2_done, 1)

            modulate(0, 0)
            take_qk(0, 0)
            modulate(0, 1)
            take_v(0, 0)
            with act.Fori(0, CHUNKS // 2 - 1) as i:
                for off in (1, 2):
                    part1(i, off - 1)
                    take_qk(i, off)
                    modulate(i, off + 1)
                    take_v(i, off)
                    part2(i, off - 1)
            last = CHUNKS // 2 - 1
            part1(last, 0)
            take_qk(last, 1)
            take_v(last, 1)
            part2(last, 0)
            part1(last, 1)
            part2(last, 1)

        @block.tensor
        def _(pe):
            def mod_columns(chunks):
                for k, m in chunks:
                    for half in range(HALF):
                        for h in range(HALF):
                            col = m * D + half * P
                            mm = nc.tensor.matmul(bank(QK_BANKS)[:, 2 * k + half:2 * k + half + 1],
                                                  w_m[:, h, col:col + P], c_silu[:, h:h + 1],
                                                  start=(h == 0), stop=(h == HALF - 1))
                mm.then_inc(mod_ps, 1)

            def turn(i, off):
                pe.wait_ge(xn_done, TILES * (i * 2 + off + 1))
                if off:
                    pe.wait_ge(hT_ev, HALF * (i * 2 + off))
                for h in range(HALF):
                    for t in range(TILES):
                        mm = nc.tensor.transpose(bank(T_BANKS[h])[:, t * P:(t + 1) * P], xn[:, t, h * P:(h + 1) * P],
                                                 a["id_f"][:, :])
                    mm.then_inc(hT_ps, 1)

            def front(i, off):
                pe.wait_ge(hT_ev, HALF * (i * 2 + off + 1))
                for eo in range(2):
                    if off:
                        pe.wait_ge(qk_ev, 2 * (i * 2 + off - 1) + eo + 1)
                    for b in range(2):
                        for h in range(HALF):
                            mm = nc.tensor.matmul(bank(QK_BANKS + 2 * eo + b), w_qk[:, h, eo, b, :],
                                                  hT[:, off % 2, h, :], start=(h == 0), stop=(h == HALF - 1))
                    mm.then_inc(qk_ps, 1)
                if not is_last(i, off):
                    turn(i, off + 1)
                if is_first(i, off):
                    pe.wait_ge(wv_in, 16)
                if off:
                    pe.wait_ge(v_ev, TILES * (i * 2 + off))
                for t in range(TILES):
                    for h in range(HALF):
                        mm = nc.tensor.matmul(bank(V_BANKS[t // 2])[:, (t % 2) * D:(t % 2 + 1) * D],
                                              hT[:, off % 2, h, t * P:(t + 1) * P], w_v[:, h, :],
                                              start=(h == 0), stop=(h == HALF - 1))
                    mm.then_inc(v_ps, 1)

            def nothing(i, off):
                pass

            pe.wait_ge(id_in, 16)
            turn(0, 0)
            pe.wait_ge(silu_s, 3)
            pe.wait_ge(wmod_in, 16)
            mod_columns(((0, 0), (1, 1)))
            pe.wait_ge(wqk_in, 16)
            pe.wait_ge(mod_ev, 2)
            slots(pe, front, nothing)
            pe.wait_ge(silu_s, 5)
            pe.wait_ge(late_in, 32)
            pe.wait_ge(hT_ev, HALF * CHUNKS)
            for n in (1, 2):
                for h in range(HALF):
                    mm = nc.tensor.matmul(bank(n - 1), c_wide[:, h, :], w_m[:, h, n * 512:(n + 1) * 512],
                                          start=(h == 0), stop=(h == HALF - 1))
            mm.then_inc(mod_ps, 1)
            pe.wait_ge(qk_ev, 2 * CHUNKS)
            mod_columns(((2, 3), (3, 4)))


def attend_block(nc, sem, bank, ctx, a, v_all):
    def sb(name, shape, dt=F32):
        return ctx.enter_context(nc.sbuf_tensor(name, shape, dt))

    QRING = 4
    k_aug = sb("k_aug", [P, JH, S], BF16)
    q_aug = sb("q_aug", [P, QRING, JH, CW], BF16)
    v_cur = sb("v_cur", [P, S // P, JH, VW])
    prob = sb("prob", [P, 2, JH, CW])
    o_sb = sb("o_sb", [P, 2, CW])
    mask = sb("mask_sb", [P, CW])
    id_b = sb("id_b", [P, P], BF16)
    later_k = sb("later_k", [P, P], BF16)
    mx = sb("mx", [P, QRING, TILES, JH, CHUNKS])
    nm = sb("nm", [P, QRING, TILES * JH])
    nm_r = sb("nm_r", [P, QRING, TILES * JH])
    nm_p = sb("nm_p", [P, QRING, TILES * JH, PARTS], BF16)
    l_inv = sb("l_inv", [P, 2, TILES, JH, 1])

    score = [bank(n) for n in range(SBANKS)]
    pv = bank(3)
    side = [bank(4, 2), bank(6, 2)]
    PV_ROWS = 32

    passed_dve, passed_pool, passed_sp = sem("a_passed_dve"), sem("a_passed_pool"), sem("a_passed_sp")
    consts_in, id_cast, pv_zero = sem("consts_in"), sem("id_cast"), sem("pv_zero")
    k_in = [sem(f"k_in{r}") for r in range(CHUNKS)]
    v_in = [sem(f"v_in{r}") for r in range(CHUNKS)]
    q_in = [sem(f"q_in{r}") for r in range(QRING)]
    st_done = sem("scores_done")
    exp_done = [sem(f"exp_done{b}") for b in range(SBANKS)]
    pv_done = [sem(f"pv_done{b}") for b in range(2)]
    out_ev = sem("out_ev")
    side_done = sem("side_done")
    side_free = [sem("side_free0"), sem("side_free1")]
    m_rows = sb("m_rows", [P, 2, CW], BF16)
    rows_done = [sem("rows_done0"), sem("rows_done1")]
    nm_done, cut_done = sem("nm_done"), sem("cut_done")
    max_done, linv_done = sem("max_done"), sem("linv_done")

    def exp_count(g, u):
        return g * (UNITS // SBANKS) + u // SBANKS + 1

    def slot_of(n, head):
        return n % 2 if head else (HEAD_N + 1 + n) % 2

    def uses_before(n, head, g):
        if head:
            return n // 2
        before = len([m for m in range(HEAD_N) if m % 2 == slot_of(n, False)])
        return g * (SIDE_N // 2) + before + n // 2

    def ready_count(n, head, g):
        return n + 1 if head else g * SIDE_N + HEAD_N + n + 1

    def maxima_before(n, head, g):
        units = HEAD_UNITS[:n] if head else SIDE_FLAT[:n]
        k = len([u for u in units if u[0] in ("full", "diag")])
        k2 = len([u for u in SIDE_FLAT if u[0] in ("full", "diag")])
        kh = len([u for u in HEAD_UNITS if u[0] in ("full", "diag")])
        return k if head else g * k2 + kh + k

    def items(c, g, head):
        if head:
            return c
        return g * CHUNKS + c if c >= AHEAD else g * CHUNKS + CHUNKS + c

    def pairs(c, g, head):
        if head:
            return c // 2
        return g * (CHUNKS // 2) + (c // 2 if c >= AHEAD else CHUNKS // 2 + c // 2)

    def steps_before(g, c, kb):
        return g * NSTEPS + first_step(c) + kb

    with nc.Block() as block:
        @block.sync
        def _(sp):
            def load_parts(to, heads, runs, g, c, done):
                rows = a["parts"][:, :, :, heads, bass.ds(g, 1), c * CW:(c + 1) * CW]\
                    .rearrange("n e d j o s -> (n e d) (j o) s")
                for block, part, blocks in runs:
                    sp.dma_start(to[block * HD:(block + blocks) * HD], rows[part * HD:(part + blocks) * HD])\
                        .then_inc(done, 16)

            def load_keys(g, r):
                load_parts(k_aug[:, :, r * CW:(r + 1) * CW], slice(JH, 2 * JH), K_RUNS, g, r, k_in[r])

            def load_values(g, r):
                sp.dma_start(v_cur[:, r * TILES:(r + 1) * TILES, :, :],
                             v_all[:, bass.ds(g, 1), r * TILES:(r + 1) * TILES, :, :]
                             .rearrange("p o k j v -> p (o k) j v")).then_inc(v_in[r], 16)

            def load_queries(g, c):
                load_parts(q_aug[:, c % QRING, :, :], slice(0, JH), Q_RUNS, g, c, q_in[c % QRING])

            sp.dma_start(mask[:, :], a["mask"]).then_inc(consts_in, 16)
            sp.dma_start(later_k[:, :], a["later"]).then_inc(consts_in, 16)
            sp.dma_start(k_aug[KROWS:KROWS + MROWS, :, :], a["lastones"]).then_inc(consts_in, 16)
            for r in range(AHEAD):
                load_keys(0, r)
                load_queries(0, r)
            load_values(0, 0)
            for r in range(AHEAD, CHUNKS):
                load_keys(0, r)
            for r in range(1, CHUNKS):
                load_values(0, r)
            with sp.Fori(0, QUADS) as g:
                for c in range(AHEAD, CHUNKS):
                    if c > AHEAD:
                        sp.wait_ge(st_done, FREE + g * UNITS + JH * first_step(c - QRING + 1))
                    else:
                        sp.wait_ge(st_done, FREE + g * UNITS)
                    alone(sp, passed_sp)
                    load_queries(g, c)
                for c in range(AHEAD):
                    sp.wait_ge(st_done, FREE + g * UNITS + JH * first_step(c + QRING + 1))
                    alone(sp, passed_sp)
                    load_queries((g + 1) % QUADS, c)
                for r in range(CHUNKS):
                    last = first_step(CHUNKS - 1) + r * TILES + TILES - 1
                    sp.wait_ge(st_done, FREE + g * UNITS + JH * (last + 1))
                    alone(sp, passed_sp)
                    load_keys((g + 1) % QUADS, r)
                    sp.wait_ge(pv_done[last % 2], FREE + g * (NSTEPS // 2) + last // 2 + 1)
                    alone(sp, passed_sp)
                    load_values((g + 1) % QUADS, r)
            for r in range(CHUNKS):
                sp.wait_ge(k_in[r], 16 * len(K_RUNS) * (QUADS + 1))
                sp.wait_ge(v_in[r], 16 * (QUADS + 1))

        @block.tensor
        def _(pe):
            begin(pe, st_done, *pv_done)
            def key_loads(g, r):
                pe.wait_ge(k_in[r], (g + 1) * (16 * len(K_RUNS)))

            def side_unit(g, n, head):
                kind, c, t, kc, pair = HEAD_UNITS[n] if head else SIDE_FLAT[n]
                slot = side[slot_of(n, head)]
                pe.wait_ge(side_free[slot_of(n, head)], FREE + uses_before(n, head, g))
                if kind in ("full", "diag"):
                    width = CW if kind == "full" else (t + 1) * P
                    for jj in range(2):
                        j = 2 * pair + jj
                        mm = nc.tensor.matmul(slot[:, jj * CW:jj * CW + width],
                                              q_aug[0:KROWS, c % QRING, j, t * P:(t + 1) * P],
                                              k_aug[0:KROWS, j, kc * CW:kc * CW + width], start=True, stop=True)
                elif kind == "turn":
                    pe.wait_ge(cut_done, (items(c, g, head) + 1) * 4)
                    for t in range(TILES):
                        mm = nc.tensor.transpose(
                            slot.bitcast(BF16)[KROWS:KROWS + MROWS, t * P:(t + 1) * P],
                            nm_p[:, c % QRING, t * JH:(t + 1) * JH, :].rearrange("p j n -> p (j n)"), id_b[:, :])
                else:
                    pe.wait_ge(out_ev, FREE + g * CHUNKS + c + 1)
                    for t in range(TILES):
                        mm = nc.tensor.transpose(slot[:, t * P:(t + 1) * P], o_sb[:, c % 2, t * P:(t + 1) * P],
                                                 a["id_f"][:, :])
                mm.then_inc(side_done, 1)

            def queries_loaded(g, c, head=False):
                uses = g * (CHUNKS // QRING) + c // QRING
                pe.wait_ge(q_in[c % QRING], (uses + 1) * (16 * len(Q_RUNS)))

            def values(g, s):
                c, kb = STEPS[s]
                t = kb - TILES * c
                q0 = max(t, 0) * P
                if kb == 0:
                    pe.wait_ge(out_ev, FREE + g * CHUNKS + c)
                u = JH * s + JH - 1
                pe.wait_ge(exp_done[u % SBANKS], FREE + exp_count(g, u))
                if t >= 0:
                    pe.wait_ge(v_in[c], (g + 1) * 16)
                for j in range(JH):
                    mm = nc.tensor.matmul(pv[32 * j:32 * j + VW, q0:CW], v_cur[:, kb, j, :],
                                          prob[:, s % 2, j, q0:CW], start=(kb == 0),
                                          stop=(kb == TILES * (c + 1) - 1), skip_group_check=True)
                mm.then_inc(pv_done[s % 2], 1)

            pe.wait_ge(consts_in, 48)
            pe.wait_ge(id_cast, 1)
            pe.wait_ge(pv_zero, 1)
            for n, unit in enumerate(HEAD_UNITS):
                if unit[0] != "turn":
                    key_loads(0, unit[3])
                    queries_loaded(0, unit[1])
                side_unit(0, n, True)
            with pe.Fori(0, QUADS) as g:
                n = 0
                for s, (c, kb) in enumerate(STEPS):
                    t = kb - TILES * c
                    q0 = max(t, 0) * P
                    if kb == 0:
                        pe.wait_ge(rows_done[c % 2], FREE + (g * (CHUNKS // 2) + c // 2 + 1) * 16)
                    if t == 0:
                        key_loads(g, c)
                    for j in range(JH):
                        u = JH * s + j
                        pe.wait_ge(exp_done[u % SBANKS], FREE + g * (UNITS // SBANKS) + u // SBANKS)
                        mm = nc.tensor.matmul(score[u % SBANKS][:, q0:CW],
                                              k_aug[0:KROWS + MROWS, j, kb * P:(kb + 1) * P],
                                              q_aug[0:KROWS + MROWS, c % QRING, j, q0:CW], start=True, stop=True)
                        if t >= 0:
                            mm = nc.tensor.matmul(score[u % SBANKS][:, q0:q0 + P], id_b[:, :], later_k[:, :],
                                                  start=False, stop=True, skip_group_check=True)
                        mm.then_inc(st_done, 1)
                        for unit in SIDE[s][j]:
                            if unit[0] in ("full", "diag"):
                                nxt = 1 if unit[1] < AHEAD else 0
                                if unit[0] == "diag" and unit[2] == 0 and unit[4] == 0 or unit[3] == 0:
                                    queries_loaded(g + nxt, unit[1])
                                key_loads(g + nxt, unit[3])
                            side_unit(g, n, False)
                            n += 1
                    if s:
                        values(g, s - 1)
                values(g, NSTEPS - 1)
                for _ in SIDE[NSTEPS][0]:
                    side_unit(g, n, False)
                    n += 1

        @block.scalar
        def _(act):
            begin(act, out_ev, *exp_done, *rows_done)
            nc.scalar.activation(id_b[:, :], a["id_f"][:, :], ACT.Copy).then_inc(id_cast, 1)

            def turn(g, n, head):
                c = (HEAD_UNITS if head else SIDE_FLAT)[n][1]
                act.wait_ge(side_done, ready_count(n, head, g))
                slot = side[slot_of(n, head)]
                act.wait_ge(rows_done[c % 2], FREE + pairs(c, g, head) * 16)
                nc.scalar.activation(m_rows[KROWS:KROWS + MROWS, c % 2, :],
                                     slot.bitcast(BF16)[KROWS:KROWS + MROWS, 0:CW], ACT.Copy)\
                    .then_inc(side_free[slot_of(n, head)], 1)

            def spread(g, n, head):
                c = (HEAD_UNITS if head else SIDE_FLAT)[n][1]
                act.wait_ge(side_free[slot_of(n, head)], FREE + uses_before(n, head, g) + 1)
                act.dma_start(q_aug[KROWS:KROWS + MROWS, c % QRING, :, :],
                              m_rows[KROWS:KROWS + MROWS, c % 2, :].unsqueeze(1).broadcast_to([MROWS, JH, CW]))\
                    .then_inc(rows_done[c % 2], 16)

            def take_out(g, c):
                last = first_step(c + 1) - 1
                act.wait_ge(pv_done[last % 2], FREE + g * (NSTEPS // 2) + last // 2 + 1)
                act.wait_ge(linv_done, FREE + g * CHUNKS + c)
                nc.scalar.activation(o_sb[:, c % 2, :], pv, ACT.Copy).then_inc(out_ev, 1)

            for n, unit in enumerate(HEAD_UNITS):
                if unit[0] == "turn":
                    turn(0, n, True)
                    spread(0, n, True)
            act.wait_ge(pv_zero, 1)
            with act.Fori(0, QUADS) as g:
                n, turned = 0, None
                for s, (c, kb) in enumerate(STEPS):
                    t = kb - TILES * c
                    q0 = max(t, 0) * P
                    for j in range(JH):
                        u = JH * s + j
                        act.wait_ge(st_done, FREE + g * UNITS + u + 1)
                        if j == 0:
                            act.wait_ge(pv_done[s % 2], FREE + g * (NSTEPS // 2) + s // 2)
                        nc.scalar.activation(prob[:, s % 2, j, q0:CW], score[u % SBANKS][:, q0:CW], ACT.Exp,
                                             scale=float(HD) ** -0.5).then_inc(exp_done[u % SBANKS], 1)
                        if c and kb == 1 and j == 1:
                            take_out(g, c - 1)
                        if turned is not None and j == 1:
                            spread(g, turned, False)
                            turned = None
                    for us in SIDE[s]:
                        for unit in us:
                            if unit[0] == "turn":
                                turn(g, n, False)
                                turned = n
                            n += 1
                take_out(g, CHUNKS - 1)
                for unit in SIDE[NSTEPS][0]:
                    if unit[0] == "turn":
                        turn(g, n, False)
                        turned = n
                    n += 1
                if turned is not None:
                    spread(g, turned, False)
            for par in range(2):
                act.wait_ge(rows_done[par], FREE + 16 * (QUADS * (CHUNKS // 2) + len(range(par, AHEAD, 2))))

        @block.vector
        def _(dve):
            begin(dve, linv_done, *side_free)
            nc.vector.memset(pv, 0.0).then_inc(pv_zero, 1)
            dve.wait_ge(consts_in, 48)

            def side_unit(g, n, head):
                kind, c, t, kc, pair = HEAD_UNITS[n] if head else SIDE_FLAT[n]
                if kind == "turn":
                    return
                dve.wait_ge(side_done, ready_count(n, head, g))
                if kind == "diag":
                    alone(dve, passed_dve)
                slot = side[slot_of(n, head)]
                free = side_free[slot_of(n, head)]
                if kind == "full":
                    nc.vector.tensor_reduce(mx[:, c % QRING, t, 2 * pair:2 * pair + 2, kc],
                                            slot.rearrange("p (j s) -> p j s", j=2), AX_X, ALU.max).then_inc(free, 1)
                elif kind == "diag":
                    width = (t + 1) * P
                    for jj in range(2):
                        ins = nc.vector.tensor_tensor_reduce(
                            slot[:, jj * CW:jj * CW + width], slot[:, jj * CW:jj * CW + width], mask[:, CW - width:CW],
                            1.0, NEG, ALU.add, ALU.max, mx[:, c % QRING, t, 2 * pair + jj, kc:kc + 1])
                        ins.then_inc(max_done if jj == 0 else free, 1)
                    if t == TILES - 1 and pair == 1:
                        dve.wait_ge(free, FREE + uses_before(n, head, g) + 1)
                        before = uses_before(n - 1, head, g) + 1
                        dve.wait_ge(side_free[slot_of(n - 1, head)], FREE + before)
                        nc.vector.tensor_reduce(nm[:, c % QRING, :],
                                                mx[:, c % QRING, :, :, 0:c + 1].rearrange("p t j k -> p (t j) k"),
                                                AX_X, ALU.max, negate=True).then_inc(nm_done, 1)
                else:
                    blocks = slot[:, 0:CW].rearrange("p (t j v) -> p t j v", t=TILES, j=JH)
                    nc.vector.reciprocal(l_inv[:, c % 2, :, :, :], blocks[:, :, :, HD:HD + 1]).then_inc(linv_done, 1)
                    dve.wait_ge(linv_done, FREE + g * CHUNKS + c + 1)
                    nc.vector.tensor_tensor(
                        a["att_o"][:, c * TILES:(c + 1) * TILES, bass.ds(g * (JH * HD), JH * HD)]
                        .rearrange("p t (j d) -> p t j d", j=JH),
                        blocks[:, :, :, 0:HD], l_inv[:, c % 2, :, :, :].broadcast_to([P, TILES, JH, HD]),
                        ALU.mult).then_inc(free, 1)

            for n in range(HEAD_N):
                side_unit(0, n, True)
            with dve.Fori(0, QUADS) as g:
                for n in range(SIDE_N):
                    side_unit(g, n, False)

        @block.gpsimd
        def _(pool):
            def cut(g, c, head):
                r = c % QRING
                k = items(c, g, head)
                pool.wait_ge(nm_done, k + 1)
                alone(pool, passed_pool)
                nc.gpsimd.tensor_copy(nm_p[:, r, :, 0], nm[:, r, :]).then_inc(cut_done, 1)
                pool.wait_ge(cut_done, 4 * k + 1)
                nc.gpsimd.tensor_tensor(nm_r[:, r, :], nm[:, r, :], nm_p[:, r, :, 0], ALU.subtract)\
                    .then_inc(cut_done, 1)
                pool.wait_ge(cut_done, 4 * k + 2)
                alone(pool, passed_pool)
                nc.gpsimd.tensor_copy(nm_p[:, r, :, 1], nm_r[:, r, :]).then_inc(cut_done, 1)
                pool.wait_ge(cut_done, 4 * k + 3)
                nc.gpsimd.tensor_tensor(nm_p[:, r, :, 2], nm_r[:, r, :], nm_p[:, r, :, 1], ALU.subtract)\
                    .then_inc(cut_done, 1)

            def after_unit(g, n, head):
                kind, c, t, kc, pair = (HEAD_UNITS if head else SIDE_FLAT)[n]
                if kind == "diag" and t == TILES - 1 and pair == 1:
                    cut(g, c, head)

            for n in range(HEAD_N):
                after_unit(0, n, True)
            with pool.Fori(0, QUADS) as g:
                for n in range(SIDE_N):
                    after_unit(g, n, False)


def feed(nc, sem, bank, a):
    with ExitStack() as ctx:
        x1 = ctx.enter_context(nc.sbuf_tensor("x1", [P, S // P, D], F32))
        xaT = ctx.enter_context(nc.sbuf_tensor("xaT", [P, HALF, S], F32))
        with ExitStack() as mine:
            mix_block(nc, sem, bank, mine, a, x1, xaT)
        with ExitStack() as mine:
            expert_block(nc, sem, bank, mine, a, x1, xaT)


def mix_block(nc, sem, bank, ctx, a, x1, xaT):
    def sb(name, shape, dt=F32):
        return ctx.enter_context(nc.sbuf_tensor(name, shape, dt))

    w_a = sb("w_a", [P, HALF, D])
    ab_col = sb("ab_col", [P, HALF])
    ln_col = sb("ln_col", [P, 2 * HALF])
    half_neg = sb("half_neg2", [P, TILES])
    xs = sb("xs2", [P, 2, TILES, D])
    oc = sb("oc", [P, 2, TILES, D])
    oT = sb("oT", [P, 2, HALF, CW])
    stats = sb("stats2", [P, 2, TILES, 6])
    mv = sb("mv2", [P, 2, TILES, 2])
    var_e = sb("var_e2", [P, 2, TILES])
    rstd = sb("rstd2", [P, 2, TILES])
    xn = sb("xn2", [P, 2, TILES, D])
    h2 = sb("h2", [P, 2, TILES, D])
    h2T = sb("h2T", [P, 2, HALF, CW])
    x3T = sb("x3T", [P, 2, HALF, CW])

    passed_dve, passed_pool, passed_sp = sem("m_passed_dve"), sem("m_passed_pool"), sem("m_passed_sp")
    w_in, x_in, o_in = sem("m_w_in"), [sem("m_x_in0"), sem("m_x_in1")], [sem("m_o_in0"), sem("m_o_in1")]
    half_set = sem("m_half_set")
    oT_ps, oT_ev, wo_ps, x1_done = sem("oT_ps"), sem("oT_ev"), sem("wo_ps"), sem("x1_done")
    st_done, mv_done, var_done, rstd_done, xn_done = (sem("m_st_done"), sem("m_mv_done"), sem("m_var_done"),
                                                      sem("m_rstd_done"), sem("m_xn_done"))
    scaled, h2_done = sem("m_scaled"), sem("h2_done")
    h2_ps, x3_ps, h2T_ev, x3T_ev, at_ps, xa_done = (sem("h2_ps"), sem("x3_ps"), sem("h2T_ev"), sem("x3T_ev"),
                                                    sem("at_ps"), sem("xa_done"))

    with nc.Block() as block:
        @block.sync
        def _(sp):
            sp.dma_start(w_a[:, :, :], a["attnT"].rearrange("(h p) n -> p h n", p=P)).then_inc(w_in, 16)
            sp.dma_start(ab_col[:, :], a["attnb"]).then_inc(w_in, 16)
            sp.dma_start(ln_col[:, :], a["lnsb"]).then_inc(w_in, 16)
            with sp.Fori(0, CHUNKS // 2) as i:
                for par in range(2):
                    sp.wait_ge(oT_ps, FREE + i * 4)
                    alone(sp, passed_sp)
                    sp.dma_start(oc[:, par, :, :], a["att_o"][:, bass.ds((i * 2 + par) * TILES, TILES), :])\
                        .then_inc(o_in[par], 16)
                    sp.wait_ge(x1_done, FREE + i * 4)
                    alone(sp, passed_sp)
                    sp.dma_start(xs[:, par, :, :],
                                 a["x"][0, bass.ds((i * 2 + par) * CW, CW), :].rearrange("(t p) d -> p t d", p=P))\
                        .then_inc(x_in[par], 16)
            for par in range(2):
                sp.wait_ge(o_in[par], 16 * CHUNKS // 2)
                sp.wait_ge(x_in[par], 16 * CHUNKS // 2)

        @block.tensor
        def _(pe):
            begin(pe, oT_ps, wo_ps, at_ps, x3_ps, h2_ps)
            pe.wait_ge(w_in, 48)
            with pe.Fori(0, CHUNKS // 2) as i:
                for par in range(2):
                    pe.wait_ge(o_in[par], i * 16 + 16)
                    pe.wait_ge(xa_done, FREE + i * 4)
                    for h in range(HALF):
                        for t in range(TILES):
                            mm = nc.tensor.transpose(bank(2 * par + h)[:, t * P:(t + 1) * P],
                                                     oc[:, par, t, h * P:(h + 1) * P], a["id_f"][:, :])
                        mm.then_inc(oT_ps, 1)
                for par in range(2):
                    pe.wait_ge(oT_ev, i * 4 + par * 2 + 2)
                    pe.wait_ge(x3T_ev, FREE + i * 4)
                    for t in range(TILES):
                        for h in range(HALF):
                            mm = nc.tensor.matmul(bank(4 + 2 * par + t // 2)[:, (t % 2) * D:(t % 2 + 1) * D],
                                                  oT[:, par, h, t * P:(t + 1) * P], a["wo_g"][:, h, :],
                                                  start=(h == 0), stop=(h == HALF - 1))
                        if t % 2:
                            mm.then_inc(wo_ps, 1)
                for par in range(2):
                    pe.wait_ge(h2_done, i * 2 + par + 1)
                    for h in range(HALF):
                        for t in range(TILES):
                            mm = nc.tensor.transpose(bank(2 * par + h)[:, t * P:(t + 1) * P],
                                                     h2[:, par, t, h * P:(h + 1) * P], a["id_f"][:, :])
                        mm.then_inc(h2_ps, 1)
                for par in range(2):
                    pe.wait_ge(xn_done, i * (4 * TILES) + (3 + par) * TILES)
                    for h in range(HALF):
                        for t in range(TILES):
                            mm = nc.tensor.transpose(bank(4 + 2 * par + h)[:, t * P:(t + 1) * P],
                                                     xn[:, par, t, h * P:(h + 1) * P], a["id_f"][:, :])
                        mm.then_inc(x3_ps, 1)
                for par in range(2):
                    pe.wait_ge(x3T_ev, FREE + i * 4 + par * 2 + 2)
                    pe.wait_ge(h2T_ev, i * 4 + par * 2 + 2)
                    for m in range(HALF):
                        for h in range(HALF):
                            mm = nc.tensor.matmul(bank(2 * par + m), w_a[:, h, m * P:(m + 1) * P],
                                                  x3T[:, par, h, :], start=(h == 0), stop=(h == HALF - 1))
                        mm.then_inc(at_ps, 1)

        @block.scalar
        def _(act):
            begin(act, x3T_ev)
            act.wait_ge(w_in, 48)
            with act.Fori(0, CHUNKS // 2) as i:
                for par in range(2):
                    act.wait_ge(oT_ps, FREE + i * 4 + par * 2 + 2)
                    act.wait_ge(wo_ps, FREE + i * 4)
                    for h in range(HALF):
                        nc.scalar.activation(oT[:, par, h, :], bank(2 * par + h), ACT.Copy).then_inc(oT_ev, 1)
                for par in range(2):
                    act.wait_ge(h2_ps, FREE + i * 4 + par * 2 + 2)
                    act.wait_ge(xa_done, FREE + i * 4)
                    for h in range(HALF):
                        nc.scalar.activation(h2T[:, par, h, :], bank(2 * par + h), ACT.Copy).then_inc(h2T_ev, 1)
                for par in range(2):
                    act.wait_ge(x3_ps, FREE + i * 4 + par * 2 + 2)
                    act.wait_ge(at_ps, FREE + i * 4)
                    for h in range(HALF):
                        nc.scalar.activation(x3T[:, par, h, :], bank(4 + 2 * par + h), ACT.Identity,
                                             bias=ln_col[:, HALF + h:HALF + h + 1], scale=ln_col[:, h:h + 1])\
                            .then_inc(x3T_ev, 1)

        @block.vector
        def _(dve):
            begin(dve, x1_done, xa_done)
            dve.wait_ge(w_in, 48)
            with dve.Fori(0, CHUNKS // 2) as i:
                def tile_stats(par, src, k):
                    base = i * (4 * TILES) + k * (2 * TILES) + par * TILES
                    for t in range(TILES):
                        nc.vector.bn_stats(stats[:, par, t, :], src(t)).then_inc(st_done, 1)
                    for t in range(TILES):
                        dve.wait_ge(st_done, base + t + 1)
                        alone(dve, passed_dve)
                        nc.vector.bn_aggr(mv[:, par, t, :], stats[:, par, t, :]).then_inc(mv_done, 1)

                for par in range(2):
                    dve.wait_ge(x_in[par], i * 16 + 16)
                    for b in range(2):
                        dve.wait_ge(wo_ps, FREE + i * 4 + par * 2 + b + 1)
                        nc.vector.tensor_tensor(
                            x1[:, bass.ds((i * 2 + par) * TILES + 2 * b, 2), :],
                            bank(4 + 2 * par + b).rearrange("p (t d) -> p t d", t=2),
                            xs[:, par, 2 * b:2 * b + 2, :], ALU.add).then_inc(x1_done, 1)
                    dve.wait_ge(x1_done, FREE + i * 4 + par * 2 + 2)
                    alone(dve, passed_dve)
                    tile_stats(par, lambda t, par=par: x1[:, bass.ds((i * 2 + par) * TILES + t, 1), :]
                               .rearrange("p o d -> p (o d)"), 0)
                for par in range(2):
                    dve.wait_ge(rstd_done, i * 4 + par + 1)
                    dve.wait_ge(x3_ps, FREE + i * 4)
                    for t in range(TILES):
                        nc.vector.tensor_scalar(
                            xn[:, par, t, :],
                            x1[:, bass.ds((i * 2 + par) * TILES + t, 1), :].rearrange("p o d -> p (o d)"),
                            mv[:, par, t, 0:1], rstd[:, par, t:t + 1], ALU.subtract, ALU.mult).then_inc(xn_done, 1)
                for par in range(2):
                    dve.wait_ge(h2_done, i * 2 + par + 1)
                    dve.wait_ge(xn_done, i * (4 * TILES) + (par + 1) * TILES)
                    tile_stats(par, lambda t, par=par: h2[:, par, t, :], 1)
                for par in range(2):
                    dve.wait_ge(rstd_done, i * 4 + 2 + par + 1)
                    for t in range(TILES):
                        nc.vector.tensor_scalar(xn[:, par, t, :], h2[:, par, t, :], mv[:, par, t, 0:1],
                                                rstd[:, par, t:t + 1], ALU.subtract, ALU.mult).then_inc(xn_done, 1)
                for par in range(2):
                    dve.wait_ge(h2T_ev, i * 4 + par * 2 + 2)
                    for m in range(HALF):
                        dve.wait_ge(at_ps, FREE + i * 4 + par * 2 + m + 1)
                        nc.vector.scalar_tensor_tensor(
                            out=xaT[:, m, bass.ds((i * 2 + par) * CW, CW)], in0=bank(2 * par + m),
                            scalar=ab_col[:, m:m + 1], in1=h2T[:, par, m, :], op0=ALU.add, op1=ALU.add)\
                            .then_inc(xa_done, 1)

        @block.gpsimd
        def _(pool):
            nc.gpsimd.memset(half_neg[:, :], -0.5).then_inc(half_set, 1)
            pool.wait_ge(half_set, 1)
            with pool.Fori(0, CHUNKS // 2) as i:
                def inverse_std(par, k):
                    n = i * 4 + 2 * k + par
                    pool.wait_ge(mv_done, (n + 1) * TILES)
                    alone(pool, passed_pool)
                    nc.gpsimd.tensor_scalar(var_e[:, par, :], mv[:, par, :, 1], EPS, None, ALU.add)\
                        .then_inc(var_done, 1)
                    pool.wait_ge(var_done, n + 1)
                    nc.gpsimd.tensor_tensor(rstd[:, par, :], var_e[:, par, :], half_neg[:, :], ALU.pow)\
                        .then_inc(rstd_done, 1)

                for par in range(2):
                    inverse_std(par, 0)
                for par in range(2):
                    pool.wait_ge(xn_done, i * (4 * TILES) + (par + 1) * TILES)
                    pool.wait_ge(h2_ps, FREE + i * 4)
                    nc.gpsimd.tensor_tensor(
                        h2[:, par, :, :], xn[:, par, :, :],
                        a["mod_bc"][:, 4 * D:5 * D].unsqueeze(1).broadcast_to([P, TILES, D]), ALU.mult).then_inc(scaled, 1)
                    pool.wait_ge(scaled, i * 2 + par + 1)
                    nc.gpsimd.tensor_tensor(
                        h2[:, par, :, :], h2[:, par, :, :],
                        a["mod_bc"][:, 3 * D:4 * D].unsqueeze(1).broadcast_to([P, TILES, D]), ALU.add).then_inc(h2_done, 1)
                for par in range(2):
                    inverse_std(par, 1)


def expert_block(nc, sem, bank, ctx, a, x1, xaT):
    def sb(name, shape, dt=F32):
        return ctx.enter_context(nc.sbuf_tensor(name, shape, dt))

    w1_s = sb("w1_s", [P, 2, HALF, HID])
    w2_s = sb("w2_s", [P, 2, HK, D])
    b1_s = sb("b1_s", [P, 2, HK])
    b2_s = sb("b2_s", [P, 2, HALF])
    w_n = sb("w_n", [P, HALF, D])
    nb_bc = sb("nb_bc", [P, D])
    hid = sb("hid", [P, HK, CW])
    eoT = sb("eoT", [P, HALF, CW])
    y = sb("y", [P, 2, 2, D])
    yg = sb("yg", [P, 2, 2, D])

    w_in, passed_sp = sem("e_w_in"), sem("e_passed_sp")
    w1_in, w2_in = [sem("w1_in0"), sem("w1_in1")], [sem("w2_in0"), sem("w2_in1")]
    h_ps, h_act, e_ps, e_ev, n_ps, y_pre, y_act, y_gate, y_done = (
        sem("h_ps"), sem("h_act"), sem("e_ps"), sem("e_ev"), sem("n_ps"), sem("y_pre"), sem("y_act"),
        sem("y_gate"), sem("y_done"))
    y_out = [sem("y_out0"), sem("y_out1")]
    HB = 4

    with nc.Block() as block:
        @block.sync
        def _(sp):
            begin(sp, *y_out)
            sp.dma_start(w_n[:, :, :], a["nextT"].rearrange("(h p) n -> p h n", p=P)).then_inc(w_in, 16)
            sp.dma_start(nb_bc[:, :], a["nextb"].rearrange("(a n) -> a n", a=1).broadcast_to([P, D])).then_inc(w_in, 16)
            def load(e, par):
                sp.dma_start(w1_s[:, par, :, :],
                             a["w1"][bass.ds(e, 1), :, :].rearrange("o (h p) n -> p (o h) n", p=P)).then_inc(w1_in[par], 16)
                sp.dma_start(b1_s[:, par, :], a["b1"][bass.ds(e, 1), :, :].rearrange("o p k -> p (o k)"))\
                    .then_inc(w1_in[par], 16)
                sp.dma_start(w2_s[:, par, :, :],
                             a["w2"][bass.ds(e, 1), :, :].rearrange("o (k p) n -> p (o k) n", p=P)).then_inc(w2_in[par], 16)
                sp.dma_start(b2_s[:, par, :], a["b2"][bass.ds(e, 1), :, :].rearrange("o p k -> p (o k)"))\
                    .then_inc(w2_in[par], 16)

            def store(e):
                for b in range(2):
                    sp.wait_ge(y_done, FREE + e * 2 + b + 1)
                    alone(sp, passed_sp)
                    sp.dma_start(a["out"][0, bass.ds(e * 256 + b * 2048, 256), :].rearrange("(t p) d -> p t d", p=P),
                                 y[:, b, :, :]).then_inc(y_out[b], 16)

            for par in range(2):
                load(par, par)
            with sp.Fori(0, EXPERTS // 2 - 1) as i:
                for par in range(2):
                    store(i * 2 + par)
                    load(i * 2 + par + 2, par)
            for par in range(2):
                store(EXPERTS - 2 + par)
            for b in range(2):
                sp.wait_ge(y_out[b], FREE + 16 * EXPERTS)

        @block.tensor
        def _(pe):
            begin(pe, n_ps, e_ps)
            pe.wait_ge(w_in, 32)
            with pe.Fori(0, EXPERTS // 2) as i:
                for par in range(2):
                    e = i * 2 + par
                    pe.wait_ge(w1_in[par], i * 32 + 32)
                    for k in range(HK):
                        pe.wait_ge(h_act, FREE + e * HK + (k - HB + 1 if k >= HB else 0))
                        for h in range(HALF):
                            rhs = xaT[:, h, :].rearrange("p (m s) -> p m s", m=2)[:, :, bass.ds(e * 256, 256)]
                            mm = nc.tensor.matmul(bank(k % HB), w1_s[:, par, h, k * P:(k + 1) * P], rhs,
                                                  start=(h == 0), stop=(h == HALF - 1))
                        mm.then_inc(h_ps, 1)
                    pe.wait_ge(w2_in[par], i * 32 + 32)
                    pe.wait_ge(e_ev, FREE + e * HALF)
                    for m in range(HALF):
                        for k in range(HK):
                            if m == 0:
                                pe.wait_ge(h_act, FREE + e * HK + k + 1)
                            mm = nc.tensor.matmul(bank(4 + m), w2_s[:, par, k, m * P:(m + 1) * P], hid[:, k, :],
                                                  start=(k == 0), stop=(k == HK - 1))
                        mm.then_inc(e_ps, 1)
                    pe.wait_ge(e_ev, FREE + e * HALF + HALF)
                    for b in range(2):
                        pe.wait_ge(y_pre, FREE + e * 2 + b if b == 0 else e * 2)
                        for t in range(2):
                            for h in range(HALF):
                                tok = (2 * b + t) * P
                                mm = nc.tensor.matmul(bank(6 + b)[:, t * D:(t + 1) * D], eoT[:, h, tok:tok + P],
                                                      w_n[:, h, :], start=(h == 0), stop=(h == HALF - 1))
                        mm.then_inc(n_ps, 1)

        @block.scalar
        def _(act):
            begin(act, h_act)
            with act.Fori(0, EXPERTS // 2) as i:
                for par in range(2):
                    e = i * 2 + par
                    act.wait_ge(w1_in[par], i * 32 + 32)
                    act.wait_ge(e_ps, FREE + e * HALF)
                    for k in range(HK):
                        act.wait_ge(h_ps, e * HK + k + 1)
                        nc.scalar.activation(hid[:, k, :], bank(k % HB), ACT.Gelu, bias=b1_s[:, par, k:k + 1])\
                            .then_inc(h_act, 1)
                    for b in range(2):
                        act.wait_ge(y_pre, FREE + e * 2 + b + 1)
                        act.wait_ge(y_done, FREE + e * 2)
                        nc.scalar.activation(yg[:, b, :, :], y[:, b, :, :], ACT.Gelu).then_inc(y_act, 1)

        @block.vector
        def _(dve):
            begin(dve, e_ev, y_pre, y_done)
            dve.wait_ge(w_in, 32)
            with dve.Fori(0, EXPERTS // 2) as i:
                for par in range(2):
                    e = i * 2 + par
                    dve.wait_ge(w2_in[par], i * 32 + 32)
                    dve.wait_ge(n_ps, FREE + e * 2)
                    for m in range(HALF):
                        dve.wait_ge(e_ps, FREE + e * HALF + m + 1)
                        nc.vector.tensor_scalar(eoT[:, m, :], bank(4 + m), b2_s[:, par, m:m + 1], None, ALU.add)\
                            .then_inc(e_ev, 1)
                    for b in range(2):
                        dve.wait_ge(n_ps, FREE + e * 2 + b + 1)
                        dve.wait_ge(y_out[b], FREE + e * 16)
                        nc.vector.tensor_tensor(y[:, b, :, :], bank(6 + b).rearrange("p (t d) -> p t d", t=2),
                                                nb_bc[:, :].unsqueeze(1).broadcast_to([P, 2, D]), ALU.add)\
                            .then_inc(y_pre, 1)

                    for b in range(2):
                        dve.wait_ge(y_act, e * 2 + b + 1)
                        nc.vector.tensor_tensor(yg[:, b, :, :], yg[:, b, :, :],
                                                a["mod_bc"][:, 5 * D:6 * D].unsqueeze(1).broadcast_to([P, 2, D]),
                                                ALU.mult).then_inc(y_gate, 1)
                    for b in range(2):
                        dve.wait_ge(y_gate, e * 2 + b + 1)
                        nc.vector.tensor_tensor(y[:, b, :, :], yg[:, b, :, :],
                                                x1[:, bass.ds(e * 2 + 16 * b, 2), :], ALU.add).then_inc(y_done, 1)


def rope_table():
    inv = (1.0 / np.float32(10000.0) ** (np.arange(0, HD, 2, dtype=np.float32) / np.float32(HD))).astype(np.float32)
    angle = (np.arange(S, dtype=np.float32)[None, :] * inv[:, None]).astype(np.float32).astype(np.float64)
    both = np.stack([np.cos(angle), np.sin(angle)], axis=1)
    both = np.tile(np.repeat(both, 2 * JH, axis=0), (2, 1, 1))
    return np.ascontiguousarray(both.astype(np.float32))


def constants():
    mask = np.zeros((P, CW), np.float32)
    q, k = np.arange(P)[:, None], np.arange(P)[None, :]
    mask[:, CW - P:] = np.where(k > q, np.float32(-1e38), np.float32(0))
    later = np.where(q > k, np.float32(-1e30), np.float32(0)).astype(mybir.dt.np(BF16))
    last = np.zeros((MROWS, JH, S), mybir.dt.np(BF16))
    for j in range(JH):
        last[PARTS * j:PARTS * (j + 1), j, :] = 1
    return {"rope": rope_table(), "ident": np.eye(P, dtype=np.float32), "mask": mask, "later": later, "lastones": last}


def kernel(**inputs):
    import concourse.bacc as _bacc
    from concourse.bass_utils import run_bass_kernel_spmd as _run

    a = {k: np.asarray(v) for k, v in inputs.items()}

    def rows_of_pairs(w):
        return w.T.reshape(D, 2, 2, JH, HD // 2, 2).transpose(0, 5, 2, 1, 4, 3)

    def column(v):
        return v.reshape(HALF, P).T

    arrays = {
        "x": a["L0_attn_x"],
        "wqk": np.stack([rows_of_pairs(a["L0_attn_Wq"]), rows_of_pairs(a["L0_attn_Wk"])], axis=5)
        .reshape(D, 2, 2, P),
        "wvT": a["L0_attn_Wv"].T,
        "woT": a["L0_attn_Wo"].T,
        "lnsb": np.concatenate([column(a["L0_ffn_ln_scale"]), column(a["L0_ffn_ln_bias"])], axis=1),
        "attnT": a["L0_ffn_attn_w"].T,
        "attnb": column(a["L0_ffn_attn_b"]),
        "w1": a["L0_ffn_w1"],
        "b1": a["L0_ffn_b1"].reshape(EXPERTS, HK, P).transpose(0, 2, 1),
        "w2": a["L0_ffn_w2"],
        "b2": a["L0_ffn_b2"].reshape(EXPERTS, HALF, P).transpose(0, 2, 1),
        "nextT": a["L0_ffn_next_w"].T,
        "nextb": a["L0_ffn_next_b"],
        "cvec": column(a["L0_c"]),
        "wmod": a["L0_wmod"],
        **constants(),
    }
    nc = _bacc.Bacc("TRN2", target_bir_lowering=False, num_devices=1)
    args, given = {}, {}
    for name, v in arrays.items():
        v = np.ascontiguousarray(v)
        given[f"in_{name}"] = v
        args[name] = nc.dram_tensor(f"in_{name}", v.shape, mybir.dt.from_np(v.dtype), kind="ExternalInput").ap()
    args["out"] = nc.dram_tensor("out_0", (1, S, D), F32, kind="ExternalOutput").ap()
    build(nc, **args)
    r = _run(nc, [given], core_ids=[0])
    return r.results[0]["out_0"]
```

```python
from contextlib import ExitStack

import numpy as np

import concourse.bass as bass
from concourse import mybir
from concourse.alu_op_type import AluOpType as ALU

F32 = mybir.dt.float32
BF16 = mybir.dt.bfloat16
F32R = mybir.dt.float32r
ACT = mybir.ActivationFunctionType
AX_X = mybir.AxisListType.X

P = 128
S = 4096
D = 256
HEADS = 16
HD = D // HEADS
QUADS = 4
JH = HEADS // QUADS
CW = 512
CHUNKS = S // CW
TILES = CW // P
HALF = D // P
PARTS = 3
Q_PART = (0, 1, 2, 0, 0, 1)
K_PART = (0, 1, 0, 1, 2, 0)
Q_RUNS = ((0, 0, 3), (3, 0, 1), (4, 0, 2))
K_RUNS = ((0, 0, 2), (2, 0, 3), (5, 0, 1))
KROWS = len(Q_PART) * HD
MROWS = PARTS * JH
VW = HD + 1
EXPERTS = 8
HID = 1024
HK = HID // P
K_HALVES = (slice(0, HK // 2), slice(HK // 2, HK))
NEG = -3.0e38
EPS = 1e-5
FREE = 1


def first_step(c):
    return 2 * c * (c + 1)


STEPS = [(c, kb) for c in range(CHUNKS) for kb in range(TILES * (c + 1))]
NSTEPS = len(STEPS)
SBANKS = 3
PROBS = 3
BEHIND = 2
UNITS = NSTEPS * JH


def max_units(c):
    return ([("full", c, t, kc, pair) for kc in range(c) for t in range(TILES) for pair in range(2)]
            + [("diag", c, t, c, pair) for t in range(TILES) for pair in range(2)])


def late_turns(chunks, lag):
    out, due = [], []
    for c in chunks:
        for u in max_units(c):
            out.append(u)
            for d in list(due):
                d[1] -= 1
                if d[1] == 0:
                    out.append(("turn", d[0], 0, 0, 0))
                    due.remove(d)
        due.append([c, lag])
    return out + [("turn", d[0], 0, 0, 0) for d in due]


QRING = 4
SHUT = (JH - 1,)
AHEAD = 3
HEAD_UNITS = late_turns(range(AHEAD), 4)


PE_COLUMN = 0.42
PV_COLUMN = 1.79
STEP_LEAST = 1400
TURNED = 1
LAG = 3
LAG_STEPS = 2
TOLERATED = 150
BACKLOG = 2000


def side_cost(unit):
    kind, c, t, kc, pair = unit
    if kind == "full":
        return 2 * CW * PE_COLUMN, 100 + 2 * CW * 1.02
    if kind == "diag":
        return 2 * (t + 1) * P * PE_COLUMN, 2 * (75 + (t + 1) * P * 1.04)
    return 400, (0 if kind == "turn" else 800)


def earliest_step(unit, next_quad):
    kind, c, t, kc, pair = unit
    if kind == "norm":
        return min(first_step(c + 1) + BEHIND + 1, NSTEPS)
    if next_quad:
        return first_step(c + QRING + 1) + 3
    return first_step(c - AHEAD) + 2


def side_units():
    at = [[[] for _ in range(JH + 1)] for _ in range(NSTEPS + 1)]
    width = [min(CW, CW * (c + 1) - P * kb) for c, kb in STEPS]
    place = [[w * PE_COLUMN] * (JH - 1) + [max(w * PV_COLUMN, STEP_LEAST - w * JH * PE_COLUMN), w * PE_COLUMN]
             for w in width]
    begins = [sum(sum(t) for t in place[:s]) for s in range(NSTEPS + 1)]
    queue = [(u, False) for u in late_turns(range(AHEAD, CHUNKS), LAG)] + [(u, True) for u in HEAD_UNITS]
    norms = [("norm", c, 0, 0, 0) for c in range(CHUNKS)]
    due, pe_work, dve_work = [], 0.0, 0.0
    for unit, next_quad in queue:
        pe_work, dve_work = pe_work + side_cost(unit)[0], dve_work + side_cost(unit)[1]
        if unit[0] == "turn":
            last = NSTEPS - 1 if next_quad else first_step(unit[1]) - TURNED
            due.append((begins[last] - LAG_STEPS * 2000, pe_work, dve_work))
    base = pe_now = paced = pe_done = dve_done = 0.0
    free_at = [0.0, 0.0]
    cut = 0
    for s in range(NSTEPS):
        for j in range(JH + 1):
            base += place[s][j]
            pe_now += place[s][j]
            if j in SHUT and s < NSTEPS - 1:
                continue
            while True:
                if norms and s >= earliest_step(norms[0], False) and j == JH:
                    unit, pace = norms.pop(0), 1.0
                elif queue and s >= earliest_step(*queue[0]) and not (queue[0][0][0] == "turn" and s < cut + LAG_STEPS):
                    pace = max([(dve - dve_done) / max(t + pe - base - pe_done, 1) for t, pe, dve in due
                                if dve > dve_done] + [0.3])
                    flush = s == NSTEPS - 1 and j == JH - 1 and len(queue) > 2
                    if (paced > pe_now + BACKLOG or free_at[0] > pe_now + TOLERATED) and not flush:
                        break
                    unit = queue.pop(0)[0]
                    pe_done += side_cost(unit)[0]
                    dve_done += side_cost(unit)[1]
                    if unit[0] == "diag":
                        cut = s
                else:
                    break
                pe_now = max(pe_now, free_at[0]) + side_cost(unit)[0]
                paced = max(paced, pe_now) + side_cost(unit)[1] / min(pace, 1.0)
                free_at = [free_at[1], max(max(free_at), pe_now) + side_cost(unit)[1]]
                at[s][j].append(unit)
    at[NSTEPS][0] += [u for u, _ in queue] + norms
    return at


SIDE = side_units()
SIDE_FLAT = [u for step in SIDE for us in step for u in us]
HEAD_N = len(HEAD_UNITS)
SIDE_N = len(SIDE_FLAT)
assert SIDE_N % 2 == 0
assert all(s < first_step(u[1]) or u[1] < AHEAD
           for s, step in enumerate(SIDE) for us in step for u in us if u[0] == "turn")


def build(nc, x, wqk, wvT, woT, lnsb, attnT, attnb, w1, b1, w2, b2, nextT, nextb, cvec, wmod,
          rope, ident, mask, later, lastones, out):
    parts = nc.dram_tensor("parts_scratch", [PARTS, 2, HD // 2, 2 * JH, QUADS, S], BF16, kind="Internal").ap()

    with ExitStack() as whole:
        def sem(name):
            return whole.enter_context(nc.semaphore(name))

        def keep(name, shape, dt=F32):
            return whole.enter_context(nc.sbuf_tensor(name, shape, dt))

        PS = whole.enter_context(nc.psum_tensor("banks", [P, 8 * 512], F32))

        def bank(b, n=1):
            return PS[:, b * 512:(b + n) * 512]

        id_f = keep("id_f", [P, P])
        mod_bc = keep("mod_bc", [P, 6 * D])
        mod_col = keep("mod_col", [P, 16])
        wo_g = keep("wo_g", [P, HALF, D])
        att_o = keep("att_o", [P, S // P, D])

        project(nc, sem, bank, whole, dict(
            x=x, wqk=wqk, wvT=wvT, woT=woT, cvec=cvec, wmod=wmod, rope=rope, ident=ident, parts=parts,
            id_f=id_f, mod_bc=mod_bc, mod_col=mod_col, wo_g=wo_g, att_o=att_o, mask=mask,
            later=later, lastones=lastones))
        feed(nc, sem, bank, dict(
            x=x, lnsb=lnsb, attnT=attnT, attnb=attnb, w1=w1, b1=b1, w2=w2, b2=b2, nextT=nextT, nextb=nextb,
            id_f=id_f, mod_bc=mod_bc, mod_col=mod_col, wo_g=wo_g, att_o=att_o, out=out))


def begin(engine, *semaphores):
    for s in semaphores:
        engine.sem_inc(s, FREE)


def alone(engine, passed):
    engine.sem_inc(passed, 1)


def project(nc, sem, bank, whole, a):
    with ExitStack() as ctx:
        v_all = ctx.enter_context(nc.sbuf_tensor("v_all", [P, QUADS, S // P, JH, VW], F32))
        with ExitStack() as mine:
            project_block(nc, sem, bank, mine, a, v_all)
        with ExitStack() as mine:
            attend_block(nc, sem, bank, mine, a, v_all)


def project_block(nc, sem, bank, ctx, a, v_all):
    def sb(name, shape, dt=F32):
        return ctx.enter_context(nc.sbuf_tensor(name, shape, dt))

    w_qk = sb("w_qk", [P, HALF, 2, 2, P])
    w_v = sb("w_v", [P, HALF, D])
    w_m = sb("w_m", [P, HALF, 6 * D])
    w_o = sb("w_o", [P, HALF, D])
    c_col = sb("c_col", [P, HALF])
    c_exp = sb("c_exp", [P, HALF])
    c_inv = sb("c_inv", [P, HALF])
    c_silu = sb("c_silu", [P, HALF])
    c_wide = sb("c_wide", [P, HALF, P])
    ones = sb("ones", [P, P])
    gate_s = sb("gate_s", [P, 2, D])
    gate_m = sb("gate_m", [P, 2, D])
    half_neg = sb("half_neg", [P, TILES])
    xs = sb("xs", [P, 2, TILES, D])
    stats = sb("stats", [P, 2, TILES, 6])
    mv = sb("mv", [P, 2, TILES, 2])
    var_e = sb("var_e", [P, 2, TILES])
    rstd = sb("rstd", [P, 2, TILES])
    xn = sb("xn", [P, TILES, D])
    hT = sb("hT", [P, 2, HALF, CW])
    cs = sb("cs", [P, 2, 2, CW])
    qk = sb("qk", [P, 2, 2, CW])
    rot = sb("rot", [P, 2, 2, 2, CW])
    rest = sb("rest", [P, 2, 2, 2, CW])
    pp = [sb(f"p{n + 1}", [P, 2, 2, CW], BF16) for n in range(PARTS)]

    passed_dve, passed_pool, passed_sp = sem("passed_dve"), sem("passed_pool"), sem("passed_sp")
    c_in, id_in, wmod_in, wqk_in, wv_in, late_in = (sem("c_in"), sem("id_in"), sem("wmod_in"), sem("wqk_in"),
                                                    sem("wv_in"), sem("late_in"))
    ones_set, silu_e, silu_s = sem("ones_set"), sem("silu_e"), sem("silu_s")
    mod_ps, mod_ev, gate_st, wo_rdy = sem("mod_ps"), sem("mod_ev"), sem("gate_st"), sem("wo_rdy")
    const_p = sem("const_p")
    x_in = [sem("x_in0"), sem("x_in1")]
    cs_in = [sem("cs_in0"), sem("cs_in1")]
    st_done, mv_done, var_done, rstd_done, xn_done = (sem("st_done"), sem("mv_done"), sem("var_done"),
                                                      sem("rstd_done"), sem("xn_done"))
    hT_ps, hT_ev = sem("hT_ps"), sem("hT_ev")
    qk_ps, qk_ev = sem("qk_ps"), sem("qk_ev")
    v_ps, v_ev = sem("v_ps"), sem("v_ev")
    cos_done, sin_done, rot_done = sem("cos_done"), sem("sin_done"), sem("rot_done")
    p1_done, r1_done, p2_done, p3_done = sem("p1_done"), sem("r1_done"), sem("p2_done"), sem("p3_done")
    stored = [sem(f"stored{n}") for n in range(PARTS)]
    STORES = 4
    T_BANKS, V_BANKS, QK_BANKS = (0, 1), (2, 3), 4

    def slots(engine, slot):
        slot(0, 0)
        with engine.Fori(0, 2) as i:
            for off in (1, 2):
                slot(i, off)
        for c in range(5, CHUNKS + 1):
            slot(0, c)

    with nc.Block() as block:
        @block.sync
        def _(sp):
            begin(sp, *stored)

            def load_x(i, off):
                if off >= 2:
                    sp.wait_ge(xn_done, TILES * (i * 2 + off - 1))
                    alone(sp, passed_sp)
                sp.dma_start(xs[:, off % 2, :, :],
                             a["x"][0, bass.ds((i * 2 + off) * CW, CW), :].rearrange("(t p) d -> p t d", p=P))\
                    .then_inc(x_in[off % 2], 16)

            def load_cs(i, off):
                if off >= 2:
                    sp.wait_ge(cos_done, 2 * (i * 2 + off - 1))
                    sp.wait_ge(sin_done, 2 * (i * 2 + off - 1))
                    alone(sp, passed_sp)
                sp.dma_start(cs[:, off % 2, :, :], a["rope"][:, :, bass.ds((i * 2 + off) * CW, CW)])\
                    .then_inc(cs_in[off % 2], 16)

            def store(i, off, n):
                done = (p1_done, p2_done, p3_done)[n]
                sp.wait_ge(done, (FREE if n == 2 else 0) + 2 * (i * 2 + off) + 2)
                alone(sp, passed_sp)
                for z in range(2):
                    rows = slice(z * P // 2, (z + 1) * P // 2)
                    for eo in range(2):
                        sp.dma_start(a["parts"][n, eo, :, :, 2 * z:2 * z + 2, bass.ds((i * 2 + off) * CW, CW)]
                                     .rearrange("d h b s -> (d h) b s"),
                                     pp[n][rows, eo, :, :]).then_inc(stored[n], 16)

            sp.dma_start(c_col[:, :], a["cvec"]).then_inc(c_in, 16)
            load_x(0, 0)
            sp.dma_start(a["id_f"][:, :], a["ident"]).then_inc(id_in, 16)
            w_mod = a["wmod"].rearrange("(h p) n -> p h n", p=P)
            sp.dma_start(w_m[:, :, 0:2 * D], w_mod[:, :, 0:2 * D]).then_inc(wmod_in, 16)
            sp.dma_start(w_qk[:, :, :, :, :], a["wqk"].rearrange("(h p) e b n -> p h e b n", p=P)).then_inc(wqk_in, 16)
            load_x(0, 1)
            load_cs(0, 0)
            sp.dma_start(w_v[:, :, :], a["wvT"].rearrange("(h p) n -> p h n", p=P)).then_inc(wv_in, 16)
            load_cs(0, 1)
            sp.dma_start(w_m[:, :, 2 * D:], w_mod[:, :, 2 * D:]).then_inc(late_in, 16)
            sp.dma_start(w_o[:, :, :], a["woT"].rearrange("(h p) n -> p h n", p=P)).then_inc(late_in, 16)

            def slot(i, off):
                if 0 < off < CHUNKS - 1:
                    load_cs(i, off + 1)
                if off:
                    store(i, off - 1, 0)
                    store(i, off - 1, 1)
                if off + 3 < CHUNKS:
                    load_x(i, off + 3)
                if off:
                    store(i, off - 1, 2)

            load_x(0, 2)
            slots(sp, slot)
            for n in range(PARTS):
                sp.wait_ge(stored[n], FREE + 16 * STORES * CHUNKS)

        @block.gpsimd
        def _(pool):
            begin(pool, p3_done)
            nc.gpsimd.memset(half_neg[:, :], -0.5).then_inc(const_p, 1)
            nc.gpsimd.memset(ones[:, :], 1.0).then_inc(ones_set, 1)
            pool.wait_ge(const_p, 1)

            def inverse_std(i, off):
                pool.wait_ge(mv_done, TILES * (i * 2 + off + 1))
                if off >= 2:
                    pool.wait_ge(xn_done, TILES * (i * 2 + off - 1))
                alone(pool, passed_pool)
                nc.gpsimd.tensor_scalar(var_e[:, off % 2, :], mv[:, off % 2, :, 1], EPS, None, ALU.add)\
                    .then_inc(var_done, 1)
                pool.wait_ge(var_done, i * 2 + off + 1)
                nc.gpsimd.tensor_tensor(rstd[:, off % 2, :], var_e[:, off % 2, :], half_neg[:, :], ALU.pow)\
                    .then_inc(rstd_done, 1)

            def by_sin(i, off):
                par = off % 2
                pool.wait_ge(cs_in[par], 16 * (i + off // 2 + 1))
                if off:
                    pool.wait_ge(p3_done, FREE + 2 * (i * 2 + off - 1))
                for eo in range(2):
                    pool.wait_ge(qk_ev, 2 * (i * 2 + off) + eo + 1)
                    nc.gpsimd.tensor_tensor(rest[:, par, eo, :, :], qk[:, eo, :, :],
                                            cs[:, par, 1:2, :].broadcast_to([P, 2, CW]), ALU.mult)\
                        .then_inc(sin_done, 1)

            def part3(i, off):
                pool.wait_ge(stored[2], FREE + 16 * STORES * (i * 2 + off))
                for eo in range(2):
                    pool.wait_ge(r1_done, FREE + 2 * (i * 2 + off) + eo + 1)
                    pool.wait_ge(p2_done, 2 * (i * 2 + off) + eo + 1)
                    nc.gpsimd.tensor_tensor(pp[2][:, eo, :, :], rest[:, off % 2, eo, :, :], pp[1][:, eo, :, :],
                                            ALU.subtract).then_inc(p3_done, 1)

            def slot(i, off):
                if off < CHUNKS:
                    by_sin(i, off)
                if off + 2 < CHUNKS:
                    inverse_std(i, off + 2)
                if 0 < off < CHUNKS:
                    part3(i, off - 1)

            inverse_std(0, 0)
            nc.gpsimd.memset(v_all[:, :, :, :, HD:VW], 1.0).then_inc(const_p, 1)
            inverse_std(0, 1)
            slots(pool, slot)

        @block.vector
        def _(dve):
            begin(dve, r1_done)

            def moments(i, off):
                par = off % 2
                dve.wait_ge(x_in[par], 16 * (i + off // 2 + 1))
                for t in range(TILES):
                    nc.vector.bn_stats(stats[:, par, t, :], xs[:, par, t, :]).then_inc(st_done, 1)
                for t in range(TILES):
                    dve.wait_ge(st_done, TILES * (i * 2 + off) + t + 1)
                    alone(dve, passed_dve)
                    nc.vector.bn_aggr(mv[:, par, t, :], stats[:, par, t, :]).then_inc(mv_done, 1)

            def normalise(i, off):
                par = off % 2
                dve.wait_ge(rstd_done, i * 2 + off + 1)
                if off:
                    dve.wait_ge(hT_ps, HALF * (i * 2 + off))
                for t in range(TILES):
                    nc.vector.tensor_scalar(xn[:, t, :], xs[:, par, t, :], mv[:, par, t, 0:1],
                                            rstd[:, par, t:t + 1], ALU.subtract, ALU.mult).then_inc(xn_done, 1)

            def by_cos(i, off):
                par = off % 2
                dve.wait_ge(cs_in[par], 16 * (i + off // 2 + 1))
                if off:
                    dve.wait_ge(r1_done, FREE + 2 * (i * 2 + off - 1))
                for eo in range(2):
                    dve.wait_ge(qk_ev, 2 * (i * 2 + off) + eo + 1)
                    nc.vector.tensor_tensor(rot[:, par, eo, :, :], qk[:, eo, :, :],
                                            cs[:, par, 0:1, :].broadcast_to([P, 2, CW]), ALU.mult)\
                        .then_inc(cos_done, 1)

            def rotate(i, off):
                par = off % 2
                dve.wait_ge(sin_done, 2 * (i * 2 + off) + 2)
                dve.wait_ge(cos_done, 2 * (i * 2 + off) + 2)
                for eo in range(2):
                    nc.vector.tensor_tensor(rot[:, par, eo, :, :], rot[:, par, eo, :, :], rest[:, par, 1 - eo, :, :],
                                            ALU.subtract if eo == 0 else ALU.add).then_inc(rot_done, 1)

            def cut(i, off):
                par = off % 2
                dve.wait_ge(rot_done, 2 * (i * 2 + off) + 2)
                for eo in range(2):
                    dve.wait_ge(p1_done, 2 * (i * 2 + off) + eo + 1)
                    nc.vector.tensor_tensor(rest[:, par, eo, :, :], rot[:, par, eo, :, :], pp[0][:, eo, :, :],
                                            ALU.subtract).then_inc(r1_done, 1)

            def modulation():
                dve.wait_ge(mod_ps, 3)
                for n in (1, 2):
                    nc.vector.tensor_copy(a["mod_bc"][:, n * 512:(n + 1) * 512], bank(n - 1)).then_inc(mod_ev, 1)
                for k, plus in ((2, 0.0), (3, 1.0)):
                    nc.vector.tensor_scalar(a["mod_col"][:, 2 * k:2 * k + 2], bank(QK_BANKS)[:, 2 * k:2 * k + 2], plus,
                                            None, ALU.add).then_inc(mod_ev, 1)
                dve.wait_ge(mod_ev, 6)
                nc.vector.tensor_scalar(a["mod_bc"][:, 4 * D:5 * D], a["mod_bc"][:, 4 * D:5 * D], 1.0, None, ALU.add)\
                    .then_inc(mod_ev, 1)
                for n, k in enumerate((2, 5)):
                    gate = a["mod_bc"][:, k * D:(k + 1) * D]
                    nc.vector.tensor_scalar(gate_s[:, n, :], gate, 0.0, 2.0, ALU.is_ge, ALU.mult).then_inc(gate_st, 1)
                    nc.vector.scalar_tensor_tensor(out=gate_m[:, n, :], in0=gate, scalar=-1.0, in1=gate,
                                                   op0=ALU.mult, op1=ALU.max).then_inc(gate_st, 1)
                dve.wait_ge(gate_st, 4)
                for n in range(2):
                    nc.vector.tensor_scalar(gate_m[:, n, :], gate_m[:, n, :], 0.25, None, ALU.max).then_inc(gate_st, 1)
                dve.wait_ge(gate_st, 6)
                for n, k in enumerate((2, 5)):
                    nc.vector.scalar_tensor_tensor(out=a["mod_bc"][:, k * D:(k + 1) * D], in0=gate_s[:, n, :],
                                                   scalar=-1.0, in1=gate_m[:, n, :], op0=ALU.add, op1=ALU.mult)\
                        .then_inc(gate_st, 1)
                dve.wait_ge(gate_st, 8)
                for h in range(HALF):
                    nc.vector.tensor_tensor(a["wo_g"][:, h, :], w_o[:, h, :], a["mod_bc"][:, 2 * D:3 * D], ALU.mult)\
                        .then_inc(wo_rdy, 1)
                dve.wait_ge(wo_rdy, 2)

            dve.wait_ge(silu_e, 1)
            nc.vector.tensor_scalar(c_inv[:, :], c_exp[:, :], 1.0, None, ALU.add).then_inc(silu_s, 1)
            dve.wait_ge(silu_s, 1)
            nc.vector.reciprocal(c_exp[:, :], c_inv[:, :]).then_inc(silu_s, 1)
            dve.wait_ge(silu_s, 2)
            nc.vector.tensor_tensor(c_silu[:, :], c_col[:, :], c_exp[:, :], ALU.mult).then_inc(silu_s, 1)
            moments(0, 0)
            normalise(0, 0)
            dve.wait_ge(mod_ps, 1)
            for k, plus in ((0, 0.0), (1, 1.0)):
                nc.vector.tensor_scalar(a["mod_col"][:, 2 * k:2 * k + 2], bank(QK_BANKS)[:, 2 * k:2 * k + 2], plus,
                                        None, ALU.add).then_inc(mod_ev, 1)
            dve.wait_ge(silu_s, 3)
            dve.wait_ge(ones_set, 1)
            for h in range(HALF):
                nc.vector.tensor_scalar(c_wide[:, h, :], ones[:, :], c_silu[:, h:h + 1], None, ALU.mult)\
                    .then_inc(silu_s, 1)

            def slot(i, off):
                if off:
                    rotate(i, off - 1)
                if off + 1 < CHUNKS:
                    normalise(i, off + 1)
                if off < CHUNKS:
                    by_cos(i, off)
                if off + 2 < CHUNKS:
                    moments(i, off + 2)
                if off:
                    cut(i, off - 1)

            moments(0, 1)
            slots(dve, slot)
            dve.wait_ge(stored[2], FREE + 16 * STORES * (CHUNKS - 1))
            dve.wait_ge(r1_done, FREE + 2 * CHUNKS)
            for eo in range(2):
                dve.wait_ge(p2_done, 2 * (CHUNKS - 1) + eo + 1)
                nc.vector.tensor_tensor(pp[2][:, eo, :, :], rest[:, (CHUNKS - 1) % 2, eo, :, :], pp[1][:, eo, :, :],
                                        ALU.subtract).then_inc(p3_done, 1)
            dve.wait_ge(late_in, 32)
            modulation()

        @block.scalar
        def _(act):
            act.wait_ge(c_in, 16)
            nc.scalar.activation(c_exp[:, :], c_col[:, :], ACT.Exp, scale=-1.0).then_inc(silu_e, 1)
            act.wait_ge(mod_ev, 2)

            def modulate(i, off):
                if off >= 2:
                    act.wait_ge(v_ps, TILES * (i * 2 + off - 1))
                for h in range(HALF):
                    act.wait_ge(hT_ps, HALF * (i * 2 + off) + h + 1)
                    nc.scalar.activation(hT[:, off % 2, h, :], bank(T_BANKS[h]), ACT.Identity,
                                         bias=a["mod_col"][:, h:h + 1], scale=a["mod_col"][:, 2 + h:3 + h])\
                        .then_inc(hT_ev, 1)

            def take_qk(i, off):
                for eo in range(2):
                    act.wait_ge(qk_ps, 2 * (i * 2 + off) + eo + 1)
                    if off:
                        act.wait_ge(cos_done, 2 * (i * 2 + off - 1) + eo + 1)
                        act.wait_ge(sin_done, 2 * (i * 2 + off - 1) + eo + 1)
                    nc.scalar.activation(qk[:, eo, :, :], bank(QK_BANKS + 2 * eo, 2).rearrange("p (b s) -> p b s", b=2),
                                         ACT.Copy).then_inc(qk_ev, 1)

            def take_v(i, off):
                for t in range(TILES):
                    act.wait_ge(v_ps, TILES * (i * 2 + off) + t - t % 2 + 2)
                    nc.scalar.activation(
                        v_all[:, :, bass.ds((i * 2 + off) * TILES + t, 1), :, 0:HD]
                        .rearrange("p g o j d -> p g (o j) d"),
                        bank(V_BANKS[t // 2])[:, (t % 2) * D:(t % 2 + 1) * D]
                        .rearrange("p (g j d) -> p g j d", g=QUADS, j=JH), ACT.Copy).then_inc(v_ev, 1)

            def part1(i, off):
                act.wait_ge(stored[0], FREE + 16 * STORES * (i * 2 + off))
                act.wait_ge(r1_done, FREE + 2 * (i * 2 + off))
                for eo in range(2):
                    act.wait_ge(rot_done, 2 * (i * 2 + off) + eo + 1)
                    nc.scalar.activation(pp[0][:, eo, :, :], rot[:, off % 2, eo, :, :], ACT.Copy).then_inc(p1_done, 1)

            def part2(i, off):
                act.wait_ge(stored[1], FREE + 16 * STORES * (i * 2 + off))
                act.wait_ge(p3_done, FREE + 2 * (i * 2 + off))
                for eo in range(2):
                    act.wait_ge(r1_done, FREE + 2 * (i * 2 + off) + eo + 1)
                    nc.scalar.activation(pp[1][:, eo, :, :], rest[:, off % 2, eo, :, :], ACT.Copy).then_inc(p2_done, 1)

            def slot(i, off):
                if off:
                    part1(i, off - 1)
                if off < CHUNKS:
                    take_qk(i, off)
                if off + 1 < CHUNKS:
                    modulate(i, off + 1)
                if off < CHUNKS:
                    take_v(i, off)
                if off:
                    part2(i, off - 1)

            modulate(0, 0)
            slots(act, slot)

        @block.tensor
        def _(pe):
            def mod_columns(chunks):
                for k, m in chunks:
                    for half in range(HALF):
                        for h in range(HALF):
                            col = m * D + half * P
                            mm = nc.tensor.matmul(bank(QK_BANKS)[:, 2 * k + half:2 * k + half + 1],
                                                  w_m[:, h, col:col + P], c_silu[:, h:h + 1],
                                                  start=(h == 0), stop=(h == HALF - 1))
                mm.then_inc(mod_ps, 1)

            def turn(i, off):
                pe.wait_ge(xn_done, TILES * (i * 2 + off + 1))
                if off:
                    pe.wait_ge(hT_ev, HALF * (i * 2 + off))
                for h in range(HALF):
                    for t in range(TILES):
                        mm = nc.tensor.transpose(bank(T_BANKS[h])[:, t * P:(t + 1) * P], xn[:, t, h * P:(h + 1) * P],
                                                 a["id_f"][:, :])
                    mm.then_inc(hT_ps, 1)

            def slot(i, off):
                if off == CHUNKS:
                    return
                pe.wait_ge(hT_ev, HALF * (i * 2 + off + 1))
                for eo in range(2):
                    if off:
                        pe.wait_ge(qk_ev, 2 * (i * 2 + off - 1) + eo + 1)
                    for b in range(2):
                        for h in range(HALF):
                            mm = nc.tensor.matmul(bank(QK_BANKS + 2 * eo + b), w_qk[:, h, eo, b, :],
                                                  hT[:, off % 2, h, :], start=(h == 0), stop=(h == HALF - 1))
                    mm.then_inc(qk_ps, 1)
                if off + 1 < CHUNKS:
                    turn(i, off + 1)
                if off == 0:
                    pe.wait_ge(wv_in, 16)
                else:
                    pe.wait_ge(v_ev, TILES * (i * 2 + off))
                for t in range(TILES):
                    for h in range(HALF):
                        mm = nc.tensor.matmul(bank(V_BANKS[t // 2])[:, (t % 2) * D:(t % 2 + 1) * D],
                                              hT[:, off % 2, h, t * P:(t + 1) * P], w_v[:, h, :],
                                              start=(h == 0), stop=(h == HALF - 1))
                    mm.then_inc(v_ps, 1)

            pe.wait_ge(id_in, 16)
            turn(0, 0)
            pe.wait_ge(silu_s, 3)
            pe.wait_ge(wmod_in, 16)
            mod_columns(((0, 0), (1, 1)))
            pe.wait_ge(wqk_in, 16)
            pe.wait_ge(mod_ev, 2)
            slots(pe, slot)
            pe.wait_ge(silu_s, 5)
            pe.wait_ge(late_in, 32)
            pe.wait_ge(hT_ev, HALF * CHUNKS)
            for n in (1, 2):
                for h in range(HALF):
                    mm = nc.tensor.matmul(bank(n - 1), c_wide[:, h, :], w_m[:, h, n * 512:(n + 1) * 512],
                                          start=(h == 0), stop=(h == HALF - 1))
            mm.then_inc(mod_ps, 1)
            pe.wait_ge(qk_ev, 2 * CHUNKS)
            mod_columns(((2, 3), (3, 4)))


def attend_block(nc, sem, bank, ctx, a, v_all):
    def sb(name, shape, dt=F32):
        return ctx.enter_context(nc.sbuf_tensor(name, shape, dt))

    k_aug = sb("k_aug", [P, JH, S], BF16)
    k_next = sb("k_next", [P, JH, AHEAD * CW], BF16)
    q_aug = sb("q_aug", [P, QRING, JH, CW], BF16)
    v_cur = sb("v_cur", [P, S // P, JH, VW])
    prob = sb("prob", [P, PROBS, JH, CW])
    o_sb = sb("o_sb", [P, 2, CW])
    mask = sb("mask_sb", [P, CW])
    id_b = sb("id_b", [P, P], BF16)
    later_k = sb("later_k", [P, P], BF16)
    mx = sb("mx", [P, QRING, TILES, JH, CHUNKS])
    nm = sb("nm", [P, QRING, TILES * JH])
    nm_r = sb("nm_r", [P, QRING, TILES * JH])
    nm_p = sb("nm_p", [P, QRING, TILES * JH, PARTS], BF16)
    l_inv = sb("l_inv", [P, 2, TILES, JH, 1])

    score = [bank(n) for n in range(SBANKS)]
    pv = bank(3)
    side = [bank(4, 2), bank(6, 2)]
    PV_ROWS = 32

    passed_dve, passed_pool, passed_sp = sem("a_passed_dve"), sem("a_passed_pool"), sem("a_passed_sp")
    consts_in, mask_in, id_cast, pv_zero = sem("consts_in"), sem("mask_in"), sem("id_cast"), sem("pv_zero")
    k_in = [sem(f"k_in{r}") for r in range(CHUNKS)]
    k_next_in = [sem(f"k_next_in{r}") for r in range(AHEAD)]
    v_in = [sem(f"v_in{r}") for r in range(CHUNKS)]
    q_in = [sem(f"q_in{r}") for r in range(QRING)]
    st_done = sem("scores_done")
    exp_done = [sem(f"exp_done{b}") for b in range(SBANKS)]
    pv_done = [sem(f"pv_done{b}") for b in range(PROBS)]
    out_ev = sem("out_ev")
    side_done = sem("side_done")
    side_free = [sem("side_free0"), sem("side_free1")]
    m_rows = sb("m_rows", [P, 2, CW], BF16)
    rows_done = [sem("rows_done0"), sem("rows_done1")]
    nm_done, cut_done = sem("nm_done"), sem("cut_done")
    max_done, linv_done = sem("max_done"), sem("linv_done")

    def exp_count(g, u):
        return g * (UNITS // SBANKS) + u // SBANKS + 1

    def slot_of(n, head):
        return n % 2 if head else (HEAD_N + 1 + n) % 2

    def uses_before(n, head, g):
        if head:
            return n // 2
        before = len([m for m in range(HEAD_N) if m % 2 == slot_of(n, False)])
        return g * (SIDE_N // 2) + before + n // 2

    def ready_count(n, head, g):
        return n + 1 if head else g * SIDE_N + HEAD_N + n + 1

    def items(c, g, head):
        if head:
            return c
        return g * CHUNKS + c if c >= AHEAD else g * CHUNKS + CHUNKS + c

    def pairs(c, g, head):
        if head:
            return c // 2
        return g * (CHUNKS // 2) + (c // 2 if c >= AHEAD else CHUNKS // 2 + c // 2)

    with nc.Block() as block:
        @block.sync
        def _(sp):
            def load_parts(to, heads, runs, g, c, done):
                rows = a["parts"][:, :, :, heads, bass.ds(g, 1), c * CW:(c + 1) * CW]\
                    .rearrange("n e d j o s -> (n e d) (j o) s")
                for block, part, blocks in runs:
                    sp.dma_start(to[block * HD:(block + blocks) * HD], rows[part * HD:(part + blocks) * HD])\
                        .then_inc(done, 16)

            def load_keys(g, r):
                load_parts(k_aug[:, :, r * CW:(r + 1) * CW], slice(JH, 2 * JH), K_RUNS, g, r, k_in[r])

            def load_values(g, r):
                sp.dma_start(v_cur[:, r * TILES:(r + 1) * TILES, :, :],
                             v_all[:, bass.ds(g, 1), r * TILES:(r + 1) * TILES, :, :]
                             .rearrange("p o k j v -> p (o k) j v")).then_inc(v_in[r], 16)

            def load_queries(g, c):
                load_parts(q_aug[:, c % QRING, :, :], slice(0, JH), Q_RUNS, g, c, q_in[c % QRING])

            for r in range(AHEAD):
                load_keys(0, r)
                load_queries(0, r)
                if r == 0:
                    sp.dma_start(mask[:, :], a["mask"]).then_inc(mask_in, 16)
            sp.dma_start(later_k[:, :], a["later"]).then_inc(consts_in, 16)
            sp.dma_start(k_aug[KROWS:KROWS + MROWS, :, :], a["lastones"]).then_inc(consts_in, 16)
            load_values(0, 0)
            for r in range(AHEAD, CHUNKS):
                load_keys(0, r)
            for r in range(1, CHUNKS):
                load_values(0, r)
            with sp.Fori(0, QUADS) as g:
                for c in range(AHEAD, CHUNKS):
                    if c > AHEAD:
                        sp.wait_ge(st_done, FREE + g * UNITS + JH * first_step(c - QRING + 1))
                    else:
                        sp.wait_ge(st_done, FREE + g * UNITS)
                    alone(sp, passed_sp)
                    load_queries(g, c)
                    if c == AHEAD:
                        sp.wait_ge(side_done, HEAD_N + g * SIDE_N)
                        alone(sp, passed_sp)
                        for r in range(AHEAD):
                            load_parts(k_next[:, :, r * CW:(r + 1) * CW], slice(JH, 2 * JH), K_RUNS, (g + 1) % QUADS,
                                       r, k_next_in[r])
                for c in range(AHEAD):
                    sp.wait_ge(st_done, FREE + g * UNITS + JH * first_step(c + QRING + 1))
                    alone(sp, passed_sp)
                    load_queries((g + 1) % QUADS, c)
                for r in range(CHUNKS):
                    last = first_step(CHUNKS - 1) + r * TILES + TILES - 1
                    sp.wait_ge(st_done, FREE + g * UNITS + JH * (last + 1))
                    alone(sp, passed_sp)
                    load_keys((g + 1) % QUADS, r)
                    sp.wait_ge(pv_done[last % PROBS], FREE + g * (NSTEPS // PROBS) + last // PROBS + 1)
                    alone(sp, passed_sp)
                    load_values((g + 1) % QUADS, r)
            for r in range(AHEAD):
                sp.wait_ge(k_next_in[r], 16 * len(K_RUNS) * QUADS)
            for r in range(CHUNKS):
                sp.wait_ge(k_in[r], 16 * len(K_RUNS) * (QUADS + 1))
                sp.wait_ge(v_in[r], 16 * (QUADS + 1))

        @block.tensor
        def _(pe):
            begin(pe, st_done, *pv_done)
            def key_loads(g, r):
                pe.wait_ge(k_in[r], (g + 1) * (16 * len(K_RUNS)))

            def side_unit(g, n, head):
                kind, c, t, kc, pair = HEAD_UNITS[n] if head else SIDE_FLAT[n]
                slot = side[slot_of(n, head)]
                pe.wait_ge(side_free[slot_of(n, head)], FREE + uses_before(n, head, g))
                if kind in ("full", "diag"):
                    width = CW if kind == "full" else (t + 1) * P
                    keys = k_next if not head and c < AHEAD else k_aug
                    for jj in range(2):
                        j = 2 * pair + jj
                        mm = nc.tensor.matmul(slot[:, jj * CW:jj * CW + width],
                                              q_aug[0:KROWS, c % QRING, j, t * P:(t + 1) * P],
                                              keys[0:KROWS, j, kc * CW:kc * CW + width], start=True, stop=True)
                elif kind == "turn":
                    pe.wait_ge(cut_done, (items(c, g, head) + 1) * 4)
                    for t in range(TILES):
                        mm = nc.tensor.transpose(
                            slot.bitcast(BF16)[KROWS:KROWS + MROWS, t * P:(t + 1) * P],
                            nm_p[:, c % QRING, t * JH:(t + 1) * JH, :].rearrange("p j n -> p (j n)"), id_b[:, :])
                else:
                    pe.wait_ge(out_ev, FREE + g * CHUNKS + c + 1)
                    for t in range(TILES):
                        mm = nc.tensor.transpose(slot[:, t * P:(t + 1) * P], o_sb[:, c % 2, t * P:(t + 1) * P],
                                                 a["id_f"][:, :])
                mm.then_inc(side_done, 1)

            def queries_loaded(g, c, head=False):
                uses = g * (CHUNKS // QRING) + c // QRING
                pe.wait_ge(q_in[c % QRING], (uses + 1) * (16 * len(Q_RUNS)))

            def beside(g, n, unit):
                if unit[0] in ("full", "diag"):
                    nxt = 1 if unit[1] < AHEAD else 0
                    if unit[0] == "diag" and unit[2] == 0 and unit[4] == 0 or unit[3] == 0:
                        queries_loaded(g + nxt, unit[1])
                    if nxt:
                        pe.wait_ge(k_next_in[unit[3]], (g + 1) * (16 * len(K_RUNS)))
                    else:
                        key_loads(g, unit[3])
                side_unit(g, n, False)

            def values(g, s):
                c, kb = STEPS[s]
                t = kb - TILES * c
                q0 = max(t, 0) * P
                if kb == 0:
                    pe.wait_ge(out_ev, FREE + g * CHUNKS + c)
                u = JH * s + JH - 1
                pe.wait_ge(exp_done[u % SBANKS], FREE + exp_count(g, u))
                if t >= 0:
                    pe.wait_ge(v_in[c], (g + 1) * 16)
                for j in range(JH):
                    mm = nc.tensor.matmul(pv[PV_ROWS * j:PV_ROWS * j + VW, q0:CW], v_cur[:, kb, j, :],
                                          prob[:, s % PROBS, j, q0:CW], start=(kb == 0),
                                          stop=(kb == TILES * (c + 1) - 1), skip_group_check=True)
                mm.then_inc(pv_done[s % PROBS], 1)

            pe.wait_ge(id_cast, 1)
            pe.wait_ge(pv_zero, 1)
            for n, unit in enumerate(HEAD_UNITS):
                if unit[0] != "turn":
                    key_loads(0, unit[3])
                    queries_loaded(0, unit[1])
                side_unit(0, n, True)
            pe.wait_ge(consts_in, 32)
            with pe.Fori(0, QUADS) as g:
                n = 0
                for s, (c, kb) in enumerate(STEPS):
                    t = kb - TILES * c
                    q0 = max(t, 0) * P
                    if kb == 0:
                        pe.wait_ge(rows_done[c % 2], FREE + (g * (CHUNKS // 2) + c // 2 + 1) * 16)
                    if t == 0:
                        key_loads(g, c)
                    for j in range(JH):
                        u = JH * s + j
                        if j == JH - 1:
                            if s >= BEHIND:
                                values(g, s - BEHIND)
                            for unit in SIDE[s][j]:
                                beside(g, n, unit)
                                n += 1
                        pe.wait_ge(exp_done[u % SBANKS], FREE + g * (UNITS // SBANKS) + u // SBANKS)
                        mm = nc.tensor.matmul(score[u % SBANKS][:, q0:CW],
                                              k_aug[0:KROWS + MROWS, j, kb * P:(kb + 1) * P],
                                              q_aug[0:KROWS + MROWS, c % QRING, j, q0:CW], start=True, stop=True)
                        if t >= 0:
                            mm = nc.tensor.matmul(score[u % SBANKS][:, q0:q0 + P], id_b[:, :], later_k[:, :],
                                                  start=False, stop=True, skip_group_check=True)
                        mm.then_inc(st_done, 1)
                        for unit in SIDE[s][j if j < JH - 1 else JH]:
                            beside(g, n, unit)
                            n += 1
                for s in range(NSTEPS - BEHIND, NSTEPS):
                    values(g, s)
                for _ in SIDE[NSTEPS][0]:
                    side_unit(g, n, False)
                    n += 1

        @block.scalar
        def _(act):
            begin(act, out_ev, *exp_done, *rows_done)
            nc.scalar.activation(id_b[:, :], a["id_f"][:, :], ACT.Copy).then_inc(id_cast, 1)

            def turn(g, n, head):
                c = (HEAD_UNITS if head else SIDE_FLAT)[n][1]
                act.wait_ge(side_done, ready_count(n, head, g))
                slot = side[slot_of(n, head)]
                act.wait_ge(rows_done[c % 2], FREE + pairs(c, g, head) * 16)
                nc.scalar.activation(m_rows[KROWS:KROWS + MROWS, c % 2, :],
                                     slot.bitcast(BF16)[KROWS:KROWS + MROWS, 0:CW], ACT.Copy)\
                    .then_inc(side_free[slot_of(n, head)], 1)

            def spread(g, n, head):
                c = (HEAD_UNITS if head else SIDE_FLAT)[n][1]
                act.wait_ge(side_free[slot_of(n, head)], FREE + uses_before(n, head, g) + 1)
                act.dma_start(q_aug[KROWS:KROWS + MROWS, c % QRING, :, :],
                              m_rows[KROWS:KROWS + MROWS, c % 2, :].unsqueeze(1).broadcast_to([MROWS, JH, CW]))\
                    .then_inc(rows_done[c % 2], 16)

            def take_out(g, c):
                last = first_step(c + 1) - 1
                act.wait_ge(pv_done[last % PROBS], FREE + g * (NSTEPS // PROBS) + last // PROBS + 1)
                act.wait_ge(linv_done, FREE + g * CHUNKS + c)
                nc.scalar.activation(o_sb[:, c % 2, :], pv, ACT.Copy).then_inc(out_ev, 1)

            for n, unit in enumerate(HEAD_UNITS):
                if unit[0] == "turn":
                    turn(0, n, True)
                    spread(0, n, True)
            act.wait_ge(pv_zero, 1)
            with act.Fori(0, QUADS) as g:
                n, turned = 0, None
                for s, (c, kb) in enumerate(STEPS):
                    t = kb - TILES * c
                    q0 = max(t, 0) * P
                    for j in range(JH):
                        u = JH * s + j
                        act.wait_ge(st_done, FREE + g * UNITS + u + 1)
                        if j == 0:
                            act.wait_ge(pv_done[s % PROBS], FREE + g * (NSTEPS // PROBS) + s // PROBS)
                        nc.scalar.activation(prob[:, s % PROBS, j, q0:CW], score[u % SBANKS][:, q0:CW], ACT.Exp,
                                             scale=float(HD) ** -0.5).then_inc(exp_done[u % SBANKS], 1)
                        if c and kb == BEHIND - 1 and j == JH - 1:
                            take_out(g, c - 1)
                        if turned is not None and j == 1 and s > turned_at:
                            spread(g, turned, False)
                            turned = None
                        for unit in (SIDE[s][JH] if j == JH - 1 else
                                     SIDE[s][j] + (SIDE[s][j + 1] if j == JH - 2 else [])):
                            if unit[0] == "turn":
                                turn(g, n, False)
                                turned, turned_at = n, s
                            n += 1
                take_out(g, CHUNKS - 1)
                for unit in SIDE[NSTEPS][0]:
                    if unit[0] == "turn":
                        turn(g, n, False)
                        turned = n
                    n += 1
                if turned is not None:
                    spread(g, turned, False)
            for par in range(2):
                act.wait_ge(rows_done[par], FREE + 16 * (QUADS * (CHUNKS // 2) + len(range(par, AHEAD, 2))))

        @block.vector
        def _(dve):
            begin(dve, linv_done, *side_free)
            nc.vector.memset(pv, 0.0).then_inc(pv_zero, 1)
            dve.wait_ge(mask_in, 16)

            def side_unit(g, n, head):
                kind, c, t, kc, pair = HEAD_UNITS[n] if head else SIDE_FLAT[n]
                if kind == "turn":
                    return
                dve.wait_ge(side_done, ready_count(n, head, g))
                if kind == "diag":
                    alone(dve, passed_dve)
                slot = side[slot_of(n, head)]
                free = side_free[slot_of(n, head)]
                if kind == "full":
                    nc.vector.tensor_reduce(mx[:, c % QRING, t, 2 * pair:2 * pair + 2, kc],
                                            slot.rearrange("p (j s) -> p j s", j=2), AX_X, ALU.max).then_inc(free, 1)
                elif kind == "diag":
                    width = (t + 1) * P
                    for jj in range(2):
                        ins = nc.vector.tensor_tensor_reduce(
                            slot[:, jj * CW:jj * CW + width], slot[:, jj * CW:jj * CW + width], mask[:, CW - width:CW],
                            1.0, NEG, ALU.add, ALU.max, mx[:, c % QRING, t, 2 * pair + jj, kc:kc + 1])
                        ins.then_inc(max_done if jj == 0 else free, 1)
                    if t == TILES - 1 and pair == 1:
                        dve.wait_ge(free, FREE + uses_before(n, head, g) + 1)
                        before = uses_before(n - 1, head, g) + 1
                        dve.wait_ge(side_free[slot_of(n - 1, head)], FREE + before)
                        nc.vector.tensor_reduce(nm[:, c % QRING, :],
                                                mx[:, c % QRING, :, :, 0:c + 1].rearrange("p t j k -> p (t j) k"),
                                                AX_X, ALU.max, negate=True).then_inc(nm_done, 1)
                else:
                    blocks = slot[:, 0:CW].rearrange("p (t j v) -> p t j v", t=TILES, j=JH)
                    nc.vector.reciprocal(l_inv[:, c % 2, :, :, :], blocks[:, :, :, HD:HD + 1]).then_inc(linv_done, 1)
                    dve.wait_ge(linv_done, FREE + g * CHUNKS + c + 1)
                    nc.vector.tensor_tensor(
                        a["att_o"][:, c * TILES:(c + 1) * TILES, bass.ds(g * (JH * HD), JH * HD)]
                        .rearrange("p t (j d) -> p t j d", j=JH),
                        blocks[:, :, :, 0:HD], l_inv[:, c % 2, :, :, :].broadcast_to([P, TILES, JH, HD]),
                        ALU.mult).then_inc(free, 1)

            for n in range(HEAD_N):
                side_unit(0, n, True)
            with dve.Fori(0, QUADS) as g:
                for n in range(SIDE_N):
                    side_unit(g, n, False)

        @block.gpsimd
        def _(pool):
            def cut(g, c, head):
                r = c % QRING
                k = items(c, g, head)
                pool.wait_ge(nm_done, k + 1)
                alone(pool, passed_pool)
                nc.gpsimd.tensor_copy(nm_p[:, r, :, 0], nm[:, r, :]).then_inc(cut_done, 1)
                pool.wait_ge(cut_done, 4 * k + 1)
                nc.gpsimd.tensor_tensor(nm_r[:, r, :], nm[:, r, :], nm_p[:, r, :, 0], ALU.subtract)\
                    .then_inc(cut_done, 1)
                pool.wait_ge(cut_done, 4 * k + 2)
                alone(pool, passed_pool)
                nc.gpsimd.tensor_copy(nm_p[:, r, :, 1], nm_r[:, r, :]).then_inc(cut_done, 1)
                pool.wait_ge(cut_done, 4 * k + 3)
                nc.gpsimd.tensor_tensor(nm_p[:, r, :, 2], nm_r[:, r, :], nm_p[:, r, :, 1], ALU.subtract)\
                    .then_inc(cut_done, 1)

            def after_unit(g, n, head):
                kind, c, t, kc, pair = (HEAD_UNITS if head else SIDE_FLAT)[n]
                if kind == "diag" and t == TILES - 1 and pair == 1:
                    cut(g, c, head)

            for n in range(HEAD_N):
                after_unit(0, n, True)
            with pool.Fori(0, QUADS) as g:
                for n in range(SIDE_N):
                    after_unit(g, n, False)


def feed(nc, sem, bank, a):
    with ExitStack() as ctx:
        x1 = ctx.enter_context(nc.sbuf_tensor("x1", [P, S // P, D], F32))
        xaT = a["att_o"][:, :, :].rearrange("p (c h t) d -> p c h (t d)", c=CHUNKS, h=HALF)
        def weights(name, shape, dt=F32):
            return ctx.enter_context(nc.sbuf_tensor(name, shape, dt))

        e = dict(w1_s=weights("w1_s", [P, HALF, HID]), w2_s=weights("w2_s", [P, HK, D]),
                 w1_p=[weights(f"w1_{part}", [P, HALF, HID], F32R) for part in ("hi", "lo")],
                 w2_p=[weights(f"w2_{part}", [P, HK, D], F32R) for part in ("hi", "lo")])
        for name in ("w1_in", "w2_in", "w1_hi", "w1_lo", "w2_hi", "w2_lo"):
            e[name] = sem(f"{name}_done")
        with ExitStack() as mine:
            mix_block(nc, sem, bank, mine, a, x1, xaT, e)
        with ExitStack() as mine:
            expert_block(nc, sem, bank, mine, a, x1, xaT, e)


def mix_block(nc, sem, bank, ctx, a, x1, xaT, e):
    def sb(name, shape, dt=F32):
        return ctx.enter_context(nc.sbuf_tensor(name, shape, dt))

    w_a = sb("w_a", [P, HALF, D])
    ab_col = sb("ab_col", [P, HALF])
    ln_col = sb("ln_col", [P, 2 * HALF])
    half_neg = sb("half_neg2", [P, TILES])
    xs = sb("xs2", [P, 2, TILES, D])
    oc = sb("oc", [P, 2, TILES, D])
    oT = sb("oT", [P, 2, HALF, CW])
    stats = sb("stats2", [P, 2, 2, TILES, 6])
    mv = sb("mv2", [P, 2, 2, TILES, 2])
    var_e = sb("var_e2", [P, 2, 2, TILES])
    rstd = sb("rstd2", [P, 2, 2, TILES])
    xn = sb("xn2", [P, 2, 2, TILES, D])
    h2 = sb("h2", [P, 2, TILES, D])
    h2T = sb("h2T", [P, 2, HALF, CW])
    x3T = sb("x3T", [P, HALF, CW])

    passed_dve, passed_pool, passed_sp = sem("m_passed_dve"), sem("m_passed_pool"), sem("m_passed_sp")
    w_in, x_in, o_in = sem("m_w_in"), [sem("m_x_in0"), sem("m_x_in1")], [sem("m_o_in0"), sem("m_o_in1")]
    half_set = sem("m_half_set")
    oT_ps, oT_ev, wo_ps, x1_done = sem("oT_ps"), sem("oT_ev"), sem("wo_ps"), sem("x1_done")
    st_done, mv_done, var_done, rstd_done, xn_done = (
        [sem(f"m_{name}{k}") for k in range(2)] for name in ("st_done", "mv_done", "var_done", "rstd_done", "xn_done"))
    scaled, h2_done = sem("m_scaled"), sem("h2_done")
    h2_ps, x3_ps, h2T_ev, x3T_ev, at_ps, xa_done = (sem("h2_ps"), sem("x3_ps"), sem("h2T_ev"), sem("x3T_ev"),
                                                    sem("at_ps"), sem("xa_done"))
    O_BANKS, H_BANKS, X3_BANKS, WO_BANKS = (0, 1), (2, 3), (4, 5), (6, 7)
    SLOTS = CHUNKS + 2

    def there(i, off):
        return not isinstance(i, int) or 0 <= off < CHUNKS

    def slots(engine, slot):
        for s in range(2):
            slot(0, s)
        with engine.Fori(0, 2) as i:
            for off in (2, 3):
                slot(i, off)
        for s in range(6, SLOTS):
            slot(0, s)

    with nc.Block() as block:
        @block.sync
        def _(sp):
            def load_o(i, off):
                if off >= 2:
                    sp.wait_ge(oT_ps, HALF * (i * 2 + off - 1))
                    alone(sp, passed_sp)
                sp.dma_start(oc[:, off % 2, :, :], a["att_o"][:, bass.ds((i * 2 + off) * TILES, TILES), :])\
                    .then_inc(o_in[off % 2], 16)

            def load_x(i, off):
                if off >= 2:
                    sp.wait_ge(x1_done, FREE + 2 * (i * 2 + off - 1))
                    alone(sp, passed_sp)
                sp.dma_start(xs[:, off % 2, :, :],
                             a["x"][0, bass.ds((i * 2 + off) * CW, CW), :].rearrange("(t p) d -> p t d", p=P))\
                    .then_inc(x_in[off % 2], 16)

            load_o(0, 0)
            load_x(0, 0)
            load_o(0, 1)
            load_x(0, 1)
            sp.dma_start(e["w1_s"][:, :, :], a["w1"][0].rearrange("(h p) n -> p h n", p=P)).then_inc(e["w1_in"], 16)
            sp.dma_start(e["w2_s"][:, :, :], a["w2"][0].rearrange("(k p) n -> p k n", p=P)).then_inc(e["w2_in"], 16)
            sp.dma_start(w_a[:, :, :], a["attnT"].rearrange("(h p) n -> p h n", p=P)).then_inc(w_in, 16)
            sp.dma_start(ab_col[:, :], a["attnb"]).then_inc(w_in, 16)
            sp.dma_start(ln_col[:, :], a["lnsb"]).then_inc(w_in, 16)
            with sp.Fori(0, CHUNKS // 2 - 1) as i:
                for off in (2, 3):
                    load_o(i, off)
                    load_x(i, off)
            for par in range(2):
                sp.wait_ge(o_in[par], 16 * CHUNKS // 2)
                sp.wait_ge(x_in[par], 16 * CHUNKS // 2)

        @block.tensor
        def _(pe):
            begin(pe, at_ps, x3_ps)

            def turn(i, off, banks, at, done):
                for h in range(HALF):
                    for t in range(TILES):
                        mm = nc.tensor.transpose(bank(banks[h])[:, t * P:(t + 1) * P], at[:, t, h * P:(h + 1) * P],
                                                 a["id_f"][:, :])
                    mm.then_inc(done, 1)

            def turn_o(i, off):
                pe.wait_ge(o_in[off % 2], 16 * (i + off // 2 + 1))
                if off:
                    pe.wait_ge(oT_ev, HALF * (i * 2 + off))
                if off >= 3:
                    pe.wait_ge(xa_done, FREE + HALF * (i * 2 + off - 3))
                turn(i, off, O_BANKS, oc[:, off % 2], oT_ps)

            def slot(i, off):
                if there(i, off):
                    pe.wait_ge(oT_ev, HALF * (i * 2 + off + 1))
                    pe.wait_ge(x1_done, FREE + 2 * (i * 2 + off))
                    for t in range(TILES):
                        for h in range(HALF):
                            mm = nc.tensor.matmul(bank(WO_BANKS[t // 2])[:, (t % 2) * D:(t % 2 + 1) * D],
                                                  oT[:, off % 2, h, t * P:(t + 1) * P], a["wo_g"][:, h, :],
                                                  start=(h == 0), stop=(h == HALF - 1))
                        if t % 2:
                            mm.then_inc(wo_ps, 1)
                back = (i, off - 2)
                if there(*back):
                    pe.wait_ge(xn_done[1], FREE + TILES * (i * 2 + off - 1))
                    pe.wait_ge(x3T_ev, FREE + HALF * (i * 2 + off - 2))
                    turn(*back, X3_BANKS, xn[:, 1, off % 2], x3_ps)
                if there(i, off + 1):
                    turn_o(i, off + 1)
                if there(i, off - 1):
                    pe.wait_ge(h2_done, i * 2 + off)
                    if off >= 2:
                        pe.wait_ge(h2T_ev, HALF * (i * 2 + off - 1))
                    turn(i, off - 1, H_BANKS, h2[:, (off - 1) % 2], h2_ps)
                if there(*back):
                    pe.wait_ge(w_in, 48)
                    pe.wait_ge(x3T_ev, FREE + HALF * (i * 2 + off - 1))
                    if there(i, off + 1):
                        pe.wait_ge(oT_ev, HALF * (i * 2 + off + 2))
                    for m in range(HALF):
                        if not there(i, off + 1):
                            pe.wait_ge(xa_done, FREE + HALF * (off - 3) + m + 1)
                        for h in range(HALF):
                            mm = nc.tensor.matmul(bank(O_BANKS[m]), w_a[:, h, m * P:(m + 1) * P],
                                                  x3T[:, h, :], start=(h == 0), stop=(h == HALF - 1))
                        mm.then_inc(at_ps, 1)

            turn_o(0, 0)
            slots(pe, slot)

        @block.scalar
        def _(act):
            begin(act, x3T_ev)

            def take_o(i, off):
                if off >= 2:
                    act.wait_ge(wo_ps, 2 * (i * 2 + off - 1))
                for h in range(HALF):
                    act.wait_ge(oT_ps, HALF * (i * 2 + off) + h + 1)
                    nc.scalar.activation(oT[:, off % 2, h, :], bank(O_BANKS[h]), ACT.Copy).then_inc(oT_ev, 1)

            def slot(i, off):
                if there(i, off - 2):
                    act.wait_ge(at_ps, FREE + HALF * (i * 2 + off - 2))
                    for h in range(HALF):
                        act.wait_ge(x3_ps, FREE + HALF * (i * 2 + off - 2) + h + 1)
                        nc.scalar.activation(x3T[:, h, :], bank(X3_BANKS[h]), ACT.Identity,
                                             bias=ln_col[:, HALF + h:HALF + h + 1], scale=ln_col[:, h:h + 1])\
                            .then_inc(x3T_ev, 1)
                if there(i, off + 1):
                    take_o(i, off + 1)
                if there(i, off - 1):
                    if off >= 2:
                        act.wait_ge(xa_done, FREE + HALF * (i * 2 + off - 2))
                    for h in range(HALF):
                        act.wait_ge(h2_ps, HALF * (i * 2 + off - 1) + h + 1)
                        nc.scalar.activation(h2T[:, (off - 1) % 2, h, :], bank(H_BANKS[h]), ACT.Copy)\
                            .then_inc(h2T_ev, 1)
                if off == SLOTS - 4:
                    act.wait_ge(e["w1_in"], 16)
                    for h in range(HALF):
                        nc.scalar.activation(e["w1_p"][0][:, h, :], e["w1_s"][:, h, :], ACT.Copy)\
                            .then_inc(e["w1_hi"], 1)
                if off == SLOTS - 3:
                    act.wait_ge(e["w2_in"], 16)
                    for ks in K_HALVES:
                        nc.scalar.activation(e["w2_p"][0][:, ks, :], e["w2_s"][:, ks, :], ACT.Copy)\
                            .then_inc(e["w2_hi"], 1)

            take_o(0, 0)
            act.wait_ge(w_in, 48)
            slots(act, slot)

        @block.vector
        def _(dve):
            begin(dve, x1_done, xa_done, xn_done[1])
            dve.wait_ge(w_in, 48)

            def moments(k, i, off, src):
                par = off % 2
                for t in range(TILES):
                    nc.vector.bn_stats(stats[:, k, par, t, :], src(t)).then_inc(st_done[k], 1)
                for t in range(TILES):
                    dve.wait_ge(st_done[k], TILES * (i * 2 + off) + t + 1)
                    alone(dve, passed_dve)
                    nc.vector.bn_aggr(mv[:, k, par, t, :], stats[:, k, par, t, :]).then_inc(mv_done[k], 1)

            def normalise(k, i, off, src):
                par = off % 2
                dve.wait_ge(rstd_done[k], i * 2 + off + 1)
                for t in range(TILES):
                    nc.vector.tensor_scalar(xn[:, k, par, t, :], src(t), mv[:, k, par, t, 0:1],
                                            rstd[:, k, par, t:t + 1], ALU.subtract, ALU.mult).then_inc(xn_done[k], 1)

            def slot(i, off):
                par, last = off % 2, (off - 1) % 2
                if there(i, off):
                    dve.wait_ge(x_in[par], 16 * (i + off // 2 + 1))
                    for b in range(2):
                        dve.wait_ge(wo_ps, 2 * (i * 2 + off) + b + 1)
                        nc.vector.tensor_tensor(
                            x1[:, bass.ds((i * 2 + off) * TILES + 2 * b, 2), :],
                            bank(WO_BANKS[b]).rearrange("p (t d) -> p t d", t=2),
                            xs[:, par, 2 * b:2 * b + 2, :], ALU.add).then_inc(x1_done, 1)
                    dve.wait_ge(x1_done, FREE + 2 * (i * 2 + off) + 2)
                    alone(dve, passed_dve)
                    tile = lambda t: x1[:, bass.ds((i * 2 + off) * TILES + t, 1), :].rearrange("p o d -> p (o d)")
                    moments(0, i, off, tile)
                if there(i, off - 1):
                    dve.wait_ge(h2_done, i * 2 + off)
                    moments(1, i, off - 1, lambda t: h2[:, last, t, :])
                if there(i, off):
                    if off >= 2:
                        dve.wait_ge(scaled, i * 2 + off - 1)
                    normalise(0, i, off, tile)
                if there(i, off - 1):
                    if off >= 2:
                        dve.wait_ge(x3_ps, FREE + HALF * (i * 2 + off - 2))
                    normalise(1, i, off - 1, lambda t: h2[:, last, t, :])
                if there(i, off - 2):
                    dve.wait_ge(h2T_ev, HALF * (i * 2 + off - 1))
                    for m in range(HALF):
                        dve.wait_ge(at_ps, FREE + HALF * (i * 2 + off - 2) + m + 1)
                        nc.vector.scalar_tensor_tensor(
                            out=xaT[:, bass.ds(i * 2 + off - 2, 1), m, :].rearrange("p o s -> p (o s)"),
                            in0=bank(O_BANKS[m]),
                            scalar=ab_col[:, m:m + 1], in1=h2T[:, par, m, :], op0=ALU.add, op1=ALU.add)\
                            .then_inc(xa_done, 1)

            slots(dve, slot)

        @block.gpsimd
        def _(pool):
            nc.gpsimd.memset(half_neg[:, :], -0.5).then_inc(half_set, 1)
            pool.wait_ge(half_set, 1)

            def inverse_std(k, i, off):
                par = off % 2
                pool.wait_ge(mv_done[k], TILES * (i * 2 + off + 1))
                if off >= 2 or (k == 1 and off >= 1):
                    pool.wait_ge(xn_done[k], (FREE if k else 0) + TILES * (i * 2 + off - 1))
                alone(pool, passed_pool)
                nc.gpsimd.tensor_scalar(var_e[:, k, par, :], mv[:, k, par, :, 1], EPS, None, ALU.add)\
                    .then_inc(var_done[k], 1)
                pool.wait_ge(var_done[k], i * 2 + off + 1)
                nc.gpsimd.tensor_tensor(rstd[:, k, par, :], var_e[:, k, par, :], half_neg[:, :], ALU.pow)\
                    .then_inc(rstd_done[k], 1)

            def slot(i, off):
                par = off % 2
                if there(i, off):
                    inverse_std(0, i, off)
                if there(i, off - 1):
                    inverse_std(1, i, off - 1)
                if there(i, off):
                    pool.wait_ge(xn_done[0], TILES * (i * 2 + off + 1))
                    if off >= 2:
                        pool.wait_ge(h2_ps, HALF * (i * 2 + off - 1))
                        pool.wait_ge(xn_done[1], FREE + TILES * (i * 2 + off - 1))
                    nc.gpsimd.tensor_tensor(
                        h2[:, par, :, :], xn[:, 0, par, :, :],
                        a["mod_bc"][:, 4 * D:5 * D].unsqueeze(1).broadcast_to([P, TILES, D]), ALU.mult)\
                        .then_inc(scaled, 1)
                    pool.wait_ge(scaled, i * 2 + off + 1)
                    nc.gpsimd.tensor_tensor(
                        h2[:, par, :, :], h2[:, par, :, :],
                        a["mod_bc"][:, 3 * D:4 * D].unsqueeze(1).broadcast_to([P, TILES, D]), ALU.add)\
                        .then_inc(h2_done, 1)

            slots(pool, slot)
            for h in range(HALF):
                pool.wait_ge(e["w1_hi"], h + 1)
                nc.gpsimd.tensor_tensor(e["w1_p"][1][:, h, :], e["w1_s"][:, h, :], e["w1_p"][0][:, h, :].bitcast(F32),
                                        ALU.subtract).then_inc(e["w1_lo"], 1)
            for n, ks in enumerate(K_HALVES):
                pool.wait_ge(e["w2_hi"], n + 1)
                nc.gpsimd.tensor_tensor(e["w2_p"][1][:, ks, :], e["w2_s"][:, ks, :],
                                        e["w2_p"][0][:, ks, :].bitcast(F32), ALU.subtract).then_inc(e["w2_lo"], 1)


def expert_block(nc, sem, bank, ctx, a, x1, xaT, early):
    def sb(name, shape, dt=F32):
        return ctx.enter_context(nc.sbuf_tensor(name, shape, dt))

    HB = 4
    MB = 2
    TE = CW // MB
    w1_s, w1_p, w2_s, w2_p = early["w1_s"], early["w1_p"], early["w2_s"], early["w2_p"]
    b1_s = sb("b1_s", [P, 2, HK])
    b2_s = sb("b2_s", [P, 2, HALF])
    w_n = sb("w_n", [P, HALF, D])
    w_n_p = [sb(f"w_n_{part}", [P, HALF, D], F32R) for part in ("hi", "lo")]
    nb_bc = sb("nb_bc", [P, D])
    xe_p = [sb(f"xe_{part}", [P, HALF, MB, TE], F32R) for part in ("hi", "lo")]
    hid = sb("hid", [P, HB, CW])
    hid_p = [sb(f"hid_{part}", [P, HK, CW], F32R) for part in ("hi", "lo")]
    eoT = sb("eoT", [P, HALF, CW])
    eo_p = [sb(f"eo_{part}", [P, HALF, CW], F32R) for part in ("hi", "lo")]
    y = sb("y", [P, 2, 2, D])
    yg = sb("yg", [P, 2, 2, D])

    w_in, w_cut = sem("e_w_in"), sem("e_w_cut")
    passed_sp, passed_pool, passed_dve = sem("e_passed_sp"), sem("e_passed_pool"), sem("e_passed_dve")
    w1_in, w2_in, w1_hi, w1_lo, w2_hi, w2_lo = (early["w1_in"], early["w2_in"], early["w1_hi"], early["w1_lo"],
                                                early["w2_hi"], early["w2_lo"])
    b1_in, b2_in = [sem("b1_in0"), sem("b1_in1")], [sem("b2_in0"), sem("b2_in1")]
    x_hi, x_lo = sem("x_hi_done"), sem("x_lo_done")
    h_ps, h_act, h_hi, h_lo = sem("h_ps"), sem("h_act"), sem("h_hi_done"), sem("h_lo_done")
    e_ps, e_ev, e_hi, e_lo = sem("e_ps"), sem("e_ev"), sem("e_hi_done"), sem("e_lo_done")
    n_ps, y_pre, y_act, y_gate, y_done = sem("n_ps"), sem("y_pre"), sem("y_act"), sem("y_gate"), sem("y_done")
    y_out = [sem("y_out0"), sem("y_out1")]
    PASSES = ((0, 0), (0, 1), (1, 0))

    def product(out, lhs, rhs, start, stop):
        for n, (p, q) in enumerate(PASSES):
            mm = nc.tensor.matmul(out, lhs(p), rhs(q), start=start and n == 0, stop=stop and n == len(PASSES) - 1)
        return mm

    def slots(engine, slot):
        slot(0, 0)
        with engine.Fori(0, EXPERTS // 2 - 1) as i:
            for off in (1, 2):
                slot(i, off)
        for e in (EXPERTS - 1, EXPERTS):
            slot(0, e)

    with nc.Block() as block:
        @block.sync
        def _(sp):
            begin(sp, y_pre, y_done, *y_out)

            def load_1(i, off):
                if off:
                    sp.wait_ge(w1_lo, 2 * (i * 2 + off))
                    alone(sp, passed_sp)
                    sp.dma_start(w1_s[:, :, :],
                                 a["w1"][bass.ds(i * 2 + off, 1), :, :].rearrange("o (h p) n -> p (o h) n", p=P))\
                        .then_inc(w1_in, 16)
                if off >= 2:
                    sp.wait_ge(h_act, HK * (i * 2 + off - 1))
                    alone(sp, passed_sp)
                sp.dma_start(b1_s[:, off % 2, :], a["b1"][bass.ds(i * 2 + off, 1), :, :].rearrange("o p k -> p (o k)"))\
                    .then_inc(b1_in[off % 2], 16)

            def load_2(i, off):
                if off:
                    sp.wait_ge(w2_lo, 2 * (i * 2 + off))
                    alone(sp, passed_sp)
                    sp.dma_start(w2_s[:, :, :],
                                 a["w2"][bass.ds(i * 2 + off, 1), :, :].rearrange("o (k p) n -> p (o k) n", p=P))\
                        .then_inc(w2_in, 16)
                if off >= 2:
                    sp.wait_ge(e_ev, HALF * (i * 2 + off - 1))
                    alone(sp, passed_sp)
                sp.dma_start(b2_s[:, off % 2, :], a["b2"][bass.ds(i * 2 + off, 1), :, :].rearrange("o p k -> p (o k)"))\
                    .then_inc(b2_in[off % 2], 16)

            def slot(i, off):
                if off < EXPERTS - 1:
                    load_1(i, off + 1)
                    load_2(i, off + 1)
                if off:
                    e = i * 2 + off - 1
                    for b in range(MB):
                        sp.wait_ge(y_done, FREE + 2 * e + b + 1)
                        alone(sp, passed_sp)
                        sp.dma_start(a["out"][0, bass.ds(e * TE + b * (S // MB), TE), :]
                                     .rearrange("(t p) d -> p t d", p=P), y[:, b, :, :]).then_inc(y_out[b], 16)

            load_1(0, 0)
            load_2(0, 0)
            sp.dma_start(w_n[:, :, :], a["nextT"].rearrange("(h p) n -> p h n", p=P)).then_inc(w_in, 16)
            sp.dma_start(nb_bc[:, :], a["nextb"].rearrange("(a n) -> a n", a=1).broadcast_to([P, D])).then_inc(w_in, 16)
            slots(sp, slot)
            for b in range(MB):
                sp.wait_ge(y_out[b], FREE + 16 * EXPERTS)

        @block.tensor
        def _(pe):
            def slot(i, off):
                e = i * 2 + off
                if off < EXPERTS:
                    pe.wait_ge(w1_lo, 2 * (e + 1))
                    pe.wait_ge(x_lo, e + 1)
                    for k in range(HK):
                        if off or k >= HB:
                            pe.wait_ge(h_act, e * HK + k - HB + 1)
                        for h in range(HALF):
                            mm = product(bank(k % HB), lambda p: w1_p[p][:, h, k * P:(k + 1) * P],
                                         lambda q: xe_p[q][:, h, :, :].rearrange("p m s -> p (m s)"),
                                         h == 0, h == HALF - 1)
                        mm.then_inc(h_ps, 1)
                if off:
                    if off == 1:
                        pe.wait_ge(w_cut, 2)
                    pe.wait_ge(e_lo, HALF * e)
                    pe.wait_ge(y_pre, FREE + 2 * (e - 1))
                    for b in range(MB):
                        for t in range(2):
                            tok = (2 * b + t) * P
                            for h in range(HALF):
                                mm = product(bank(6 + b)[:, t * D:(t + 1) * D], lambda p: eo_p[p][:, h, tok:tok + P],
                                             lambda q: w_n_p[q][:, h, :], h == 0, h == HALF - 1)
                        mm.then_inc(n_ps, 1)
                if off < EXPERTS:
                    pe.wait_ge(w2_lo, 2 * (e + 1))
                    if off:
                        pe.wait_ge(e_ev, HALF * e)
                    for m in range(HALF):
                        for k in range(HK):
                            if m == 0:
                                pe.wait_ge(h_lo, e * HK + k + 1)
                            mm = product(bank(4 + m), lambda p: w2_p[p][:, k, m * P:(m + 1) * P],
                                         lambda q: hid_p[q][:, k, :], k == 0, k == HK - 1)
                        mm.then_inc(e_ps, 1)

            slots(pe, slot)

        @block.scalar
        def _(act):
            def high(to, src, done):
                nc.scalar.activation(to, src, ACT.Copy).then_inc(done, 1)

            def high_1(i, off):
                act.wait_ge(w1_in, 16 * (i * 2 + off + 1))
                act.wait_ge(h_ps, HK * (i * 2 + off))
                for h in range(HALF):
                    high(w1_p[0][:, h, :], w1_s[:, h, :], w1_hi)

            def high_2(i, off):
                act.wait_ge(w2_in, 16 * (i * 2 + off + 1))
                act.wait_ge(e_ps, HALF * (i * 2 + off))
                for ks in K_HALVES:
                    high(w2_p[0][:, ks, :], w2_s[:, ks, :], w2_hi)

            def slot(i, off):
                e = i * 2 + off
                if off < EXPERTS:
                    if off:
                        high_2(i, off)
                    act.wait_ge(b1_in[off % 2], 16 * (i + off // 2 + 1))
                    for k in range(HK + 1):
                        if k < HK:
                            act.wait_ge(h_ps, e * HK + k + 1)
                            if off or k >= HB:
                                act.wait_ge(h_lo, e * HK + k - HB + 1)
                            nc.scalar.activation(hid[:, k % HB, :], bank(k % HB), ACT.Gelu,
                                                 bias=b1_s[:, off % 2, k:k + 1]).then_inc(h_act, 1)
                        if k:
                            act.wait_ge(h_act, e * HK + k)
                            high(hid_p[0][:, k - 1, :], hid[:, (k - 1) % HB, :], h_hi)
                if off < EXPERTS - 1:
                    high_1(i, off + 1)
                if off:
                    for b in range(MB):
                        act.wait_ge(y_pre, FREE + 2 * (e - 1) + b + 1)
                        act.wait_ge(y_done, FREE + 2 * (e - 1))
                        nc.scalar.activation(yg[:, b, :, :], y[:, b, :, :], ACT.Gelu).then_inc(y_act, 1)

            slots(act, slot)

        @block.vector
        def _(dve):
            def cut_x(i, off):
                e = i * 2 + off
                if off:
                    dve.wait_ge(h_ps, HK * e)
                tokens = xaT.rearrange("p (m c) h s -> p m c h s", m=MB)[:, :, bass.ds(i + off // 2, 1), :,
                                                                        (off % 2) * TE:(off % 2 + 1) * TE]\
                    .rearrange("p m c h s -> p m (c h) s")
                hi, lo = [part[:, :, :, :].rearrange("p h m s -> p m h s") for part in xe_p]
                nc.vector.tensor_copy(hi, tokens).then_inc(x_hi, 1)
                dve.wait_ge(x_hi, e + 1)
                nc.vector.tensor_tensor(lo, tokens, hi.bitcast(F32), ALU.subtract).then_inc(x_lo, 1)

            def slot(i, off):
                e = i * 2 + off
                if off < EXPERTS:
                    if off:
                        dve.wait_ge(e_ps, HALF * e)
                    for k in range(HK):
                        dve.wait_ge(h_hi, e * HK + k + 1)
                        nc.vector.tensor_tensor(hid_p[1][:, k, :], hid[:, k % HB, :], hid_p[0][:, k, :].bitcast(F32),
                                                ALU.subtract).then_inc(h_lo, 1)
                if off < EXPERTS - 1:
                    cut_x(i, off + 1)
                if off:
                    for b in range(MB):
                        dve.wait_ge(n_ps, 2 * (e - 1) + b + 1)
                        dve.wait_ge(y_out[b], FREE + 16 * (e - 1))
                        nc.vector.tensor_tensor(y[:, b, :, :], bank(6 + b).rearrange("p (t d) -> p t d", t=2),
                                                nb_bc[:, :].unsqueeze(1).broadcast_to([P, 2, D]), ALU.add)\
                            .then_inc(y_pre, 1)
                    for b in range(MB):
                        dve.wait_ge(y_act, 2 * (e - 1) + b + 1)
                        nc.vector.tensor_tensor(yg[:, b, :, :], yg[:, b, :, :],
                                                a["mod_bc"][:, 5 * D:6 * D].unsqueeze(1).broadcast_to([P, 2, D]),
                                                ALU.mult).then_inc(y_gate, 1)
                    for b in range(MB):
                        dve.wait_ge(y_gate, 2 * (e - 1) + b + 1)
                        nc.vector.tensor_tensor(y[:, b, :, :], yg[:, b, :, :],
                                                x1[:, bass.ds((e - 1) * 2 + 16 * b, 2), :], ALU.add).then_inc(y_done, 1)
                if off < EXPERTS:
                    dve.wait_ge(b2_in[off % 2], 16 * (i + off // 2 + 1))
                    for m in range(HALF):
                        dve.wait_ge(e_ps, HALF * e + m + 1)
                        nc.vector.tensor_scalar(eoT[:, m, :], bank(4 + m), b2_s[:, off % 2, m:m + 1], None, ALU.add)\
                            .then_inc(e_ev, 1)
                        dve.wait_ge(e_ev, HALF * e + m + 1)
                        nc.vector.tensor_copy(eo_p[0][:, m, :], eoT[:, m, :]).then_inc(e_hi, 1)
                        dve.wait_ge(e_hi, HALF * e + m + 1)
                        nc.vector.tensor_tensor(eo_p[1][:, m, :], eoT[:, m, :], eo_p[0][:, m, :].bitcast(F32),
                                                ALU.subtract).then_inc(e_lo, 1)

            cut_x(0, 0)
            dve.wait_ge(w_in, 32)
            nc.vector.tensor_copy(w_n_p[0][:, :, :], w_n[:, :, :]).then_inc(w_cut, 1)
            dve.wait_ge(w_cut, 1)
            nc.vector.tensor_tensor(w_n_p[1][:, :, :], w_n[:, :, :], w_n_p[0][:, :, :].bitcast(F32), ALU.subtract)\
                .then_inc(w_cut, 1)
            slots(dve, slot)

        @block.gpsimd
        def _(pool):
            def slot(i, off):
                e = i * 2 + off
                if 0 < off < EXPERTS:
                    pool.wait_ge(e_ps, HALF * e)
                    for half, ks in enumerate(K_HALVES):
                        pool.wait_ge(w2_hi, 2 * e + half + 1)
                        nc.gpsimd.tensor_tensor(w2_p[1][:, ks, :], w2_s[:, ks, :], w2_p[0][:, ks, :].bitcast(F32),
                                                ALU.subtract).then_inc(w2_lo, 1)
                if off < EXPERTS - 1:
                    pool.wait_ge(h_ps, HK * (e + 1))
                    for h in range(HALF):
                        pool.wait_ge(w1_hi, 2 * (e + 1) + h + 1)
                        nc.gpsimd.tensor_tensor(w1_p[1][:, h, :], w1_s[:, h, :], w1_p[0][:, h, :].bitcast(F32),
                                                ALU.subtract).then_inc(w1_lo, 1)

            slots(pool, slot)


def rope_table():
    inv = (1.0 / np.float32(10000.0) ** (np.arange(0, HD, 2, dtype=np.float32) / np.float32(HD))).astype(np.float32)
    angle = (np.arange(S, dtype=np.float32)[None, :] * inv[:, None]).astype(np.float32).astype(np.float64)
    both = np.stack([np.cos(angle), np.sin(angle)], axis=1)
    both = np.tile(np.repeat(both, 2 * JH, axis=0), (2, 1, 1))
    return np.ascontiguousarray(both.astype(np.float32))


def constants():
    mask = np.zeros((P, CW), np.float32)
    q, k = np.arange(P)[:, None], np.arange(P)[None, :]
    mask[:, CW - P:] = np.where(k > q, np.float32(-1e38), np.float32(0))
    later = np.where(q > k, np.float32(-1e30), np.float32(0)).astype(mybir.dt.np(BF16))
    last = np.zeros((MROWS, JH, S), mybir.dt.np(BF16))
    for j in range(JH):
        last[PARTS * j:PARTS * (j + 1), j, :] = 1
    return {"rope": rope_table(), "ident": np.eye(P, dtype=np.float32), "mask": mask, "later": later, "lastones": last}


def kernel(**inputs):
    import concourse.bacc as _bacc
    from concourse.bass_utils import run_bass_kernel_spmd as _run

    a = {k: np.asarray(v) for k, v in inputs.items()}

    def rows_of_pairs(w):
        return w.T.reshape(D, 2, 2, JH, HD // 2, 2).transpose(0, 5, 2, 1, 4, 3)

    def column(v):
        return v.reshape(HALF, P).T

    arrays = {
        "x": a["L0_attn_x"],
        "wqk": np.stack([rows_of_pairs(a["L0_attn_Wq"]), rows_of_pairs(a["L0_attn_Wk"])], axis=5)
        .reshape(D, 2, 2, P),
        "wvT": a["L0_attn_Wv"].T,
        "woT": a["L0_attn_Wo"].T,
        "lnsb": np.concatenate([column(a["L0_ffn_ln_scale"]), column(a["L0_ffn_ln_bias"])], axis=1),
        "attnT": a["L0_ffn_attn_w"].T,
        "attnb": column(a["L0_ffn_attn_b"]),
        "w1": a["L0_ffn_w1"],
        "b1": a["L0_ffn_b1"].reshape(EXPERTS, HK, P).transpose(0, 2, 1),
        "w2": a["L0_ffn_w2"],
        "b2": a["L0_ffn_b2"].reshape(EXPERTS, HALF, P).transpose(0, 2, 1),
        "nextT": a["L0_ffn_next_w"].T,
        "nextb": a["L0_ffn_next_b"],
        "cvec": column(a["L0_c"]),
        "wmod": a["L0_wmod"],
        **constants(),
    }
    nc = _bacc.Bacc("TRN2", target_bir_lowering=False, num_devices=1)
    args, given = {}, {}
    for name, v in arrays.items():
        v = np.ascontiguousarray(v)
        given[f"in_{name}"] = v
        args[name] = nc.dram_tensor(f"in_{name}", v.shape, mybir.dt.from_np(v.dtype), kind="ExternalInput").ap()
    args["out"] = nc.dram_tensor("out_0", (1, S, D), F32, kind="ExternalOutput").ap()
    build(nc, **args)
    r = _run(nc, [given], core_ids=[0])
    return r.results[0]["out_0"]
```
